# Optimizing a Trainium2 kernel written in Bass

```python
import numpy as np
import jax
import jax.numpy as jnp

def _softmax(x, axis=-1):
    return jax.nn.softmax(x, axis=axis)

def _gelu(x):
    return jax.nn.gelu(x, approximate=True)

def _silu(x):
    return jax.nn.silu(x)

def _sigmoid(x):
    return jax.nn.sigmoid(x)

def _layernorm(x, axis=-1, eps=1e-05):
    m = jnp.mean(x, axis=axis, keepdims=True)
    v = jnp.var(x, axis=axis, keepdims=True)
    return (x - m) / jnp.sqrt(v + eps)

def _scatter_add(tgt, idx, src, axis=0):
    return tgt.at[idx].add(src)

def _segment_sum(src, seg, n):
    return jax.ops.segment_sum(src, seg, n)
kernel_name = 'mk_gnn_resnorm_d4_gnn_r32_6be6a3'

def setup_inputs(seed: int=0):
    np.random.seed(seed)
    _w = jnp.asarray

    def _rec_inputs():
        import jax
        import jax.numpy as jnp
        _gk = jax.random.key(seed)
        x = -6.415e-05 + 1 * jax.random.normal(jax.random.fold_in(_gk, 1), (625, 512), jnp.float32)
        src = jax.random.randint(jax.random.fold_in(_gk, 2), (20000,), 0, 625, jnp.int32)
        dst = jnp.minimum((625 * jax.random.uniform(jax.random.fold_in(_gk, 3), (20000,)) ** 2.0).astype(jnp.int32), 19999)
        _o = jnp.argsort(dst, stable=True)
        src = src[_o]
        dst = dst[_o]
        edge_type_8 = jax.random.randint(jax.random.fold_in(_gk, 13), (20000,), 0, 8, jnp.int32)
        edge_weight1 = -0.00598325 + 0.997157 * jax.random.normal(jax.random.fold_in(_gk, 14), (20000, 1), jnp.float32)
        node_vec1 = jax.random.uniform(jax.random.fold_in(_gk, 15), (625, 1), jnp.float32, 0.0, 0.999957)
        return (x, src, dst, edge_type_8, edge_weight1, node_vec1)
    x, src, dst, edge_type_8, edge_weight1, node_vec1 = _rec_inputs()

    def _L0_gnn_setup():
        import jax, jax.numpy as jnp
        import numpy as np
        N = 625
        E = 5000
        D = 512
        R = 8
        key = jax.random.key(seed)
        ks = jax.random.split(key, 8)
        inp = {'input': jax.random.normal(ks[0], (N, D), dtype=jnp.float32), 'heads': jax.random.randint(ks[1], (E,), 0, N), 'tails': jax.random.randint(ks[2], (E,), 0, N), 'rel': jax.random.randint(ks[3], (E,), 0, R), 'W_self': jax.random.normal(ks[4], (D, D), dtype=jnp.float32) * 0.03, 'b_self': jnp.zeros((D,), dtype=jnp.float32), 'W_rel': jax.random.normal(ks[5], (2 * R, D, D), dtype=jnp.float32) * 0.03, 'b_rel': jnp.zeros((2 * R, D), dtype=jnp.float32)}
        return inp
    _L0_gnn_all = _L0_gnn_setup()
    _L0_gnn_in = {k: v for k, v in _L0_gnn_all.items() if k in ('W_self', 'b_self', 'W_rel', 'b_rel')}
    del _L0_gnn_all

    def _L1_gnn_setup():
        import jax, jax.numpy as jnp
        import numpy as np
        N = 50000
        IN_CH = 512
        OUT_CH = 512
        DEG = 32
        E = N * DEG
        key = jax.random.key(seed)
        kx, kwc, kwn, kb, ke = jax.random.split(key, 5)
        x = jax.random.normal(kx, (N, IN_CH), dtype=jnp.float32)
        bound = 1.0 / np.sqrt(IN_CH)
        wc = jax.random.uniform(kwc, (IN_CH, OUT_CH), minval=-bound, maxval=bound, dtype=jnp.float32)
        wn = jax.random.uniform(kwn, (IN_CH, OUT_CH), minval=-bound, maxval=bound, dtype=jnp.float32)
        bias = jax.random.uniform(kb, (OUT_CH,), minval=-bound, maxval=bound, dtype=jnp.float32)
        src = jnp.repeat(jnp.arange(N, dtype=jnp.int64), DEG)
        dst = jax.random.randint(ke, (E,), 0, N, dtype=jnp.int64)
        edge_index = jnp.stack([src, dst], axis=0)
        return {'x': x, 'wc': wc, 'wn': wn, 'bias': bias, 'edge_index': edge_index}
    _L1_gnn_all = _L1_gnn_setup()
    _L1_gnn_in = {k: v for k, v in _L1_gnn_all.items() if k in ('wc', 'wn', 'bias')}
    del _L1_gnn_all

    def _L2_gnn_setup():
        import jax, jax.numpy as jnp
        import numpy as np
        N_NODES = 40962
        LATENT_DIM = 512
        N_EDGES = 20481
        NUM_BLOCKS = 4
        NUM_HEADS = 4
        NUM_FREQ = 32
        BASE_PERIOD = 16
        NOISE_EMB_DIM = 16
        EPS = 1e-05

        def _cond_layer_norm(x, cond, sw, sb, bw, bb):
            mu = jnp.mean(x, axis=-1, keepdims=True)
            var = jnp.var(x, axis=-1, keepdims=True)
            xn = (x - mu) * jax.lax.rsqrt(var + EPS)
            scale = cond @ sw + sb
            bias = cond @ bw + bb
            return xn * (1.0 + scale) + bias

        def _sparse_attention(x, src, dst, wq, bq, wk, bk, wv, bv, wo, bo):
            N, D = x.shape
            H, Dh = (NUM_HEADS, D // NUM_HEADS)
            q = (x @ wq + bq).reshape(N, H, Dh) * Dh ** (-0.5)
            k = (x @ wk + bk).reshape(N, H, Dh)
            v = (x @ wv + bv).reshape(N, H, Dh)
            scores = jnp.einsum('ehd,ehd->eh', q[src], k[dst])
            smax = jax.ops.segment_max(scores, src, num_segments=N)
            ex = jnp.exp(scores - smax[src])
            denom = jax.ops.segment_sum(ex, src, num_segments=N)
            attn = ex / denom[src]
            out = jax.ops.segment_sum(attn[:, :, None] * v[dst], src, num_segments=N)
            return out.reshape(N, D) @ wo + bo

        def _forward(x, edge_index, noise_levels, f_w1, f_b1, f_w2, f_b2, s1_w, s1_b, b1_w, b1_b, wq, bq, wk, bk, wv, bv, wo, bo, s2_w, s2_b, b2_w, b2_b, m_w1, m_b1, m_w2, m_b2):
            src, dst = (edge_index[0], edge_index[1])
            freqs = jnp.arange(1, NUM_FREQ + 1, dtype=x.dtype) * (2.0 * np.pi / BASE_PERIOD)
            ph = noise_levels * freqs
            emb = jnp.concatenate([jnp.sin(ph), jnp.cos(ph)], axis=-1)
            cond = jax.nn.silu(emb @ f_w1 + f_b1) @ f_w2 + f_b2
            for i in range(NUM_BLOCKS):
                y = _cond_layer_norm(x, cond, s1_w[i], s1_b[i], b1_w[i], b1_b[i])
                y = _sparse_attention(y, src, dst, wq[i], bq[i], wk[i], bk[i], wv[i], bv[i], wo[i], bo[i])
                x = x + y
                y = _cond_layer_norm(x, cond, s2_w[i], s2_b[i], b2_w[i], b2_b[i])
                y = jax.nn.relu(y @ m_w1[i] + m_b1[i]) @ m_w2[i] + m_b2[i]
                x = x + y
            return x
        key = jax.random.key(seed)
        ks = jax.random.split(key, 20)

        def w(k, shape, s=0.02):
            return jax.random.normal(k, shape, dtype=jnp.float32) * s
        D, B, C = (LATENT_DIM, NUM_BLOCKS, NOISE_EMB_DIM)
        z = lambda *s: jnp.zeros(s, jnp.float32)
        return {'latent_mesh_nodes': jax.random.normal(ks[0], (N_NODES, D), dtype=jnp.float32), 'edge_index': jax.random.randint(ks[1], (2, N_EDGES), 0, N_NODES, dtype=jnp.int32), 'noise_levels': jax.random.uniform(ks[2], (N_NODES, 1), dtype=jnp.float32), 'f_w1': w(ks[3], (2 * NUM_FREQ, C)), 'f_b1': z(C), 'f_w2': w(ks[4], (C, C)), 'f_b2': z(C), 's1_w': w(ks[5], (B, C, D)), 's1_b': z(B, D), 'b1_w': w(ks[6], (B, C, D)), 'b1_b': z(B, D), 'wq': w(ks[7], (B, D, D)), 'bq': z(B, D), 'wk': w(ks[8], (B, D, D)), 'bk': z(B, D), 'wv': w(ks[9], (B, D, D)), 'bv': z(B, D), 'wo': w(ks[10], (B, D, D)), 'bo': z(B, D), 's2_w': w(ks[11], (B, C, D)), 's2_b': z(B, D), 'b2_w': w(ks[12], (B, C, D)), 'b2_b': z(B, D), 'm_w1': w(ks[13], (B, D, D)), 'm_b1': z(B, D), 'm_w2': w(ks[14], (B, D, D)), 'm_b2': z(B, D)}
    _L2_gnn_all = _L2_gnn_setup()
    _L2_gnn_in = {k: v for k, v in _L2_gnn_all.items() if k in ('f_w1', 'f_b1', 'f_w2', 'f_b2', 's1_w', 's1_b', 'b1_w', 'b1_b', 'wq', 'bq', 'wk', 'bk', 'wv', 'bv', 'wo', 'bo', 's2_w', 's2_b', 'b2_w', 'b2_b', 'm_w1', 'm_b1', 'm_w2', 'm_b2')}
    del _L2_gnn_all

    def _L3_gnn_setup():
        import jax, jax.numpy as jnp
        import numpy as np
        N, D, E, L = (625, 512, 5000, 4)
        BN_EPS = 1e-05

        def _gine_layer(x, src, dst, edge_attr, eps, We, be, W1, b1, gamma, beta, W2, b2):
            e = edge_attr @ We + be
            m = jax.nn.relu(x[src] + e)
            agg = jax.ops.segment_sum(m, dst, num_segments=x.shape[0])
            h = ((1.0 + eps) * x + agg) @ W1 + b1
            mu = jnp.mean(h, axis=0)
            var = jnp.mean(jnp.square(h - mu), axis=0)
            h = (h - mu) * jax.lax.rsqrt(var + BN_EPS) * gamma + beta
            h = jax.nn.relu(h)
            return jax.nn.relu(h @ W2 + b2)
        key = jax.random.key(seed)
        ks = jax.random.split(key, 10)
        x = jax.random.normal(ks[0], (N, D), dtype=jnp.float32)
        edge_index = jax.random.randint(ks[1], (2, E), 0, N, dtype=jnp.int64)
        edge_attr = jax.random.normal(ks[2], (E, 1), dtype=jnp.float32)
        s1 = 1.0 / np.sqrt(D)
        params = {'eps': jnp.zeros((L,), jnp.float32), 'We': jax.random.normal(ks[3], (L, 1, D), jnp.float32) * 1.0, 'be': jnp.zeros((L, D), jnp.float32), 'W1': jax.random.normal(ks[4], (L, D, D), jnp.float32) * s1, 'b1': jnp.zeros((L, D), jnp.float32), 'gamma': jnp.ones((L, D), jnp.float32), 'beta': jnp.zeros((L, D), jnp.float32), 'W2': jax.random.normal(ks[5], (L, D, D), jnp.float32) * s1, 'b2': jnp.zeros((L, D), jnp.float32)}
        return {'x': x, 'edge_index': edge_index, 'edge_attr': edge_attr, **params}
    _L3_gnn_all = _L3_gnn_setup()
    _L3_gnn_in = {k: v for k, v in _L3_gnn_all.items() if k in ('eps', 'We', 'be', 'W1', 'b1', 'gamma', 'beta', 'W2', 'b2')}
    del _L3_gnn_all
    return {'x': x, 'src': src, 'dst': dst, 'edge_type_8': edge_type_8, 'edge_weight1': edge_weight1, 'node_vec1': node_vec1, 'L0_gnn_W_self': _L0_gnn_in['W_self'], 'L0_gnn_b_self': _L0_gnn_in['b_self'], 'L0_gnn_W_rel': _L0_gnn_in['W_rel'], 'L0_gnn_b_rel': _L0_gnn_in['b_rel'], 'L1_gnn_wc': _L1_gnn_in['wc'], 'L1_gnn_wn': _L1_gnn_in['wn'], 'L1_gnn_bias': _L1_gnn_in['bias'], 'L2_gnn_f_w1': _L2_gnn_in['f_w1'], 'L2_gnn_f_b1': _L2_gnn_in['f_b1'], 'L2_gnn_f_w2': _L2_gnn_in['f_w2'], 'L2_gnn_f_b2': _L2_gnn_in['f_b2'], 'L2_gnn_s1_w': _L2_gnn_in['s1_w'], 'L2_gnn_s1_b': _L2_gnn_in['s1_b'], 'L2_gnn_b1_w': _L2_gnn_in['b1_w'], 'L2_gnn_b1_b': _L2_gnn_in['b1_b'], 'L2_gnn_wq': _L2_gnn_in['wq'], 'L2_gnn_bq': _L2_gnn_in['bq'], 'L2_gnn_wk': _L2_gnn_in['wk'], 'L2_gnn_bk': _L2_gnn_in['bk'], 'L2_gnn_wv': _L2_gnn_in['wv'], 'L2_gnn_bv': _L2_gnn_in['bv'], 'L2_gnn_wo': _L2_gnn_in['wo'], 'L2_gnn_bo': _L2_gnn_in['bo'], 'L2_gnn_s2_w': _L2_gnn_in['s2_w'], 'L2_gnn_s2_b': _L2_gnn_in['s2_b'], 'L2_gnn_b2_w': _L2_gnn_in['b2_w'], 'L2_gnn_b2_b': _L2_gnn_in['b2_b'], 'L2_gnn_m_w1': _L2_gnn_in['m_w1'], 'L2_gnn_m_b1': _L2_gnn_in['m_b1'], 'L2_gnn_m_w2': _L2_gnn_in['m_w2'], 'L2_gnn_m_b2': _L2_gnn_in['m_b2'], 'L3_gnn_eps': _L3_gnn_in['eps'], 'L3_gnn_We': _L3_gnn_in['We'], 'L3_gnn_be': _L3_gnn_in['be'], 'L3_gnn_W1': _L3_gnn_in['W1'], 'L3_gnn_b1': _L3_gnn_in['b1'], 'L3_gnn_gamma': _L3_gnn_in['gamma'], 'L3_gnn_beta': _L3_gnn_in['beta'], 'L3_gnn_W2': _L3_gnn_in['W2'], 'L3_gnn_b2': _L3_gnn_in['b2']}

def reference(x, src, dst, edge_type_8, edge_weight1, node_vec1, L0_gnn_W_self, L0_gnn_b_self, L0_gnn_W_rel, L0_gnn_b_rel, L1_gnn_wc, L1_gnn_wn, L1_gnn_bias, L2_gnn_f_w1, L2_gnn_f_b1, L2_gnn_f_w2, L2_gnn_f_b2, L2_gnn_s1_w, L2_gnn_s1_b, L2_gnn_b1_w, L2_gnn_b1_b, L2_gnn_wq, L2_gnn_bq, L2_gnn_wk, L2_gnn_bk, L2_gnn_wv, L2_gnn_bv, L2_gnn_wo, L2_gnn_bo, L2_gnn_s2_w, L2_gnn_s2_b, L2_gnn_b2_w, L2_gnn_b2_b, L2_gnn_m_w1, L2_gnn_m_b1, L2_gnn_m_w2, L2_gnn_m_b2, L3_gnn_eps, L3_gnn_We, L3_gnn_be, L3_gnn_W1, L3_gnn_b1, L3_gnn_gamma, L3_gnn_beta, L3_gnn_W2, L3_gnn_b2):
    import jax
    import jax.numpy as jnp

    def _L0_gnn_ref(input, heads, tails, rel, W_self, b_self, W_rel, b_rel):
        import jax, jax.numpy as jnp
        import numpy as np
        N = 625
        E = 5000
        D = 512
        R = 8
        h_self = input @ W_self.T + b_self
        H_all = jnp.einsum('rod,nd->rno', W_rel, input) + b_rel[:, None, :]
        msg_to_heads = H_all[rel, tails]
        msg_to_tails = H_all[rel + R, heads]
        agg = jax.ops.segment_sum(msg_to_heads, heads, num_segments=N) + jax.ops.segment_sum(msg_to_tails, tails, num_segments=N)
        return jax.nn.relu(h_self + agg)

    def _L1_gnn_ref(x, wc, wn, bias, edge_index):
        import jax, jax.numpy as jnp
        import numpy as np
        N = 50000
        IN_CH = 512
        OUT_CH = 512
        DEG = 32
        E = N * DEG
        alpha = x @ wc
        beta = x @ wn
        src, dst = (edge_index[0], edge_index[1])
        sums = jax.ops.segment_sum(beta[dst], src, num_segments=x.shape[0])
        counts = jax.ops.segment_sum(jnp.ones_like(src, dtype=beta.dtype), src, num_segments=x.shape[0])
        gamma = sums / counts[:, None]
        return alpha + gamma + bias

    def _L2_gnn_ref(latent_mesh_nodes, edge_index, noise_levels, f_w1, f_b1, f_w2, f_b2, s1_w, s1_b, b1_w, b1_b, wq, bq, wk, bk, wv, bv, wo, bo, s2_w, s2_b, b2_w, b2_b, m_w1, m_b1, m_w2, m_b2):
        import jax, jax.numpy as jnp
        import numpy as np
        N_NODES = 40962
        LATENT_DIM = 512
        N_EDGES = 20481
        NUM_BLOCKS = 4
        NUM_HEADS = 4
        NUM_FREQ = 32
        BASE_PERIOD = 16
        NOISE_EMB_DIM = 16
        EPS = 1e-05

        def _cond_layer_norm(x, cond, sw, sb, bw, bb):
            mu = jnp.mean(x, axis=-1, keepdims=True)
            var = jnp.var(x, axis=-1, keepdims=True)
            xn = (x - mu) * jax.lax.rsqrt(var + EPS)
            scale = cond @ sw + sb
            bias = cond @ bw + bb
            return xn * (1.0 + scale) + bias

        def _sparse_attention(x, src, dst, wq, bq, wk, bk, wv, bv, wo, bo):
            N, D = x.shape
            H, Dh = (NUM_HEADS, D // NUM_HEADS)
            q = (x @ wq + bq).reshape(N, H, Dh) * Dh ** (-0.5)
            k = (x @ wk + bk).reshape(N, H, Dh)
            v = (x @ wv + bv).reshape(N, H, Dh)
            scores = jnp.einsum('ehd,ehd->eh', q[src], k[dst])
            smax = jax.ops.segment_max(scores, src, num_segments=N)
            ex = jnp.exp(scores - smax[src])
            denom = jax.ops.segment_sum(ex, src, num_segments=N)
            attn = ex / denom[src]
            out = jax.ops.segment_sum(attn[:, :, None] * v[dst], src, num_segments=N)
            return out.reshape(N, D) @ wo + bo

        def _forward(x, edge_index, noise_levels, f_w1, f_b1, f_w2, f_b2, s1_w, s1_b, b1_w, b1_b, wq, bq, wk, bk, wv, bv, wo, bo, s2_w, s2_b, b2_w, b2_b, m_w1, m_b1, m_w2, m_b2):
            src, dst = (edge_index[0], edge_index[1])
            freqs = jnp.arange(1, NUM_FREQ + 1, dtype=x.dtype) * (2.0 * np.pi / BASE_PERIOD)
            ph = noise_levels * freqs
            emb = jnp.concatenate([jnp.sin(ph), jnp.cos(ph)], axis=-1)
            cond = jax.nn.silu(emb @ f_w1 + f_b1) @ f_w2 + f_b2
            for i in range(NUM_BLOCKS):
                y = _cond_layer_norm(x, cond, s1_w[i], s1_b[i], b1_w[i], b1_b[i])
                y = _sparse_attention(y, src, dst, wq[i], bq[i], wk[i], bk[i], wv[i], bv[i], wo[i], bo[i])
                x = x + y
                y = _cond_layer_norm(x, cond, s2_w[i], s2_b[i], b2_w[i], b2_b[i])
                y = jax.nn.relu(y @ m_w1[i] + m_b1[i]) @ m_w2[i] + m_b2[i]
                x = x + y
            return x
        return _forward(latent_mesh_nodes, edge_index, noise_levels, f_w1, f_b1, f_w2, f_b2, s1_w, s1_b, b1_w, b1_b, wq, bq, wk, bk, wv, bv, wo, bo, s2_w, s2_b, b2_w, b2_b, m_w1, m_b1, m_w2, m_b2)

    def _L3_gnn_ref(x, edge_index, edge_attr, eps, We, be, W1, b1, gamma, beta, W2, b2):
        import jax, jax.numpy as jnp
        import numpy as np
        N, D, E, L = (625, 512, 5000, 4)
        BN_EPS = 1e-05

        def _gine_layer(x, src, dst, edge_attr, eps, We, be, W1, b1, gamma, beta, W2, b2):
            e = edge_attr @ We + be
            m = jax.nn.relu(x[src] + e)
            agg = jax.ops.segment_sum(m, dst, num_segments=x.shape[0])
            h = ((1.0 + eps) * x + agg) @ W1 + b1
            mu = jnp.mean(h, axis=0)
            var = jnp.mean(jnp.square(h - mu), axis=0)
            h = (h - mu) * jax.lax.rsqrt(var + BN_EPS) * gamma + beta
            h = jax.nn.relu(h)
            return jax.nn.relu(h @ W2 + b2)
        src, dst = (edge_index[0], edge_index[1])
        for l in range(L):
            x = _gine_layer(x, src, dst, edge_attr, eps[l], We[l], be[l], W1[l], b1[l], gamma[l], beta[l], W2[l], b2[l])
        return x
    edge_index = jnp.stack([src, dst])
    x = _layernorm(x + _L0_gnn_ref(x, src, dst, edge_type_8, L0_gnn_W_self, L0_gnn_b_self, L0_gnn_W_rel, L0_gnn_b_rel), axis=-1)
    x = _layernorm(x + _L1_gnn_ref(x, L1_gnn_wc, L1_gnn_wn, L1_gnn_bias, edge_index), axis=-1)
    x = _layernorm(x + _L2_gnn_ref(x, edge_index, node_vec1, L2_gnn_f_w1, L2_gnn_f_b1, L2_gnn_f_w2, L2_gnn_f_b2, L2_gnn_s1_w, L2_gnn_s1_b, L2_gnn_b1_w, L2_gnn_b1_b, L2_gnn_wq, L2_gnn_bq, L2_gnn_wk, L2_gnn_bk, L2_gnn_wv, L2_gnn_bv, L2_gnn_wo, L2_gnn_bo, L2_gnn_s2_w, L2_gnn_s2_b, L2_gnn_b2_w, L2_gnn_b2_b, L2_gnn_m_w1, L2_gnn_m_b1, L2_gnn_m_w2, L2_gnn_m_b2), axis=-1)
    x = _layernorm(x + _L3_gnn_ref(x, edge_index, edge_weight1, L3_gnn_eps, L3_gnn_We, L3_gnn_be, L3_gnn_W1, L3_gnn_b1, L3_gnn_gamma, L3_gnn_beta, L3_gnn_W2, L3_gnn_b2), axis=-1)
    return x

_drawn_inputs = setup_inputs


def setup_inputs(seed=0):
    import zlib

    import numpy as np

    out = dict(_drawn_inputs(seed))
    spreads = {'L0_gnn_b_self': (0.0, 0.356),
     'L0_gnn_b_rel': (0.0, 0.1),
     'L2_gnn_f_b1': (0.0, 0.8),
     'L2_gnn_f_b2': (0.0, 0.8),
     'L2_gnn_s1_b': (0.0, 0.8),
     'L2_gnn_b1_b': (0.0, 0.412),
     'L2_gnn_bq': (0.0, 0.8),
     'L2_gnn_bk': (0.0, 0.8),
     'L2_gnn_bv': (0.0, 0.1),
     'L2_gnn_bo': (0.0, 0.1),
     'L2_gnn_s2_b': (0.0, 0.563),
     'L2_gnn_b2_b': (0.0, 0.572),
     'L2_gnn_m_b1': (0.0, 0.275),
     'L2_gnn_m_b2': (0.0, 0.1),
     'L3_gnn_eps': (0.0, 0.8),
     'L3_gnn_be': (0.0, 0.1),
     'L3_gnn_b1': (0.0, 0.8),
     'L3_gnn_gamma': (1.0, 0.2),
     'L3_gnn_beta': (0.0, 0.1),
     'L3_gnn_b2': (0.0, 0.1)}
    factors = {'node_vec1': 8.0,
     'L1_gnn_bias': 2.84,
     'L2_gnn_f_w1': 8.0,
     'L2_gnn_f_w2': 8.0,
     'L2_gnn_s1_w': 8.0,
     'L2_gnn_b1_w': 8.0,
     'L2_gnn_wq': 7.961,
     'L2_gnn_wk': 7.756,
     'L2_gnn_s2_w': 8.0,
     'L2_gnn_b2_w': 8.0}
    for name, (base, spread) in spreads.items():
        noise = np.random.default_rng([zlib.crc32(name.encode()), seed]).standard_normal(out[name].shape)
        drawn = base * np.exp(spread * noise) if base else spread * noise
        out[name] = jnp.asarray(drawn.astype(out[name].dtype))
    for name, factor in factors.items():
        out[name] = (out[name] * factor).astype(out[name].dtype)
    return out
```

```python
from contextlib import ExitStack
from math import pi

import concourse.bass as bass
from concourse import mybir

F32 = mybir.dt.float32
BF16 = mybir.dt.bfloat16
I32 = mybir.dt.int32
U32 = mybir.dt.uint32
ALU = mybir.AluOpType
ACT = mybir.ActivationFunctionType
AX = mybir.AxisListType
ds = bass.ds

P = 128
N = 625
NB = 125
B = N // NB
D = 512
C = D // P
E = 20000
EC = E // NB
R = 8
K = B * B
U = 3
G = 10
NT = -(-(E // P + K + 1) // U) * U
H = 4
L = 4
NF = 32
CD = 16
EPS = 1e-5
FAR = -1.0e30
assert NT * P >= E + K * (P - 1)


class Chain:

    def __init__(self, eng, sem):
        self.eng, self.sem, self.base, self.n = eng, sem, 0, 0

    def __call__(self, ins):
        ins.then_inc(self.sem, 1)
        self.n += 1
        self.eng.wait_ge(self.sem, self.base + self.n)

    def enter(self, i, per):
        self.start, self.per = self.base + self.n, per
        self.base, self.n = i * per + self.start, 0

    def leave(self, times):
        assert self.n == self.per, self.n
        self.base, self.n = self.start + times * self.per, 0


def gnn_stack(nc, a, out):
    ctx = ExitStack()
    with ctx:
        def sb(name, shape, dt=F32):
            return ctx.enter_context(nc.sbuf_tensor(name, shape, dt))

        banks = ctx.enter_context(nc.psum_tensor("banks", [P, 8 * D], F32))

        def bank(i):
            return banks[:, i * D:(i + 1) * D]

        def pair(i):
            return banks[:, 2 * i * D:2 * i * D + B * P].rearrange("p (b n) -> p b n", n=P)

        def blocks(t):
            return t.rearrange("p (b n) -> p b n", n=NB)

        ident = sb("ident", [P, P])
        identb = sb("identb", [P, P], BF16)
        ones = sb("ones", [P, P])
        earlier = sb("earlier", [P, P])
        zerob = sb("zerob", [P, D], BF16)
        iota_n = sb("iota_n", [P, NB])
        iota_nb = sb("iota_nb", [P, NB + 3], BF16)[:, 0:NB]
        iota_k = sb("iota_k", [P, K])
        iota_t = sb("iota_t", [P, NT])
        freq = sb("freq", [2 * NF, 1])
        turn = sb("turn", [2 * NF, 2])
        eps_c = sb("eps_c", [P, 1])

        meta = sb("meta", [P, NT * 4])
        meta4 = meta[:, :].rearrange("p (t v) -> p t v", v=4)
        tab_k = sb("tab_k", [P, NT], I32)
        tab_d = sb("tab_d", [P, NT], I32)
        tab_s = sb("tab_s", [P, NT], I32)
        w3 = sb("w3", [P, NT * 3], BF16)
        w3v = w3[:, :].rearrange("p (t v) -> p t v", v=3)
        rows_of = sb("rows_of", [P, NT * 2], U32)
        rows_v = rows_of[:, :].rearrange("p (t v) -> p t v", v=2)
        rows_now = [sb(f"rows_now{j}", [P, 2], U32)[:, :] for j in range(U)]
        pay_now = [sb(f"pay_now{j}", [P, G * 4])[:, :] for j in range(2)]
        addr_now = [sb(f"addr_now{j}", [P, G], U32)[:, :] for j in range(2)]
        x = sb("x", [P, B * D])
        xv = x[:, :].rearrange("p (b d) -> p b d", b=B)
        xn = sb("xn", [P, B * D])
        xnv = xn[:, :].rearrange("p (b d) -> p b d", b=B)
        xres = sb("xres", [P, B * D])
        xresv = xres[:, :].rearrange("p (b d) -> p b d", b=B)
        yT = sb("yT", [P, C * N])
        yTv = yT[:, :].rearrange("p (c n) -> p c n", c=C)
        cnt_sd = sb("cnt_sd", [P, B * N])
        csd = cnt_sd[:, :].rearrange("p (s n) -> p s n", s=B)
        condT = sb("condT", [CD + 1, N])
        st6 = sb("st6", [P, B * 12])
        mv = sb("mv", [P, B * 2])
        mvv = mv[:, :].rearrange("p (b v) -> p b v", v=2)
        std = sb("std", [P, B])
        rstd = sb("rstd", [P, B])
        small = sb("small", [P, 64])

        ARENA = 34800
        arena = sb("arena", [P, ARENA])
        top = [0]

        def take(words, dt=F32):
            at = top[0]
            top[0] += words
            assert top[0] <= ARENA, top[0]
            v = arena[:, at:at + words]
            return v if dt == F32 else v.bitcast(dt)

        member = take(K * EC)
        rank = take(K * EC)
        wc, wn = take(C * D), take(C * D)
        bias1 = take(D)
        degree, rdeg = take(B), take(B)
        beta = xn[:, :]
        src_i, dst_i, rel_i = take(EC, I32), take(EC, I32), take(EC, I32)
        w_in = take(EC)
        s_f, d_f, s_b, d_b, key, pos = (take(EC) for _ in range(6))
        pos_i, slot_t, slot_p = (take(EC, I32) for _ in range(3))
        addr = take(EC, U32)
        payload = take(EC * 4)
        pads = take(NT * 4)
        xT = take(C * N)
        xTv = xT.rearrange("p (c n) -> p c n", c=C)
        wr = [take(C * D) for _ in range(2)]
        br = [take(D) for _ in range(2)]
        hst = [take(B * D) for _ in range(2)]
        hself = take(B * D)
        tk, tdb, tsb, t0 = (take(NT) for _ in range(4))
        tiles_i = take(K, I32)
        emb = take(N)
        ph = take(N)
        emb_i = take(N, I32)
        z1, z2 = emb, ph
        fw1, fw2 = take(CD), take(CD)
        fb1, fb2 = take(1), take(1)
        top[0] = 0
        oh_s = [take(64, BF16)[:, 0:NB] for _ in range(U)]
        oh_d = [take(64, BF16)[:, 0:NB] for _ in range(U)]
        ohf_s = [take(NB) for _ in range(U)]
        ohf_d = [take(NB) for _ in range(U)]
        got = [[take(D) for _ in range(2)] for _ in range(U)]
        cnt_ds = take(B * N)
        cds = cnt_ds.rearrange("p (k n) -> p k n", n=NB)
        assert top[0] <= 2 * K * EC
        top[0] = 0
        w2 = [take(C * D) for _ in range(6)]
        wb = [take(D) for _ in range(3)]
        wcol = [take(C) for _ in range(3)]
        lnw = [take(D) for _ in range(4)]
        mask = take(B * N)
        qT, kT, vN, oT = take(C * N), take(C * N), take(B * D), xn[:, 0:C * N]
        sm, ex, pr = ([take(N) for _ in range(2)] for _ in range(3))
        dg = [take(NB) for _ in range(2)]
        pT = take(B * N)
        top[0] = 0
        stat = take(NT * P // 2, BF16)
        xp = [take(B * D // 2, BF16) for _ in range(3)]
        xst = take(B * D)
        g1, g2 = take(C * D), take(C * D)
        gb_e, gb_2 = take(D), take(D)
        gcol = take(3 * C)
        gcv = gcol.rearrange("p (v c) -> p v c", v=3)
        geps, gep1 = take(1), take(1)
        msg = [take(D) for _ in range(U)]
        odf = [take(NB) for _ in range(U)]
        ohw = [take(64, BF16) for _ in range(U)]
        hp = take(C * N)
        bnc = take(4 * C)

        meta_d = nc.dram_tensor("meta_d", [P * NT, 4], F32, kind="Internal").ap()
        proj_d = nc.dram_tensor("proj_d", [2 * R * N, D], F32, kind="Internal").ap()

        names = """consts edges_in x_in fnet_in pads_made pads_out totals offsets_mm slot_addr
            scattered0 scattered1 addr_set rows_set meta_in tables proj_psum proj_free proj_out0 proj_out1 wr_in0 wr_in1
            onehots cnt_free cnt_psum cnt_sb csd_psum csd_sb got0 got1 got2 onef msg_free msg_done
            ln_var ln_std x0_ready t_psum t_sb m1_in beta_psum beta_sb agg_psum agg_used
            ph_ready emb_ready z1_psum z1_exp z1_ready z2_psum cond_ready stage7
            w_in0 w_in1 w_in2 w_in3 w_in4 w_in5 ln_in0 ln_in1 xn_ready mod_psum mod_sc mod_done
            qk_psum q_done k_done v_psum v_done
            s_psum s_read sm_ready e_ready p_ready pt_psum pt_done wo_psum x_upd m1_psum h_done m2_psum
            stage8 we_in g_in g2_in xst_ready part0 rest1 part1 parts ohw_ready ohw_free st_psum st_sb
            u_psum msg_ready odf_ready tile_free tile_done
            xa_ready xat_psum xat_sb h1_psum h1_sb bn_var bn_std bn_ready hp_ready h2_psum x_new out_ready out_done
            pool_go dve_go dve_step act_step pool_step""".split()
        S = {n: ctx.enter_context(nc.semaphore(n)) for n in names}

        block = ctx.enter_context(nc.Block())
        e = slice(0, NB)

        @block.sync
        def _(sp):
            def load_square(dst, src):
                return sp.dma_start(dst.rearrange("p (c o) -> p c o", c=C), src.rearrange("(c p) o -> p c o", p=P))

            def one(ap, i):
                return ap[ds(i, 1)].rearrange("a b c -> (a b) c") if len(ap.shape) == 3 else ap[ds(i, 1)]

            def row_to_all(dst, src_row, n=P):
                return sp.dma_start(dst, src_row.broadcast_to([n, dst.shape[-1]]))

            for dst, name in ((src_i, "src"), (dst_i, "dst"), (rel_i, "edge_type_8"), (w_in, "edge_weight1")):
                sp.dma_start(dst[e, :], a[name]).then_inc(S["edges_in"], 16)
            sp.dma_start(xTv, a["xT"].rearrange("(c p) n -> p c n", p=P)).then_inc(S["x_in"], 16)

            def load_proj(r, j):
                load_square(wr[j], one(a["W0"], r)).then_inc(S[f"wr_in{j}"], 16)
                row_to_all(br[j], one(a["b0"], r)).then_inc(S[f"wr_in{j}"], 16)

            load_proj(0, 0)
            load_proj(1, 1)
            sp.dma_start(xv[e], a["x"].rearrange("(b p) d -> p b d", p=NB)).then_inc(S["x_in"], 16)
            row_to_all(ph[0:2 * NF], a["node_vec1"], 2 * NF).then_inc(S["fnet_in"], 16)
            sp.dma_start(fw1[0:2 * NF, :], a["L2_gnn_f_w1"]).then_inc(S["fnet_in"], 16)
            sp.dma_start(fw2[0:CD, :], a["L2_gnn_f_w2"]).then_inc(S["fnet_in"], 16)
            sp.dma_start(fb1[0:CD, :], a["L2_gnn_f_b1"]).then_inc(S["fnet_in"], 16)
            sp.dma_start(fb2[0:CD, :], a["L2_gnn_f_b2"]).then_inc(S["fnet_in"], 16)
            sp.wait_ge(S["pads_made"], 2)
            sp.dma_start(meta_d.rearrange("(p t) v -> p (t v)", p=P), pads).then_inc(S["pads_out"], 16)
            load_square(wc, a["L1_gnn_wc"]).then_inc(S["m1_in"], 16)
            load_square(wn, a["L1_gnn_wn"]).then_inc(S["m1_in"], 16)
            row_to_all(bias1, a["L1_gnn_bias"]).then_inc(S["m1_in"], 16)

            rows = proj_d.rearrange("(r b p) d -> r p b d", p=NB, b=B)

            def store(r, j):
                sp.dma_start(rows[ds(r - 1, 1)].rearrange("a p b d -> (a p) b d"),
                             hst[j].rearrange("p (b d) -> p b d", b=B)[e]).then_inc(S[f"proj_out{j}"], 16)

            sp.wait_ge(S["proj_free"], B + B)
            load_proj(2, 0)
            with sp.Fori(0, R - 1) as i:
                for j in (1, 0):
                    r = 2 * i + 2 - j
                    sp.wait_ge(S["proj_free"], r * B + 2 * B)
                    store(r, j)
                    load_proj(r + 2, j)
            for j in (1, 0):
                r = 2 * R - j
                sp.wait_ge(S["proj_free"], r * B + 2 * B)
                store(r, j)

            sp.wait_ge(S["scattered0"], 8 * EC)
            sp.wait_ge(S["scattered1"], 8 * EC)
            sp.dma_start(meta[:, :], meta_d.rearrange("(p t) v -> p (t v)", p=P)).then_inc(S["meta_in"], 16)

            def load_w(k, l):
                load_square(w2[k], one(a["L2_gnn_" + ("wq", "wk", "wv", "wo", "m_w1", "m_w2")[k]], l)
                            ).then_inc(S[f"w_in{k}"], 16)
                if k in (0, 1, 4):
                    sp.dma_start(wcol[(0, 1, 4).index(k)], one(a[("bq", "bk", "", "", "m_b1")[k]], l)
                                 ).then_inc(S[f"w_in{k}"], 16)
                else:
                    row_to_all(wb[(2, 3, 5).index(k)], one(a["L2_gnn_" + ("", "", "bv", "bo", "", "m_b2")[k]], l)
                               ).then_inc(S[f"w_in{k}"], 16)

            def load_ln(h, l):
                for q, name in enumerate(("s", "b")):
                    sp.dma_start(lnw[2 * h + q][0:CD, :], one(a[f"L2_gnn_{name}{h + 1}_w"], l)
                                 ).then_inc(S[f"ln_in{h}"], 16)
                    sp.dma_start(lnw[2 * h + q][CD:CD + 1, :], one(a[f"L2_gnn_{name}{h + 1}_b"], l)
                                 ).then_inc(S[f"ln_in{h}"], 16)

            sp.wait_ge(S["stage7"], 1)
            load_ln(0, 0)
            for k in range(4):
                load_w(k, 0)
            load_ln(1, 0)
            for k in (4, 5):
                load_w(k, 0)
            with sp.Fori(0, L - 1) as l:
                sp.wait_ge(S["mod_done"], l * (2 * C) + C)
                load_ln(0, l + 1)
                sp.wait_ge(S["q_done"], l * H + H)
                load_w(0, l + 1)
                sp.wait_ge(S["k_done"], l * H + H)
                load_w(1, l + 1)
                sp.wait_ge(S["v_done"], l * B + B)
                load_w(2, l + 1)
                sp.wait_ge(S["x_upd"], l * (2 * B) + B)
                load_w(3, l + 1)
                sp.wait_ge(S["mod_done"], l * (2 * C) + 2 * C)
                load_ln(1, l + 1)
                sp.wait_ge(S["h_done"], l * C + C)
                load_w(4, l + 1)
                sp.wait_ge(S["x_upd"], l * (2 * B) + 2 * B)
                load_w(5, l + 1)

            def load_gine_in(l):
                row_to_all(gb_e, one(a["L3_gnn_be"], l)).then_inc(S["we_in"], 16)
                row_to_all(geps, one(a["eps3"], l)).then_inc(S["we_in"], 16)
                for b in range(B):
                    row_to_all(xst[NB:P, b * D:(b + 1) * D], one(a["L3_gnn_We"], l), P - NB
                               ).then_inc(S["we_in"], 16)

            def load_g1(l):
                load_square(g1, one(a["L3_gnn_W1"], l)).then_inc(S["g_in"], 16)
                sp.dma_start(gcol, one(a["cols3"], l)).then_inc(S["g_in"], 16)

            def load_g2(l):
                load_square(g2, one(a["L3_gnn_W2"], l)).then_inc(S["g2_in"], 16)
                row_to_all(gb_2, one(a["L3_gnn_b2"], l)).then_inc(S["g2_in"], 16)

            sp.wait_ge(S["stage8"], 1)
            load_gine_in(0)
            load_g1(0)
            load_g2(0)
            with sp.Fori(0, L - 1) as l:
                sp.wait_ge(S["parts"], l + 1)
                sp.wait_ge(S["xa_ready"], l * B + B)
                load_gine_in(l + 1)
                sp.wait_ge(S["hp_ready"], l * C + C)
                load_g1(l + 1)
                sp.wait_ge(S["x_new"], l * B + B)
                load_g2(l + 1)

            sp.wait_ge(S["out_ready"], B)
            sp.dma_start(out.rearrange("(b p) d -> p b d", p=NB), xnv[e]).then_inc(S["out_done"], 16)
            sp.wait_ge(S["out_done"], 16)

        @block.gpsimd
        def _(pool):
            step = Chain(pool, S["pool_step"])
            step(pool.memset(ident[:, :], 0.0))
            step(pool.affine_select(out=ident[:, :], in_=ident[:, :], compare_op=ALU.not_equal, fill=1.0, base=0,
                                    pattern=[[-1, P]], channel_multiplier=1))
            step(pool.tensor_copy(identb[:, :], ident[:, :]))
            step(pool.memset(ones[:, :], 1.0))
            step(pool.affine_select(out=earlier[:, :], in_=ones[:, :], compare_op=ALU.is_gt, fill=0.0, base=0,
                               pattern=[[1, P]], channel_multiplier=-1))
            step(pool.memset(zerob[:, :], 0.0))
            many = dict(allow_small_or_imprecise_dtypes=True)
            for t, n in ((iota_n[:, :], NB), (iota_nb, NB), (iota_k[:, :], K), (iota_t[:, :], NT)):
                step(pool.iota(t, [[1, n]], base=0, channel_multiplier=0, **many))
            for q in range(2):
                rows = slice(q * NF, (q + 1) * NF)
                step(pool.iota(freq[rows, :], [[0, 1]], base=1, channel_multiplier=1, **many))
                step(pool.memset(turn[rows, 0:1], 0.25 * q))
                step(pool.memset(turn[rows, 1:2], 0.5 * pi * q))
            step(pool.memset(eps_c[:, :], EPS))
            pool.memset(condT[:, :], 1.0).then_inc(S["consts"], 1)
            pool.wait_ge(S["consts"], 1)
            pv = pads.rearrange("p (t v) -> p t v", v=4)
            pool.memset(pv[:, :, 0:2], -1.0).then_inc(S["pads_made"], 1)
            pool.memset(pv[:, :, 2:4], 0.0).then_inc(S["pads_made"], 1)

            pool.wait_ge(S["pads_out"], 16)
            pool.wait_ge(S["slot_addr"], 1)
            with pool.Fori(0, EC // (2 * G)) as i:
                for j in range(2):
                    pool.tensor_copy(addr_now[j][e], addr[e, ds((2 * i + j) * G, G)]).then_inc(S["addr_set"], 1)
                    pool.tensor_copy(pay_now[j][e], payload[e, ds((2 * i + j) * G * 4, G * 4)]
                                     ).then_inc(S["addr_set"], 1)
                    pool.wait_ge(S["addr_set"], 4 * i + 2 * j + 2)
                    pool.sem_inc(S["pool_go"], 1)
                    for q in range(G):
                        pool.indirect_dma_start(
                            out=meta_d, out_offset=bass.IndirectOffsetOnAxis(ap=addr_now[j][e, q:q + 1], axis=0),
                            in_=pay_now[j][e, q * 4:q * 4 + 4], in_offset=None
                        ).then_inc(S[f"scattered{j}"], 16)
                pool.wait_ge(S["scattered0"], 16 * G * i + 16 * G)
                pool.wait_ge(S["scattered1"], 16 * G * i + 16 * G)

            pool.wait_ge(S["proj_out0"], 16 * R)
            pool.wait_ge(S["proj_out1"], 16 * R)
            pool.wait_ge(S["tables"], 3)
            with pool.Fori(0, NT // U) as i:
                for j in range(U):
                    pool.wait_ge(S["msg_free"], i * U + j + 1)
                    pool.tensor_copy(rows_now[j], rows_of[:, ds((i * U + j) * 2, 2)]).then_inc(S["rows_set"], 1)
                    pool.wait_ge(S["rows_set"], i * U + j + 1)
                    pool.sem_inc(S["pool_go"], 1)
                    for q in range(2):
                        pool.indirect_dma_start(
                            out=got[j][q], out_offset=None, in_=proj_d,
                            in_offset=bass.IndirectOffsetOnAxis(ap=rows_now[j][:, q:q + 1], axis=0)
                        ).then_inc(S[f"got{j}"], 16)

        @block.vector
        def _(dve):
            step = Chain(dve, S["dve_step"])
            v = nc.vector
            v.sem_inc(S["proj_free"], B)
            v.sem_inc(S["cnt_free"], U)
            v.sem_inc(S["msg_free"], U)
            v.sem_inc(S["ohw_free"], U)
            v.sem_inc(S["tile_free"], U)
            dve.wait_ge(S["edges_in"], 64)
            dve.wait_ge(S["consts"], 1)

            pay = payload.rearrange("p (e v) -> p e v", v=4)
            step(v.tensor_copy(s_f[e], src_i[e]))
            step(v.tensor_copy(d_f[e], dst_i[e]))
            for f, blk in ((s_f, s_b), (d_f, d_b)):
                step(v.tensor_scalar(blk[e], f[e], float(NB), None, ALU.is_ge))
                for b in range(2, B):
                    step(v.scalar_tensor_tensor(blk[e], f[e], float(b * NB), blk[e], ALU.is_ge, ALU.add))
            step(v.scalar_tensor_tensor(pay[e, :, 0], s_b[e], -float(NB), s_f[e], ALU.mult, ALU.add))
            step(v.scalar_tensor_tensor(pay[e, :, 1], d_b[e], -float(NB), d_f[e], ALU.mult, ALU.add))
            step(v.tensor_copy(pay[e, :, 2], w_in[e]))
            step(v.tensor_copy(pay[e, :, 3], rel_i[e]))
            step(v.scalar_tensor_tensor(key[e], d_b[e], float(B), s_b[e], ALU.mult, ALU.add))

            mem = member.rearrange("p (k e) -> p k e", k=K)
            rnk = rank.rearrange("p (k e) -> p k e", k=K)
            wide = [NB, K, EC]
            step(v.tensor_tensor(mem[e], key[e].unsqueeze(1).broadcast_to(wide),
                                 iota_k[e].unsqueeze(2).broadcast_to(wide), ALU.is_equal))
            step(v.tensor_tensor_scan(rank[e], member[e], zerob[e, 0:1].broadcast_to([NB, K * EC]), 0.0,
                                      ALU.add, ALU.add))
            tot, before = small[:, 0:K], small[:, K:2 * K]
            incl, tiles, start, off, cntf = (t0[:, q * K:(q + 1) * K] for q in range(5))
            v.tensor_reduce(tot[e], mem[e], AX.X, ALU.add).then_inc(S["totals"], 1)
            dve.wait_ge(S["totals"], 1)
            step(v.tensor_tensor_scan(before[e], tot[e], zerob[e, 0:K], 0.0, ALU.add, ALU.add))
            step(v.tensor_tensor(before[e], before[e], tot[e], ALU.subtract))
            dve.wait_ge(S["offsets_mm"], 1)
            pre, cnt = bank(7)[e, 0:K], bank(7)[:, 32:32 + K]
            step(v.tensor_scalar(cntf, cnt, float(P - 1), None, ALU.add))
            step(v.tensor_copy(tiles_i, cntf))
            step(v.tensor_scalar(tiles_i, tiles_i, 7, None, ALU.arith_shift_right))
            step(v.tensor_copy(tiles, tiles_i))
            step(v.tensor_tensor_scan(incl, tiles, zerob[:, 0:K], 0.0, ALU.add, ALU.add))
            step(v.tensor_tensor(start, incl, tiles, ALU.subtract))
            step(v.scalar_tensor_tensor(off[e], start[e], float(P), pre, ALU.mult, ALU.add))
            step(v.scalar_tensor_tensor(off[e], off[e], -1.0, before[e], ALU.add, ALU.subtract))
            step(v.tensor_tensor(rnk[e], rnk[e], off[e].unsqueeze(2).broadcast_to(wide), ALU.add))
            step(v.tensor_tensor(rank[e], rank[e], member[e], ALU.mult))
            step(v.tensor_reduce(pos[e], rank[e].rearrange("p (k e) -> p e k", k=K), AX.X, ALU.add))
            step(v.tensor_copy(pos_i[e], pos[e]))
            step(v.tensor_scalar(slot_t[e], pos_i[e], 7, None, ALU.arith_shift_right))
            step(v.tensor_scalar(slot_p[e], pos_i[e], P - 1, None, ALU.bitwise_and))
            v.scalar_tensor_tensor(addr[e], slot_p[e], float(NT), slot_t[e], ALU.mult, ALU.add
                                   ).then_inc(S["slot_addr"], 1)

            step(v.tensor_scalar(tk, iota_t[:, :], start[:, 1:2], None, ALU.is_ge))
            for k in range(2, K):
                step(v.scalar_tensor_tensor(tk, iota_t[:, :], start[:, k:k + 1], tk, ALU.is_ge, ALU.add))
            step(v.tensor_scalar(tdb, tk, float(B), None, ALU.is_ge))
            for b in range(2, B):
                step(v.scalar_tensor_tensor(tdb, tk, float(b * B), tdb, ALU.is_ge, ALU.add))
            step(v.scalar_tensor_tensor(tsb, tdb, -float(B), tk, ALU.mult, ALU.add))
            v.tensor_scalar(tab_k[:, :], tk, float(P), None, ALU.mult).then_inc(S["tables"], 1)
            v.tensor_scalar(tab_d[:, :], tdb, float(D), None, ALU.mult).then_inc(S["tables"], 1)
            step(v.tensor_scalar(tab_s[:, :], tsb, float(D), None, ALU.mult))

            dve.wait_ge(S["fnet_in"], 80)
            f = slice(0, 2 * NF)
            step(v.tensor_scalar(freq[f, :], freq[f, :], 2.0 * pi / 16, None, ALU.mult))
            step(v.tensor_scalar(ph[f], ph[f], freq[f, 0:1], None, ALU.mult))
            step(v.tensor_scalar(emb[f], ph[f], 1.0 / (2 * pi), turn[f, 0:1], ALU.mult, ALU.add))
            step(v.tensor_copy(emb_i[f], emb[f]))
            step(v.tensor_copy(emb[f], emb_i[f]))
            c1 = 6.28125
            c2 = float(int((2 * pi - c1) * 2 ** 20)) / 2 ** 20
            for part in (c1, c2, 2 * pi - c1 - c2):
                step(v.scalar_tensor_tensor(ph[f], emb[f], -part, ph[f], ALU.mult, ALU.add))
            step(v.tensor_scalar(ph[f], ph[f], turn[f, 1:2], None, ALU.add))
            v.tensor_scalar(ph[f], ph[f], 3.1415925, -3.1415925, ALU.min, ALU.max).then_inc(S["ph_ready"], 1)

            def evac_block(n, b, dst, bias):
                dve.wait_ge(S["proj_psum"], n + 1)
                v.tensor_tensor(dst[e, b * D:(b + 1) * D], bank(b)[e], bias[e], ALU.add
                                ).then_inc(S["proj_free"], 1)

            dve.wait_ge(S["wr_in0"], 32)
            for b in range(B):
                evac_block(b, b, hself, br[0])

            def evac_two(i, first):
                for j in (1, 0):
                    dve.wait_ge(S[f"wr_in{j}"], 32 * i + 64 - 32 * j)
                    if not first:
                        dve.wait_ge(S[f"proj_out{j}"], 16 * i)
                    for b in range(B):
                        evac_block((2 * i + 2 - j) * B + b, b, hst[j], br[j])

            evac_two(0, True)
            with dve.Fori(1, R) as i:
                evac_two(i, False)

            dve.wait_ge(S["z1_exp"], 1)
            cd = slice(0, CD)
            step(v.tensor_scalar(z2[cd], z2[cd], 1.0, None, ALU.add))
            step(v.reciprocal(z2[cd], z2[cd]))
            v.tensor_tensor(z1[cd], z1[cd], z2[cd], ALU.mult).then_inc(S["z1_ready"], 1)

            dve.wait_ge(S["meta_in"], 16)
            for q, base, blk, col in ((0, 0.0, tdb, 1), (1, float(R), tsb, 0)):
                step(v.tensor_scalar(t0, meta4[:, :, 3], base, float(N), ALU.add, ALU.mult))
                step(v.scalar_tensor_tensor(t0, blk, float(NB), t0, ALU.mult, ALU.add))
                step(v.scalar_tensor_tensor(rows_v[:, :, q], meta4[:, :, col], 0.0, t0, ALU.max, ALU.add))
            step(v.tensor_copy(w3v[:, :, 0], meta4[:, :, 2]))
            step(v.tensor_tensor(t0, meta4[:, :, 2], w3v[:, :, 0], ALU.subtract))
            step(v.tensor_copy(w3v[:, :, 1], t0))
            step(v.tensor_tensor(t0, t0, w3v[:, :, 1], ALU.subtract))
            v.tensor_copy(w3v[:, :, 2], t0).then_inc(S["tables"], 1)
            dve.wait_ge(S["tables"], 3)

            def one_hot(dst, iota, t, place):
                return v.tensor_scalar(dst, iota, meta[:, ds(t * 4 + place, 1)], None, ALU.is_equal)

            with dve.Fori(0, NT // U) as i:
                for j in range(U):
                    dve.wait_ge(S["cnt_free"], i * U + j + 1)
                    one_hot(oh_s[j], iota_nb, i * U + j, 0).then_inc(S["onehots"], 1)
                    one_hot(oh_d[j], iota_nb, i * U + j, 1).then_inc(S["onehots"], 1)
            with dve.Fori(0, NT // U) as i:
                for j in range(U):
                    dve.wait_ge(S["msg_free"], i * U + j + 1)
                    one_hot(ohf_s[j], iota_n[:, :], i * U + j, 0).then_inc(S["onef"], 1)
                    one_hot(ohf_d[j], iota_n[:, :], i * U + j, 1).then_inc(S["onef"], 1)

            def norm(ln, dst, done):
                for b in range(B):
                    step(v.bn_stats(st6[e, b * 6:b * 6 + 6], xv[e, b]))
                dve.sem_inc(S["dve_go"], 1)
                for b in range(B):
                    v.bn_aggr(mvv[e, b], st6[e, b * 6:b * 6 + 6]).then_inc(S["ln_var"], 1)
                dve.wait_ge(S["ln_std"], ln + 1)
                step(v.reciprocal(rstd[e, :], std[e, :]))
                for b in range(B):
                    v.tensor_scalar(dst[e, b], xv[e, b], mvv[e, b, 0:1], rstd[e, b:b + 1],
                                    ALU.subtract, ALU.mult).then_inc(done, 1)

            NORM = B + 1

            dve.wait_ge(S["x_in"], 32)
            dve.wait_ge(S["msg_free"], NT + U)
            for b in range(B):
                hb = hself[e, b * D:(b + 1) * D]
                step(v.tensor_tensor(hb, hb, bank(b)[e], ALU.add))
                step(v.scalar_tensor_tensor(xv[e, b], hb, 0.0, xv[e, b], ALU.max, ALU.add))
            norm(0, xv, S["x0_ready"])

            dve.wait_ge(S["csd_sb"], 1)
            step(v.tensor_reduce(degree[e], csd[e], AX.X, ALU.add))
            step(v.reciprocal(rdeg[e], degree[e]))
            for b in range(B):
                dve.wait_ge(S["beta_psum"], b + 1)
                v.tensor_copy(beta[e, b * D:(b + 1) * D], bank(b)[e]).then_inc(S["beta_sb"], 1)
            dve.wait_ge(S["m1_in"], 48)
            dve.wait_ge(S["x0_ready"], B)
            for b in range(B):
                dve.wait_ge(S["agg_psum"], b + 1)
                q = 2 * (b % 2)
                step(v.scalar_tensor_tensor(xv[e, b], bank(q + 1)[e], rdeg[e, b:b + 1], xv[e, b], ALU.mult, ALU.add))
                step(v.tensor_tensor(xv[e, b], bank(q)[e], xv[e, b], ALU.add))
                v.tensor_tensor(xv[e, b], xv[e, b], bias1[e], ALU.add).then_inc(S["agg_used"], 1)
            dve.wait_ge(S["agg_used"], B)
            norm(1, xv, S["x0_ready"])
            dve.wait_ge(S["x0_ready"], 2 * B)
            step(v.tensor_copy(xres[e, :], x[e, :]))
            v.tensor_scalar(mask[e], cnt_sd[e, :], 0.0, FAR, ALU.is_equal, ALU.mult).then_inc(S["stage7"], 1)
            dve.wait_ge(S["stage7"], 1)

            STEPS7 = 2 * NORM + 2 * C + 5 * H * B + 2 * B
            with dve.Fori(0, L) as l:
                step.enter(l, STEPS7)

                def modulate(h):
                    norm(2 * l + 2 + h, xnv, S["xn_ready"])
                    for c in range(C):
                        dve.wait_ge(S["mod_sc"], l * (2 * C) + h * C + c + 1)
                        step(v.tensor_tensor(blocks(yTv[:, c]), pair(0)[:, :, e], blocks(yTv[:, c]), ALU.mult))
                        v.tensor_tensor(blocks(yTv[:, c]), pair(2)[:, :, e], blocks(yTv[:, c]), ALU.add
                                        ).then_inc(S["mod_done"], 1)

                modulate(0)
                dve.wait_ge(S["w_in0"], 32 * l + 32)
                for h in range(H):
                    dve.wait_ge(S["qk_psum"], l * (2 * H) + 2 * h + 1)
                    v.tensor_scalar(blocks(qT[:, h * N:(h + 1) * N]), pair(2 * h % 4)[:, :, e], wcol[0][:, h:h + 1],
                                    float(P) ** -0.5, ALU.add, ALU.mult).then_inc(S["q_done"], 1)
                dve.wait_ge(S["w_in2"], 32 * l + 32)
                for b in range(B):
                    dve.wait_ge(S["v_psum"], l * B + b + 1)
                    v.tensor_tensor(vN[e, b * D:(b + 1) * D], bank(b)[e], wb[0][e], ALU.add
                                    ).then_inc(S["v_done"], 1)
                for u in range(H * B + 1):
                    if u < H * B:
                        z, s = u % 2, u % B
                        dve.wait_ge(S["s_psum"], l * (H * B) + u + 1)
                        v.tensor_tensor(blocks(sm[z][e]), pair(z)[e, :, e], blocks(mask[e, s * N:(s + 1) * N]),
                                        ALU.add).then_inc(S["s_read"], 1)
                        dve.wait_ge(S["s_read"], l * (H * B) + u + 1)
                        step(v.tensor_reduce(small[e, z:z + 1], sm[z][e], AX.X, ALU.max))
                        v.tensor_scalar(small[e, 2 + z:3 + z], small[e, z:z + 1], -1.0, None, ALU.mult
                                        ).then_inc(S["sm_ready"], 1)
                    if u > 0:
                        z, s = (u - 1) % 2, (u - 1) % B
                        dve.wait_ge(S["e_ready"], l * (H * B) + u)
                        if u > 2:
                            dve.wait_ge(S["pt_psum"], l * (H * (B + 1)) + (u - 3) + (u - 3) // B + 1)
                        step(v.tensor_tensor_reduce(pr[z][e], ex[z][e], csd[e, s], 1.0, 0.0, ALU.mult, ALU.add,
                                                    small[e, 4 + z:5 + z]))
                        step(v.tensor_scalar(small[e, 6 + z:7 + z], small[e, 4 + z:5 + z], 1.0e-30, None, ALU.max))
                        step(v.reciprocal(small[e, 8 + z:9 + z], small[e, 6 + z:7 + z]))
                        step(v.tensor_scalar(dg[z][e], ident[e, e], small[e, 8 + z:9 + z], None, ALU.mult))
                        v.sem_inc(S["p_ready"], 1)
                dve.wait_ge(S["w_in3"], 32 * l + 32)
                for b in range(B):
                    dve.wait_ge(S["wo_psum"], l * B + b + 1)
                    step(v.tensor_tensor(xv[e, b], bank(b)[e], xv[e, b], ALU.add))
                    v.tensor_tensor(xv[e, b], xv[e, b], wb[1][e], ALU.add).then_inc(S["x_upd"], 1)
                dve.wait_ge(S["x_upd"], l * (2 * B) + B)
                modulate(1)
                dve.wait_ge(S["w_in5"], 32 * l + 32)
                for b in range(B):
                    dve.wait_ge(S["m2_psum"], l * B + b + 1)
                    step(v.tensor_tensor(xv[e, b], bank(b)[e], xv[e, b], ALU.add))
                    v.tensor_tensor(xv[e, b], xv[e, b], wb[2][e], ALU.add).then_inc(S["x_upd"], 1)
                dve.wait_ge(S["x_upd"], l * (2 * B) + 2 * B)
            step.leave(L)
            step(v.tensor_tensor(x[e, :], x[e, :], xres[e, :], ALU.add))
            norm(2 * L + 2, xv, S["x0_ready"])
            dve.wait_ge(S["x0_ready"], 3 * B)
            v.tensor_copy(xres[e, :], x[e, :]).then_inc(S["stage8"], 1)
            dve.wait_ge(S["stage8"], 1)

            with dve.Fori(0, NT // U) as i:
                for j in range(U):
                    dve.wait_ge(S["ohw_free"], i * U + j + 1)
                    one_hot(ohw[j][:, 0:NB], iota_nb, i * U + j, 0).then_inc(S["ohw_ready"], 1)
                    v.tensor_copy(ohw[j][:, NB:P], w3[:, ds((i * U + j) * 3, 3)]).then_inc(S["ohw_ready"], 1)

            STEPS8 = 1 + 2 * C + 4 + B
            with dve.Fori(0, L) as l:
                step.enter(l, STEPS8)
                dve.wait_ge(S["we_in"], 112 * l + 112)
                v.tensor_tensor(xst[e].rearrange("p (b d) -> p b d", b=B), xv[e],
                                gb_e[e].unsqueeze(1).broadcast_to([NB, B, D]), ALU.add).then_inc(S["xst_ready"], 1)
                dve.wait_ge(S["xst_ready"], l + 1)
                dve.wait_ge(S["part0"], l + 1)
                v.tensor_tensor(xst, xst, xp[0], ALU.subtract).then_inc(S["rest1"], 1)
                dve.wait_ge(S["part1"], l + 1)
                v.tensor_tensor(xp[2], xst, xp[1], ALU.subtract).then_inc(S["parts"], 1)
                with dve.Fori(0, NT // U) as i:
                    for j in range(U):
                        dve.wait_ge(S["tile_free"], l * NT + i * U + j + 1)
                        one_hot(odf[j], iota_n[:, :], i * U + j, 1).then_inc(S["odf_ready"], 1)
                dve.wait_ge(S["tile_free"], l * NT + NT + U)
                step(v.tensor_scalar(gep1[e], geps[e], 1.0, None, ALU.add))
                for b in range(B):
                    v.scalar_tensor_tensor(xnv[e, b], xv[e, b], gep1[e], bank(b)[e], ALU.mult, ALU.add
                                           ).then_inc(S["xa_ready"], 1)
                for c in range(C):
                    dve.wait_ge(S["xat_psum"], l * C + c + 1)
                    v.tensor_copy(blocks(yTv[:, c]), pair(c)[:, :, e]).then_inc(S["xat_sb"], 1)
                for c in range(C):
                    dve.wait_ge(S["h1_sb"], l * C + c + 1)
                    step(v.bn_stats(st6[:, c * 12:c * 12 + 6], hp[:, c * N:c * N + 500]))
                    step(v.bn_stats(st6[:, c * 12 + 6:c * 12 + 12], hp[:, c * N + 500:(c + 1) * N]))
                dve.sem_inc(S["dve_go"], 1)
                for c in range(C):
                    v.bn_aggr(mvv[:, c], st6[:, c * 12:c * 12 + 12]).then_inc(S["bn_var"], 1)
                dve.wait_ge(S["bn_std"], l + 1)
                step(v.reciprocal(bnc[:, 0:C], std[:, 0:C]))
                step(v.tensor_tensor(bnc[:, C:2 * C], bnc[:, 0:C], gcv[:, 1], ALU.mult))
                step(v.tensor_tensor(bnc[:, 2 * C:3 * C], mvv[:, 0:C, 0], bnc[:, C:2 * C], ALU.mult))
                step(v.tensor_tensor(bnc[:, 3 * C:4 * C], gcv[:, 2], bnc[:, 2 * C:3 * C], ALU.subtract))
                v.sem_inc(S["bn_ready"], 1)
                dve.wait_ge(S["g2_in"], 32 * l + 32)
                for b in range(B):
                    dve.wait_ge(S["h2_psum"], l * B + b + 1)
                    step(v.tensor_tensor(xnv[e, b], bank(b)[e], gb_2[e], ALU.add))
                    v.tensor_scalar(xv[e, b], xnv[e, b], 0.0, None, ALU.max).then_inc(S["x_new"], 1)
                dve.wait_ge(S["x_new"], l * B + B)
            step.leave(L)
            step(v.tensor_tensor(x[e, :], x[e, :], xres[e, :], ALU.add))
            norm(2 * L + 3, xnv, S["out_ready"])

        @block.scalar
        def _(act):
            s = nc.scalar

            def norm_std(ln):
                act.wait_ge(S["ln_var"], ln * B + B)
                s.activation(std[e, :], mvv[e, :, 1], ACT.Sqrt, bias=eps_c[e, :]).then_inc(S["ln_std"], 1)

            act.wait_ge(S["ph_ready"], 1)
            s.activation(emb[0:2 * NF], ph[0:2 * NF], ACT.Sin).then_inc(S["emb_ready"], 1)
            cd = slice(0, CD)
            act.wait_ge(S["z1_psum"], 1)
            s.activation(blocks(z1[cd]), pair(3)[cd, :, e], ACT.Identity, bias=fb1[cd]).then_inc(S["act_step"], 1)
            act.wait_ge(S["act_step"], 1)
            s.activation(z2[cd], z1[cd], ACT.Exp, scale=-1.0).then_inc(S["z1_exp"], 1)
            act.wait_ge(S["z2_psum"], 1)
            s.activation(blocks(condT[cd, :]), pair(3)[cd, :, e], ACT.Identity, bias=fb2[cd]
                         ).then_inc(S["cond_ready"], 1)

            act.wait_ge(S["cnt_free"], NT + U)
            s.activation(cds[e], banks[e, 0:K * P].rearrange("p (k n) -> p k n", n=P)[:, :, e], ACT.Copy
                         ).then_inc(S["cnt_sb"], 1)
            act.wait_ge(S["csd_psum"], 1)
            s.activation(cnt_sd[e, :].rearrange("p (k n) -> p k n", n=NB),
                         banks[e, 0:K * P].rearrange("p (k n) -> p k n", n=P)[:, :, e], ACT.Copy
                         ).then_inc(S["csd_sb"], 1)

            norm_std(0)
            for c in range(C):
                act.wait_ge(S["t_psum"], c + 1)
                s.activation(blocks(yTv[:, c]), pair(c)[:, :, e], ACT.Copy).then_inc(S["t_sb"], 1)
            norm_std(1)

            with act.Fori(0, L) as l:
                def modulate(h):
                    norm_std(2 * l + 2 + h)
                    for c in range(C):
                        act.wait_ge(S["mod_psum"], l * (2 * C) + h * C + c + 1)
                        s.activation(blocks(yTv[:, c]), pair(1)[:, :, e], ACT.Identity, bias=ones[:, 0:1]
                                     ).then_inc(S["mod_sc"], 1)

                modulate(0)
                act.wait_ge(S["w_in1"], 32 * l + 32)
                for h in range(H):
                    act.wait_ge(S["qk_psum"], l * (2 * H) + 2 * h + 2)
                    s.activation(blocks(kT[:, h * N:(h + 1) * N]), pair((2 * h + 1) % 4)[:, :, e], ACT.Identity,
                                 bias=wcol[1][:, h:h + 1]).then_inc(S["k_done"], 1)
                for u in range(H * B + 2):
                    if u < H * B:
                        act.wait_ge(S["sm_ready"], l * (H * B) + u + 1)
                        if u > 1:
                            act.wait_ge(S["p_ready"], l * (H * B) + u - 1)
                        s.activation(ex[u % 2][e], sm[u % 2][e], ACT.Exp, bias=small[e, 2 + u % 2:3 + u % 2]
                                     ).then_inc(S["e_ready"], 1)
                    if u >= 2 and (u - 2) % B == B - 1:
                        h = (u - 2) // B
                        n = h * (B + 1) + B
                        act.wait_ge(S["pt_psum"], l * (H * (B + 1)) + n + 1)
                        s.activation(blocks(oT[:, h * N:(h + 1) * N]), pair(2 + n % 2)[:, :, e], ACT.Copy
                                     ).then_inc(S["pt_done"], 1)
                    if 1 <= u <= H * B:
                        n, sblk = (u - 1) + (u - 1) // B, (u - 1) % B
                        act.wait_ge(S["pt_psum"], l * (H * (B + 1)) + n + 1)
                        s.activation(pT[e].rearrange("p (d n) -> p d n", d=B)[:, :, sblk * NB:(sblk + 1) * NB],
                                     pair(2 + n % 2)[e, :, e], ACT.Copy).then_inc(S["pt_done"], 1)
                modulate(1)
                act.wait_ge(S["w_in4"], 32 * l + 32)
                for c in range(C):
                    act.wait_ge(S["m1_psum"], l * C + c + 1)
                    s.activation(blocks(qT[:, c * N:(c + 1) * N]), pair(c)[:, :, e], ACT.Relu,
                                 bias=wcol[2][:, c:c + 1]).then_inc(S["h_done"], 1)
            norm_std(2 * L + 2)

            act.wait_ge(S["stage8"], 1)
            psum_bf = [bank(5 + j).bitcast(BF16) for j in range(U)]
            with act.Fori(0, NT // U) as i:
                for j in range(U):
                    act.wait_ge(S["st_psum"], i * U + j + 1)
                    s.activation(stat[:, ds((i * U + j) * P, P)], psum_bf[j][:, 0:P], ACT.Copy
                                 ).then_inc(S["ohw_free"], 1)
            with act.Fori(0, L) as l:
                act.wait_ge(S["xst_ready"], l + 1)
                act.wait_ge(S["we_in"], 112 * l + 112)
                s.activation(xp[0], xst, ACT.Copy).then_inc(S["part0"], 1)
                act.wait_ge(S["rest1"], l + 1)
                s.activation(xp[1], xst, ACT.Copy).then_inc(S["part1"], 1)
                with act.Fori(0, NT // U) as i:
                    for j in range(U):
                        act.wait_ge(S["u_psum"], l * NT + i * U + j + 1)
                        act.wait_ge(S["tile_free"], l * NT + i * U + j + 1)
                        s.activation(msg[j], bank(5 + j), ACT.Relu).then_inc(S["msg_ready"], 1)
                act.wait_ge(S["g_in"], 32 * l + 32)
                for c in range(C):
                    act.wait_ge(S["h1_psum"], l * C + c + 1)
                    s.activation(blocks(hp[:, c * N:(c + 1) * N]), pair(c)[:, :, e], ACT.Identity,
                                 bias=gcv[:, 0, c:c + 1]).then_inc(S["h1_sb"], 1)
                act.wait_ge(S["bn_var"], l * C + C)
                s.activation(std[:, 0:C], mvv[:, 0:C, 1], ACT.Sqrt, bias=eps_c[:, :]).then_inc(S["bn_std"], 1)
                act.wait_ge(S["bn_ready"], l + 1)
                for c in range(C):
                    s.activation(hp[:, c * N:(c + 1) * N], hp[:, c * N:(c + 1) * N], ACT.Relu,
                                 bias=bnc[:, 3 * C + c:3 * C + c + 1], scale=bnc[:, C + c:C + c + 1]
                                 ).then_inc(S["hp_ready"], 1)
            norm_std(2 * L + 3)

        @block.tensor
        def _(pe):
            mm = nc.tensor.matmul

            def wide_mm(out_pair, lhsT, rhs, **flags):
                r = blocks(rhs)
                mm(out_pair[:, 0:4, e], lhsT, r[:, 0:4], **flags)
                return mm(out_pair[:, 4, e], lhsT, r[:, 4], **flags)

            def project(b, bnk, left, weight):
                for c in range(C):
                    ins = mm(bank(bnk)[e], left[:, c, b * NB:(b + 1) * NB], weight[:, c * D:(c + 1) * D],
                             start=(c == 0), stop=(c == C - 1))
                return ins

            def turn_chunk(c, where, src):
                for b in range(B):
                    ins = nc.tensor.transpose(pair(where)[:, b, e], src[e, b, c * P:(c + 1) * P], ident[e, e])
                return ins

            def clear(n):
                for q in range(n):
                    mm(bank(q)[e], zerob[:, e], zerob[:, :], start=True, stop=False, skip_group_check=True)

            def column(table, t, bound):
                return pe.value_load(table[0:1, ds(t, 1)], min_val=0, max_val=bound)

            pe.wait_ge(S["x_in"], 16)
            pe.wait_ge(S["wr_in0"], 32)
            for b in range(B):
                project(b, b, xTv, wr[0]).then_inc(S["proj_psum"], 1)
            pe.wait_ge(S["consts"], 1)
            pe.wait_ge(S["totals"], 1)
            tot = small[e, 0:K]
            mm(bank(7)[e, 0:K], earlier[e, e], tot, start=True, stop=True)
            mm(bank(7)[:, 32:32 + K], ones[e, :], tot, start=True, stop=True).then_inc(S["offsets_mm"], 1)
            with pe.Fori(0, R) as i:
                for j in (1, 0):
                    pe.wait_ge(S[f"wr_in{j}"], 32 * i + 64 - 32 * j)
                    for b in range(B):
                        pe.wait_ge(S["proj_free"], (2 * i + 2 - j) * B + b + 1)
                        project(b, b, xTv, wr[j]).then_inc(S["proj_psum"], 1)

            pe.wait_ge(S["emb_ready"], 1)
            pe.wait_ge(S["fnet_in"], 80)
            pe.wait_ge(S["slot_addr"], 1)
            wide_mm(pair(3)[0:CD], fw1[0:2 * NF], emb[0:2 * NF], start=True, stop=True).then_inc(S["z1_psum"], 1)
            pe.wait_ge(S["z1_ready"], 1)
            wide_mm(pair(3)[0:CD], fw2[0:CD], z1[0:CD], start=True, stop=True).then_inc(S["z2_psum"], 1)

            pe.wait_ge(S["proj_free"], B * (2 * R + 2))
            pe.wait_ge(S["cond_ready"], 1)
            pe.wait_ge(S["tables"], 3)
            clear(7)
            with pe.Fori(0, NT // U) as i:
                for j in range(U):
                    at = column(tab_k, i * U + j, (K - 1) * P)
                    pe.wait_ge(S["onehots"], (i * U + j) * 2 + 2)
                    mm(banks[e, ds(at, NB)], oh_d[j], oh_s[j], start=False, stop=False, skip_group_check=True
                       ).then_inc(S["cnt_free"], 1)
            pe.wait_ge(S["cnt_sb"], 1)
            for s in range(B):
                for d in range(B):
                    k = s * B + d
                    ins = nc.tensor.transpose(banks[e, k * P:k * P + NB], cds[e, d * B + s], ident[e, e])
            ins.then_inc(S["csd_psum"], 1)

            pe.wait_ge(S["csd_sb"], 1)
            clear(B)
            with pe.Fori(0, NT // U) as i:
                for j in range(U):
                    at_s = column(tab_s, i * U + j, (B - 1) * D)
                    at_d = column(tab_d, i * U + j, (B - 1) * D)
                    pe.wait_ge(S["onef"], (i * U + j) * 2 + 2)
                    pe.wait_ge(S[f"got{j}"], 32 * i + 32)
                    mm(banks[e, ds(at_s, D)], ohf_s[j], got[j][0], start=False, stop=False, skip_group_check=True)
                    mm(banks[e, ds(at_d, D)], ohf_d[j], got[j][1], start=False, stop=False, skip_group_check=True
                       ).then_inc(S["msg_free"], 1)

            pe.wait_ge(S["x0_ready"], B)
            for c in range(C):
                turn_chunk(c, c, xv).then_inc(S["t_psum"], 1)
            pe.wait_ge(S["t_sb"], C)
            pe.wait_ge(S["m1_in"], 48)
            for b in range(B):
                project(b, b, yTv, wn).then_inc(S["beta_psum"], 1)
            pe.wait_ge(S["beta_sb"], B)
            for b in range(B):
                q = 2 * (b % 2)
                if b >= 2:
                    pe.wait_ge(S["agg_used"], b - 1)
                project(b, q, yTv, wc)
                for d in range(B):
                    ins = mm(bank(q + 1)[e], cds[e, d * B + b], beta[e, d * D:(d + 1) * D],
                             start=(d == 0), stop=(d == B - 1))
                ins.then_inc(S["agg_psum"], 1)

            with pe.Fori(0, L) as l:
                def modulate(h):
                    pe.wait_ge(S["xn_ready"], l * (2 * B) + h * B + B)
                    pe.wait_ge(S[f"ln_in{h}"], 64 * l + 64)
                    for c in range(C):
                        if c > 0:
                            pe.wait_ge(S["mod_done"], l * (2 * C) + h * C + c)
                        turn_chunk(c, 0, xnv)
                        for q in range(2):
                            ins = wide_mm(pair(1 + q), lnw[2 * h + q][0:CD + 1, c * P:(c + 1) * P], condT[:, :],
                                          start=True, stop=True)
                        ins.then_inc(S["mod_psum"], 1)
                    pe.wait_ge(S["mod_done"], l * (2 * C) + h * C + C)

                def wide_project(where, left, o):
                    for c in range(C):
                        ins = wide_mm(pair(where), left[:, c * D + o * P:c * D + (o + 1) * P], yTv[:, c],
                                      start=(c == 0), stop=(c == C - 1))
                    return ins

                modulate(0)
                pe.wait_ge(S["w_in0"], 32 * l + 32)
                pe.wait_ge(S["w_in1"], 32 * l + 32)
                for h in range(H):
                    for q, done in enumerate(("q_done", "k_done")):
                        if h >= 2:
                            pe.wait_ge(S[done], l * H + h - 1)
                        wide_project((2 * h + q) % 4, w2[q], h).then_inc(S["qk_psum"], 1)
                pe.wait_ge(S["q_done"], l * H + H)
                pe.wait_ge(S["k_done"], l * H + H)
                pe.wait_ge(S["w_in2"], 32 * l + 32)
                for b in range(B):
                    project(b, b, yTv, w2[2]).then_inc(S["v_psum"], 1)
                pe.wait_ge(S["v_done"], l * B + B)
                for u in range(H * B + 2):
                    if u < H * B:
                        h, sblk = u // B, u % B
                        if u >= 2:
                            pe.wait_ge(S["s_read"], l * (H * B) + u - 1)
                        wide_mm(pair(u % 2)[e], qT[:, h * N + sblk * NB:h * N + (sblk + 1) * NB],
                                kT[:, h * N:(h + 1) * N], start=True, stop=True).then_inc(S["s_psum"], 1)
                    if u >= 2 and (u - 2) % B == B - 1:
                        h = (u - 2) // B
                        n = h * (B + 1) + B
                        pe.wait_ge(S["pt_done"], l * (H * (B + 1)) + n)
                        for d in range(B):
                            ins = wide_mm(pair(2 + n % 2), vN[e, d * D + h * P:d * D + (h + 1) * P],
                                          pT[e, d * N:(d + 1) * N], start=(d == 0), stop=(d == B - 1))
                        ins.then_inc(S["pt_psum"], 1)
                    if 1 <= u <= H * B:
                        n, z = (u - 1) + (u - 1) // B, (u - 1) % 2
                        pe.wait_ge(S["p_ready"], l * (H * B) + u)
                        if n >= 2:
                            pe.wait_ge(S["pt_done"], l * (H * (B + 1)) + n - 1)
                        for d in range(B):
                            ins = mm(pair(2 + n % 2)[e, d, e], pr[z][e, d * NB:(d + 1) * NB], dg[z][e],
                                     start=True, stop=True)
                        ins.then_inc(S["pt_psum"], 1)
                pe.wait_ge(S["s_read"], l * (H * B) + H * B)
                pe.wait_ge(S["pt_done"], l * (H * (B + 1)) + H * (B + 1))
                pe.wait_ge(S["w_in3"], 32 * l + 32)
                oTv = oT.rearrange("p (c n) -> p c n", c=C)
                for b in range(B):
                    project(b, b, oTv, w2[3]).then_inc(S["wo_psum"], 1)
                modulate(1)
                pe.wait_ge(S["w_in4"], 32 * l + 32)
                for c in range(C):
                    wide_project(c, w2[4], c).then_inc(S["m1_psum"], 1)
                pe.wait_ge(S["h_done"], l * C + C)
                pe.wait_ge(S["w_in5"], 32 * l + 32)
                hT = qT.rearrange("p (c n) -> p c n", c=C)
                for b in range(B):
                    project(b, b, hT, w2[5]).then_inc(S["m2_psum"], 1)

            psum_bf = [bank(5 + j).bitcast(BF16) for j in range(U)]
            with pe.Fori(0, NT // U) as i:
                for j in range(U):
                    pe.wait_ge(S["ohw_free"], i * U + j + 1)
                    pe.wait_ge(S["ohw_ready"], (i * U + j) * 2 + 2)
                    nc.tensor.transpose(psum_bf[j][:, 0:P], ohw[j], identb[:, :]).then_inc(S["st_psum"], 1)
            pe.wait_ge(S["ohw_free"], NT + U)
            with pe.Fori(0, L) as l:
                pe.wait_ge(S["parts"], l + 1)
                clear(B)
                with pe.Fori(0, NT // U) as i:
                    for j in range(U):
                        at = column(tab_s, i * U + j, (B - 1) * D)
                        pe.wait_ge(S["tile_free"], l * NT + i * U + j + 1)
                        for q in range(3):
                            ins = mm(bank(5 + j), stat[:, ds((i * U + j) * P, P)], xp[q][:, ds(at, D)],
                                     start=(q == 0), stop=(q == 2))
                        ins.then_inc(S["u_psum"], 1)
                    for j in range(U):
                        at = column(tab_d, i * U + j, (B - 1) * D)
                        pe.wait_ge(S["odf_ready"], l * NT + i * U + j + 1)
                        pe.wait_ge(S["msg_ready"], l * NT + i * U + j + 1)
                        mm(banks[e, ds(at, D)], odf[j], msg[j], start=False, stop=False, skip_group_check=True
                           ).then_inc(S["tile_free"], 1)
                pe.wait_ge(S["xa_ready"], l * B + B)
                for c in range(C):
                    turn_chunk(c, c, xnv).then_inc(S["xat_psum"], 1)
                pe.wait_ge(S["xat_sb"], l * C + C)
                pe.wait_ge(S["g_in"], 32 * l + 32)
                for o in range(C):
                    for c in range(C):
                        ins = wide_mm(pair(o), g1[:, c * D + o * P:c * D + (o + 1) * P], yTv[:, c],
                                      start=(c == 0), stop=(c == C - 1))
                    ins.then_inc(S["h1_psum"], 1)
                pe.wait_ge(S["hp_ready"], l * C + C)
                pe.wait_ge(S["g2_in"], 32 * l + 32)
                hpv = hp.rearrange("p (c n) -> p c n", c=C)
                for b in range(B):
                    project(b, b, hpv, g2).then_inc(S["h2_psum"], 1)
                pe.wait_ge(S["x_new"], l * B + B)


def kernel(**inputs):
    import numpy as np
    import concourse.bacc as bacc
    from concourse.bass_utils import run_bass_kernel_spmd

    i = {n: np.asarray(v) for n, v in inputs.items()}

    def columns(v):
        return v.reshape(L, C, P).transpose(0, 2, 1)

    arrays = {n: v for n, v in i.items() if n.startswith(("L1_", "L2_", "L3_")) and n not in (
        "L2_gnn_bq", "L2_gnn_bk", "L2_gnn_m_b1", "L3_gnn_eps", "L3_gnn_b1", "L3_gnn_gamma", "L3_gnn_beta")}
    arrays["L1_gnn_bias"] = i["L1_gnn_bias"].reshape(1, D)
    arrays["L2_gnn_f_b1"] = i["L2_gnn_f_b1"].reshape(CD, 1)
    arrays["L2_gnn_f_b2"] = i["L2_gnn_f_b2"].reshape(CD, 1)
    arrays["x"] = i["x"]
    arrays["xT"] = i["x"].T
    for n in ("src", "dst", "edge_type_8", "edge_weight1"):
        arrays[n] = i[n].reshape(NB, EC)
    arrays["node_vec1"] = i["node_vec1"].reshape(1, N)
    arrays["W0"] = np.concatenate([i["L0_gnn_W_self"][None], i["L0_gnn_W_rel"]]).transpose(0, 2, 1)
    arrays["b0"] = np.concatenate([i["L0_gnn_b_self"][None], i["L0_gnn_b_rel"]])
    for n in ("bq", "bk", "m_b1"):
        arrays[n] = columns(i["L2_gnn_" + n])
    arrays["eps3"] = i["L3_gnn_eps"].reshape(L, 1)
    arrays["L3_gnn_We"] = i["L3_gnn_We"].reshape(L, D)
    arrays["cols3"] = np.concatenate([columns(i["L3_gnn_" + n]) for n in ("b1", "gamma", "beta")], axis=2)
    arrays = {n: np.ascontiguousarray(v) for n, v in arrays.items()}

    nc = bacc.Bacc("TRN2", target_bir_lowering=False, num_devices=1)
    aps = {n: nc.dram_tensor("in_" + n, v.shape, mybir.dt.from_np(v.dtype), kind="ExternalInput").ap()
           for n, v in arrays.items()}
    out = nc.dram_tensor("out_x", (N, D), F32, kind="ExternalOutput").ap()
    gnn_stack(nc, aps, out)
    r = run_bass_kernel_spmd(nc, [{"in_" + n: v for n, v in arrays.items()}], core_ids=[0])
    return r.results[0]["out_x"]
```

```python
from contextlib import ExitStack
from math import pi

import concourse.bass as bass
from concourse import mybir

F32 = mybir.dt.float32
BF16 = mybir.dt.bfloat16
I32 = mybir.dt.int32
U32 = mybir.dt.uint32
ALU = mybir.AluOpType
ACT = mybir.ActivationFunctionType
AX = mybir.AxisListType
ds = bass.ds

P = 128
N = 625
NB = 125
B = N // NB
D = 512
C = D // P
E = 20000
EC = E // NB
R = 8
K = B * B
U = 3
G = 10
NT = -(-(E // P + K + 1) // U) * U
H = 4
L = 4
NF = 32
CD = 16
EPS = 1e-5
FAR = -1.0e30
assert NT * P >= E + K * (P - 1)


class Chain:

    def __init__(self, eng, sem):
        self.eng, self.sem, self.base, self.n = eng, sem, 0, 0

    def __call__(self, ins):
        ins.then_inc(self.sem, 1)
        self.n += 1
        self.eng.wait_ge(self.sem, self.base + self.n)

    def enter(self, i, per):
        self.start, self.per = self.base + self.n, per
        self.base, self.n = i * per + self.start, 0

    def leave(self, times):
        assert self.n == self.per, self.n
        self.base, self.n = self.start + times * self.per, 0


def gnn_stack(nc, a, out):
    ctx = ExitStack()
    with ctx:
        def sb(name, shape, dt=F32):
            return ctx.enter_context(nc.sbuf_tensor(name, shape, dt))

        banks = ctx.enter_context(nc.psum_tensor("banks", [P, 8 * D], F32))

        def bank(i):
            return banks[:, i * D:(i + 1) * D]

        def pair(i):
            return banks[:, 2 * i * D:2 * i * D + B * P].rearrange("p (b n) -> p b n", n=P)

        def chunks(t):
            return t[:, 0:C * NB].rearrange("p (c n) -> p c n", c=C)

        def blocks(t):
            return t.rearrange("p (b n) -> p b n", n=NB)

        ident = sb("ident", [P, P])
        identb = sb("identb", [P, P], BF16)
        ones = sb("ones", [P, P])
        earlier = sb("earlier", [P, P])
        zerob = sb("zerob", [P, D], BF16)
        iota_n = sb("iota_n", [P, NB])
        iota_nb = sb("iota_nb", [P, NB + 3], BF16)[:, 0:NB]
        iota_k = sb("iota_k", [P, K])
        iota_t = sb("iota_t", [P, NT])
        freq = sb("freq", [2 * NF, 1])
        turn = sb("turn", [2 * NF, 2])
        eps_c = sb("eps_c", [P, 1])

        meta = sb("meta", [P, NT * 4])
        meta4 = meta[:, :].rearrange("p (t v) -> p t v", v=4)
        tab_k = sb("tab_k", [P, NT // U], I32)
        tab_sd = sb("tab_sd", [P, NT // U], I32)
        w3 = sb("w3", [P, NT * 3], BF16)
        w3v = w3[:, :].rearrange("p (t v) -> p t v", v=3)
        rows_of = sb("rows_of", [P, NT * 2], U32)
        rows_v = rows_of[:, :].rearrange("p (t v) -> p t v", v=2)
        rows_now = [sb(f"rows_now{j}", [P, 2], U32)[:, :] for j in range(U)]
        pay_now = [sb(f"pay_now{j}", [P, G * 4])[:, :] for j in range(2)]
        addr_now = [sb(f"addr_now{j}", [P, G], U32)[:, :] for j in range(2)]
        x = sb("x", [P, B * D])
        xv = x[:, :].rearrange("p (b d) -> p b d", b=B)
        xn = sb("xn", [P, B * D])
        xnv = xn[:, :].rearrange("p (b d) -> p b d", b=B)
        xres = sb("xres", [P, B * D])
        xresv = xres[:, :].rearrange("p (b d) -> p b d", b=B)
        yT = sb("yT", [P, C * N])
        yTv = yT[:, :].rearrange("p (c n) -> p c n", c=C)
        cnt_sd = sb("cnt_sd", [P, B * N])
        csd = cnt_sd[:, :].rearrange("p (s n) -> p s n", s=B)
        condT = sb("condT", [CD + 1, N])
        st6 = sb("st6", [P, B * 12])
        mv = sb("mv", [P, B * 2])
        mvv = mv[:, :].rearrange("p (b v) -> p b v", v=2)
        std = sb("std", [P, B])
        rstd = sb("rstd", [P, B])
        small = sb("small", [P, 64])

        ARENA = 34800
        arena = sb("arena", [P, ARENA])
        top = [0]

        def take(words, dt=F32):
            at = top[0]
            top[0] += words
            assert top[0] <= ARENA, top[0]
            v = arena[:, at:at + words]
            return v if dt == F32 else v.bitcast(dt)

        member = take(K * EC)
        rank = take(K * EC)
        wc, wn = take(C * D), take(C * D)
        bias1 = take(D)
        degree, rdeg = take(B), take(B)
        beta = xn[:, :]
        src_i, dst_i, rel_i = take(EC, I32), take(EC, I32), take(EC, I32)
        w_in = take(EC)
        s_f, d_f, s_b, d_b, key, pos = (take(EC) for _ in range(6))
        pos_i, slot_t, slot_p = (take(EC, I32) for _ in range(3))
        addr = take(EC, U32)
        payload = take(EC * 4)
        pads = take(NT * 4)
        xT = take(C * N)
        xTv = xT.rearrange("p (c n) -> p c n", c=C)
        wr = [take(C * D) for _ in range(2)]
        br = [take(D) for _ in range(2)]
        hst = [take(B * D) for _ in range(2)]
        hself = take(B * D)
        tk, tdb, tsb, t0 = (take(NT) for _ in range(4))
        tiles_i = take(K, I32)
        emb = take(N)
        ph = take(N)
        emb_i = take(N, I32)
        z1, z2 = emb, ph
        fw1, fw2 = take(CD), take(CD)
        fb1, fb2 = take(1), take(1)
        top[0] = 0
        oh_s = [take(64, BF16)[:, 0:NB] for _ in range(U)]
        oh_d = [take(64, BF16)[:, 0:NB] for _ in range(U)]
        ohf_s = [take(NB) for _ in range(U)]
        ohf_d = [take(NB) for _ in range(U)]
        got = [[take(D) for _ in range(2)] for _ in range(U)]
        cnt_ds = take(B * N)
        cds = cnt_ds.rearrange("p (k n) -> p k n", n=NB)
        assert top[0] <= 2 * K * EC
        top[0] = 0
        w2 = [take(C * D) for _ in range(6)]
        wb = [take(D) for _ in range(3)]
        wcol = [take(C) for _ in range(3)]
        lnw = [take(D) for _ in range(4)]
        mask = take(B * N)
        qT, kT, vN = take(C * N), take(C * N), take(B * D)
        oT = qT
        sm, ex, pr = ([take(N) for _ in range(2)] for _ in range(3))
        dg = [take(NB) for _ in range(2)]
        pT = take(B * N)
        top[0] = 0
        stat = take(NT * P // 2, BF16)
        xp = [take(B * D // 2, BF16) for _ in range(3)]
        xst = take(B * D)
        g1, g2 = take(C * D), take(C * D)
        gb_e, gb_2 = take(D), take(D)
        gcol = take(3 * C)
        gcv = gcol.rearrange("p (v c) -> p v c", v=3)
        geps, gep1 = take(1), take(1)
        msg = [take(D) for _ in range(U)]
        odf = [take(NB) for _ in range(U)]
        ohw = [take(64, BF16) for _ in range(U)]
        hp = take(C * N)
        bnc = take(4 * C)

        meta_d = nc.dram_tensor("meta_d", [P * NT, 4], F32, kind="Internal").ap()
        proj_d = nc.dram_tensor("proj_d", [2 * R * N, D], F32, kind="Internal").ap()

        names = """consts edges_in x_in fnet_in pads_made pads_out totals offsets_mm slot_addr
            scattered0 scattered1 addr_set rows_set meta_in tables proj_psum proj_free proj_out0 proj_out1 wr_in0 wr_in1
            onehots cnt_free cnt_psum cnt_sb csd_psum csd_sb got0 got1 got2 onef msg_free msg_done
            ln_var ln_std x0_ready t_psum t_sb m1_in beta_psum beta_sb agg_psum agg_used
            ph_ready emb_ready z1_psum z1_exp z1_ready z2_psum cond_ready stage7 x_biased
            w_in0 w_in1 w_in2 w_in3 w_in4 w_in5 ln_in0 ln_in1 xn_ready mod_psum mod_sc mod_done
            qk_psum q_done k_done v_psum v_done
            s_psum s_read sm_ready e_ready p_ready pt_psum pt_done wo_psum x_upd m1_psum h_done m2_psum
            stage8 we_in g_in g2_in xst_ready part0 rest1 part1 parts ohw_ready ohw_free st_psum st_sb
            u_psum msg_ready odf_ready tile_free tile_done
            xa_ready xat_psum xat_sb h1_psum h1_sb bn_var bn_std bn_ready hp_ready h2_psum x_new out_ready out_done
            pool_go dve_go dve_step act_step pool_step""".split()
        S = {n: ctx.enter_context(nc.semaphore(n)) for n in names}

        block = ctx.enter_context(nc.Block())
        e = slice(0, NB)

        @block.sync
        def _(sp):
            def load_square(dst, src):
                return sp.dma_start(dst.rearrange("p (c o) -> p c o", c=C), src.rearrange("(c p) o -> p c o", p=P))

            def one(ap, i):
                return ap[ds(i, 1)].rearrange("a b c -> (a b) c") if len(ap.shape) == 3 else ap[ds(i, 1)]

            def row_to_all(dst, src_row, n=P):
                return sp.dma_start(dst, src_row.broadcast_to([n, dst.shape[-1]]))

            for dst, name in ((src_i, "src"), (dst_i, "dst"), (rel_i, "edge_type_8"), (w_in, "edge_weight1")):
                sp.dma_start(dst[e, :], a[name]).then_inc(S["edges_in"], 16)
            sp.dma_start(xTv, a["xT"].rearrange("(c p) n -> p c n", p=P)).then_inc(S["x_in"], 16)

            def load_proj(r, j):
                load_square(wr[j], one(a["W0"], r)).then_inc(S[f"wr_in{j}"], 16)
                row_to_all(br[j], one(a["b0"], r)).then_inc(S[f"wr_in{j}"], 16)

            load_proj(0, 0)
            load_proj(1, 1)
            sp.dma_start(xv[e], a["x"].rearrange("(b p) d -> p b d", p=NB)).then_inc(S["x_in"], 16)
            row_to_all(ph[0:2 * NF], a["node_vec1"], 2 * NF).then_inc(S["fnet_in"], 16)
            sp.dma_start(fw1[0:2 * NF, :], a["L2_gnn_f_w1"]).then_inc(S["fnet_in"], 16)
            sp.dma_start(fw2[0:CD, :], a["L2_gnn_f_w2"]).then_inc(S["fnet_in"], 16)
            sp.dma_start(fb1[0:CD, :], a["L2_gnn_f_b1"]).then_inc(S["fnet_in"], 16)
            sp.dma_start(fb2[0:CD, :], a["L2_gnn_f_b2"]).then_inc(S["fnet_in"], 16)
            sp.wait_ge(S["pads_made"], 2)
            sp.dma_start(meta_d.rearrange("(p t) v -> p (t v)", p=P), pads).then_inc(S["pads_out"], 16)
            load_square(wc, a["L1_gnn_wc"]).then_inc(S["m1_in"], 16)
            load_square(wn, a["L1_gnn_wn"]).then_inc(S["m1_in"], 16)
            row_to_all(bias1, a["L1_gnn_bias"]).then_inc(S["m1_in"], 16)

            rows = proj_d.rearrange("(r b p) d -> r p b d", p=NB, b=B)

            def store(r, j):
                sp.dma_start(rows[ds(r - 1, 1)].rearrange("a p b d -> (a p) b d"),
                             hst[j].rearrange("p (b d) -> p b d", b=B)[e]).then_inc(S[f"proj_out{j}"], 16)

            sp.wait_ge(S["proj_free"], B + B)
            load_proj(2, 0)
            with sp.Fori(0, R - 1) as i:
                for j in (1, 0):
                    r = 2 * i + 2 - j
                    sp.wait_ge(S["proj_free"], r * B + 2 * B)
                    store(r, j)
                    load_proj(r + 2, j)
            for j in (1, 0):
                r = 2 * R - j
                sp.wait_ge(S["proj_free"], r * B + 2 * B)
                store(r, j)

            sp.wait_ge(S["scattered0"], 8 * EC)
            sp.wait_ge(S["scattered1"], 8 * EC)
            sp.dma_start(meta[:, :], meta_d.rearrange("(p t) v -> p (t v)", p=P)).then_inc(S["meta_in"], 16)

            def load_w(k, l):
                load_square(w2[k], one(a["L2_gnn_" + ("wq", "wk", "wv", "wo", "m_w1", "m_w2")[k]], l)
                            ).then_inc(S[f"w_in{k}"], 16)
                if k in (0, 1, 4):
                    sp.dma_start(wcol[(0, 1, 4).index(k)], one(a[("bq", "bk", "", "", "m_b1")[k]], l)
                                 ).then_inc(S[f"w_in{k}"], 16)
                else:
                    row_to_all(wb[(2, 3, 5).index(k)], one(a["L2_gnn_" + ("", "", "bv", "bo", "", "m_b2")[k]], l)
                               ).then_inc(S[f"w_in{k}"], 16)

            def load_ln(h, l):
                for q, name in enumerate(("s", "b")):
                    sp.dma_start(lnw[2 * h + q][0:CD, :], one(a[f"L2_gnn_{name}{h + 1}_w"], l)
                                 ).then_inc(S[f"ln_in{h}"], 16)
                    sp.dma_start(lnw[2 * h + q][CD:CD + 1, :], one(a[f"L2_gnn_{name}{h + 1}_b"], l)
                                 ).then_inc(S[f"ln_in{h}"], 16)

            sp.wait_ge(S["stage7"], 1)
            load_ln(0, 0)
            for k in (2, 0, 1, 3):
                load_w(k, 0)
            load_ln(1, 0)
            for k in (4, 5):
                load_w(k, 0)
            with sp.Fori(0, L - 1) as l:
                sp.wait_ge(S["mod_done"], l * (2 * B) + B)
                load_ln(0, l + 1)
                sp.wait_ge(S["v_done"], l * B + B)
                load_w(2, l + 1)
                sp.wait_ge(S["q_done"], l * H + H)
                load_w(0, l + 1)
                sp.wait_ge(S["k_done"], l * H + H)
                load_w(1, l + 1)
                sp.wait_ge(S["x_upd"], l * (2 * B) + B)
                load_w(3, l + 1)
                sp.wait_ge(S["mod_done"], l * (2 * B) + 2 * B)
                load_ln(1, l + 1)
                sp.wait_ge(S["h_done"], l * C + C)
                load_w(4, l + 1)
                sp.wait_ge(S["x_upd"], l * (2 * B) + 2 * B)
                load_w(5, l + 1)

            def load_gine_in(l):
                row_to_all(gb_e, one(a["L3_gnn_be"], l)).then_inc(S["we_in"], 16)
                row_to_all(geps, one(a["eps3"], l)).then_inc(S["we_in"], 16)
                for b in range(B):
                    row_to_all(xst[NB:P, b * D:(b + 1) * D], one(a["L3_gnn_We"], l), P - NB
                               ).then_inc(S["we_in"], 16)

            def load_g1(l):
                load_square(g1, one(a["L3_gnn_W1"], l)).then_inc(S["g_in"], 16)
                sp.dma_start(gcol, one(a["cols3"], l)).then_inc(S["g_in"], 16)

            def load_g2(l):
                load_square(g2, one(a["L3_gnn_W2"], l)).then_inc(S["g2_in"], 16)
                row_to_all(gb_2, one(a["L3_gnn_b2"], l)).then_inc(S["g2_in"], 16)

            sp.wait_ge(S["stage8"], 1)
            load_gine_in(0)
            load_g1(0)
            load_g2(0)
            with sp.Fori(0, L - 1) as l:
                sp.wait_ge(S["parts"], l + 1)
                sp.wait_ge(S["xa_ready"], l * B + B)
                load_gine_in(l + 1)
                sp.wait_ge(S["hp_ready"], l * C + C)
                load_g1(l + 1)
                sp.wait_ge(S["x_new"], l * B + B)
                load_g2(l + 1)

            sp.wait_ge(S["out_ready"], B)
            sp.dma_start(out.rearrange("(b p) d -> p b d", p=NB), xnv[e]).then_inc(S["out_done"], 16)
            sp.wait_ge(S["out_done"], 16)

        @block.gpsimd
        def _(pool):
            step = Chain(pool, S["pool_step"])
            step(pool.memset(ident[:, :], 0.0))
            step(pool.affine_select(out=ident[:, :], in_=ident[:, :], compare_op=ALU.not_equal, fill=1.0, base=0,
                                    pattern=[[-1, P]], channel_multiplier=1))
            step(pool.tensor_copy(identb[:, :], ident[:, :]))
            step(pool.memset(ones[:, :], 1.0))
            step(pool.affine_select(out=earlier[:, :], in_=ones[:, :], compare_op=ALU.is_gt, fill=0.0, base=0,
                               pattern=[[1, P]], channel_multiplier=-1))
            step(pool.memset(zerob[:, :], 0.0))
            many = dict(allow_small_or_imprecise_dtypes=True)
            for t, n in ((iota_n[:, :], NB), (iota_nb, NB), (iota_k[:, :], K), (iota_t[:, :], NT)):
                step(pool.iota(t, [[1, n]], base=0, channel_multiplier=0, **many))
            for q in range(2):
                rows = slice(q * NF, (q + 1) * NF)
                step(pool.iota(freq[rows, :], [[0, 1]], base=1, channel_multiplier=1, **many))
                step(pool.memset(turn[rows, 0:1], 0.25 * q))
                step(pool.memset(turn[rows, 1:2], 0.5 * pi * q))
            step(pool.memset(eps_c[:, :], EPS))
            pool.memset(condT[:, :], 1.0).then_inc(S["consts"], 1)
            pool.wait_ge(S["consts"], 1)
            pv = pads.rearrange("p (t v) -> p t v", v=4)
            pool.memset(pv[:, :, 0:2], -1.0).then_inc(S["pads_made"], 1)
            pool.memset(pv[:, :, 2:4], 0.0).then_inc(S["pads_made"], 1)

            pool.wait_ge(S["pads_out"], 16)
            pool.wait_ge(S["slot_addr"], 1)
            with pool.Fori(0, EC // (2 * G)) as i:
                for j in range(2):
                    pool.tensor_copy(addr_now[j][e], addr[e, ds((2 * i + j) * G, G)]).then_inc(S["addr_set"], 1)
                    pool.tensor_copy(pay_now[j][e], payload[e, ds((2 * i + j) * G * 4, G * 4)]
                                     ).then_inc(S["addr_set"], 1)
                    pool.wait_ge(S["addr_set"], 4 * i + 2 * j + 2)
                    pool.sem_inc(S["pool_go"], 1)
                    for q in range(G):
                        pool.indirect_dma_start(
                            out=meta_d, out_offset=bass.IndirectOffsetOnAxis(ap=addr_now[j][e, q:q + 1], axis=0),
                            in_=pay_now[j][e, q * 4:q * 4 + 4], in_offset=None
                        ).then_inc(S[f"scattered{j}"], 16)
                pool.wait_ge(S["scattered0"], 16 * G * i + 16 * G)
                pool.wait_ge(S["scattered1"], 16 * G * i + 16 * G)

            pool.wait_ge(S["proj_out0"], 16 * R)
            pool.wait_ge(S["proj_out1"], 16 * R)
            pool.wait_ge(S["tables"], 3)
            with pool.Fori(0, NT // U) as i:
                for j in range(U):
                    pool.wait_ge(S["msg_free"], i * U + j + 1)
                    pool.tensor_copy(rows_now[j], rows_of[:, ds((i * U + j) * 2, 2)]).then_inc(S["rows_set"], 1)
                    pool.wait_ge(S["rows_set"], i * U + j + 1)
                    pool.sem_inc(S["pool_go"], 1)
                    for q in range(2):
                        pool.indirect_dma_start(
                            out=got[j][q], out_offset=None, in_=proj_d,
                            in_offset=bass.IndirectOffsetOnAxis(ap=rows_now[j][:, q:q + 1], axis=0)
                        ).then_inc(S[f"got{j}"], 16)


            with pool.Fori(0, L) as l:
                for h in range(2):
                    pool.wait_ge(S["xn_ready"], l * (2 * B) + h * B + B)
                    pool.wait_ge(S[f"w_in{(3, 5)[h]}"], 32 * l + 32)
                    pool.tensor_tensor(xv[e], xv[e], wb[1 + h][e].unsqueeze(1).broadcast_to([NB, B, D]), ALU.add
                                       ).then_inc(S["x_biased"], 1)

        @block.vector
        def _(dve):
            step = Chain(dve, S["dve_step"])
            v = nc.vector
            v.sem_inc(S["proj_free"], B)
            v.sem_inc(S["cnt_free"], U)
            v.sem_inc(S["msg_free"], U)
            v.sem_inc(S["ohw_free"], U)
            v.sem_inc(S["tile_free"], U)
            dve.wait_ge(S["edges_in"], 64)
            dve.wait_ge(S["consts"], 1)

            pay = payload.rearrange("p (e v) -> p e v", v=4)
            step(v.tensor_copy(s_f[e], src_i[e]))
            step(v.tensor_copy(d_f[e], dst_i[e]))
            for f, blk in ((s_f, s_b), (d_f, d_b)):
                step(v.tensor_scalar(blk[e], f[e], float(NB), None, ALU.is_ge))
                for b in range(2, B):
                    step(v.scalar_tensor_tensor(blk[e], f[e], float(b * NB), blk[e], ALU.is_ge, ALU.add))
            step(v.scalar_tensor_tensor(pay[e, :, 0], s_b[e], -float(NB), s_f[e], ALU.mult, ALU.add))
            step(v.scalar_tensor_tensor(pay[e, :, 1], d_b[e], -float(NB), d_f[e], ALU.mult, ALU.add))
            step(v.tensor_copy(pay[e, :, 2], w_in[e]))
            step(v.tensor_copy(pay[e, :, 3], rel_i[e]))
            step(v.scalar_tensor_tensor(key[e], d_b[e], float(B), s_b[e], ALU.mult, ALU.add))

            mem = member.rearrange("p (k e) -> p k e", k=K)
            rnk = rank.rearrange("p (k e) -> p k e", k=K)
            wide = [NB, K, EC]
            step(v.tensor_tensor(mem[e], key[e].unsqueeze(1).broadcast_to(wide),
                                 iota_k[e].unsqueeze(2).broadcast_to(wide), ALU.is_equal))
            step(v.tensor_tensor_scan(rank[e], member[e], zerob[e, 0:1].broadcast_to([NB, K * EC]), 0.0,
                                      ALU.add, ALU.add))
            tot, before = small[:, 0:K], small[:, K:2 * K]
            incl, tiles, start, off, cntf = (t0[:, q * K:(q + 1) * K] for q in range(5))
            v.tensor_reduce(tot[e], mem[e], AX.X, ALU.add).then_inc(S["totals"], 1)
            dve.wait_ge(S["totals"], 1)
            step(v.tensor_tensor_scan(before[e], tot[e], zerob[e, 0:K], 0.0, ALU.add, ALU.add))
            step(v.tensor_tensor(before[e], before[e], tot[e], ALU.subtract))
            dve.wait_ge(S["offsets_mm"], 1)
            pre, cnt = bank(7)[e, 0:K], bank(7)[:, 32:32 + K]
            step(v.tensor_scalar(cntf, cnt, float(P - 1), None, ALU.add))
            step(v.tensor_copy(tiles_i, cntf))
            step(v.tensor_scalar(tiles_i, tiles_i, 7, None, ALU.arith_shift_right))
            step(v.tensor_copy(tiles, tiles_i))
            step(v.tensor_tensor_scan(incl, tiles, zerob[:, 0:K], 0.0, ALU.add, ALU.add))
            step(v.tensor_tensor(start, incl, tiles, ALU.subtract))
            step(v.scalar_tensor_tensor(off[e], start[e], float(P), pre, ALU.mult, ALU.add))
            step(v.scalar_tensor_tensor(off[e], off[e], -1.0, before[e], ALU.add, ALU.subtract))
            step(v.tensor_tensor(rnk[e], rnk[e], off[e].unsqueeze(2).broadcast_to(wide), ALU.add))
            step(v.tensor_tensor(rank[e], rank[e], member[e], ALU.mult))
            step(v.tensor_reduce(pos[e], rank[e].rearrange("p (k e) -> p e k", k=K), AX.X, ALU.add))
            step(v.tensor_copy(pos_i[e], pos[e]))
            step(v.tensor_scalar(slot_t[e], pos_i[e], 7, None, ALU.arith_shift_right))
            step(v.tensor_scalar(slot_p[e], pos_i[e], P - 1, None, ALU.bitwise_and))
            v.scalar_tensor_tensor(addr[e], slot_p[e], float(NT), slot_t[e], ALU.mult, ALU.add
                                   ).then_inc(S["slot_addr"], 1)

            step(v.tensor_scalar(tk, iota_t[:, :], start[:, 1:2], None, ALU.is_ge))
            for k in range(2, K):
                step(v.scalar_tensor_tensor(tk, iota_t[:, :], start[:, k:k + 1], tk, ALU.is_ge, ALU.add))
            step(v.tensor_scalar(tdb, tk, float(B), None, ALU.is_ge))
            for b in range(2, B):
                step(v.scalar_tensor_tensor(tdb, tk, float(b * B), tdb, ALU.is_ge, ALU.add))
            step(v.scalar_tensor_tensor(tsb, tdb, -float(B), tk, ALU.mult, ALU.add))
            step(v.scalar_tensor_tensor(t0, tdb, 8.0, tsb, ALU.mult, ALU.add))
            for table, numbers, bits in ((tab_k, tk, 5), (tab_sd, t0, 6)):
                nj = numbers.rearrange("p (i j) -> p i j", j=U)
                word = rank[:, 0:NT // U]
                step(v.tensor_copy(word, nj[:, :, U - 1]))
                for j in range(U - 2, -1, -1):
                    step(v.scalar_tensor_tensor(word, word, float(2 ** bits), nj[:, :, j], ALU.mult, ALU.add))
                v.tensor_copy(table[:, :], word).then_inc(S["tables"], 1)
                dve.wait_ge(S["tables"], 1 if table is tab_k else 2)

            dve.wait_ge(S["fnet_in"], 80)
            f = slice(0, 2 * NF)
            step(v.tensor_scalar(freq[f, :], freq[f, :], 2.0 * pi / 16, None, ALU.mult))
            step(v.tensor_scalar(ph[f], ph[f], freq[f, 0:1], None, ALU.mult))
            step(v.tensor_scalar(emb[f], ph[f], 1.0 / (2 * pi), turn[f, 0:1], ALU.mult, ALU.add))
            step(v.tensor_copy(emb_i[f], emb[f]))
            step(v.tensor_copy(emb[f], emb_i[f]))
            c1 = 6.28125
            c2 = float(int((2 * pi - c1) * 2 ** 20)) / 2 ** 20
            for part in (c1, c2, 2 * pi - c1 - c2):
                step(v.scalar_tensor_tensor(ph[f], emb[f], -part, ph[f], ALU.mult, ALU.add))
            step(v.tensor_scalar(ph[f], ph[f], turn[f, 1:2], None, ALU.add))
            v.tensor_scalar(ph[f], ph[f], 3.1415925, -3.1415925, ALU.min, ALU.max).then_inc(S["ph_ready"], 1)

            def evac_block(n, b, dst, bias):
                dve.wait_ge(S["proj_psum"], n + 1)
                v.tensor_tensor(dst[e, b * D:(b + 1) * D], bank(b)[e], bias[e], ALU.add
                                ).then_inc(S["proj_free"], 1)

            dve.wait_ge(S["wr_in0"], 32)
            for b in range(B):
                evac_block(b, b, hself, br[0])

            def evac_two(i, first):
                for j in (1, 0):
                    dve.wait_ge(S[f"wr_in{j}"], 32 * i + 64 - 32 * j)
                    if not first:
                        dve.wait_ge(S[f"proj_out{j}"], 16 * i)
                    for b in range(B):
                        evac_block((2 * i + 2 - j) * B + b, b, hst[j], br[j])

            evac_two(0, True)
            with dve.Fori(1, R) as i:
                evac_two(i, False)

            dve.wait_ge(S["z1_exp"], 1)
            cd = slice(0, CD)
            step(v.tensor_scalar(z2[cd], z2[cd], 1.0, None, ALU.add))
            step(v.reciprocal(z2[cd], z2[cd]))
            v.tensor_tensor(z1[cd], z1[cd], z2[cd], ALU.mult).then_inc(S["z1_ready"], 1)

            dve.wait_ge(S["meta_in"], 16)
            for q, base, blk, col in ((0, 0.0, tdb, 1), (1, float(R), tsb, 0)):
                step(v.tensor_scalar(t0, meta4[:, :, 3], base, float(N), ALU.add, ALU.mult))
                step(v.scalar_tensor_tensor(t0, blk, float(NB), t0, ALU.mult, ALU.add))
                step(v.scalar_tensor_tensor(rows_v[:, :, q], meta4[:, :, col], 0.0, t0, ALU.max, ALU.add))
            step(v.tensor_copy(w3v[:, :, 0], meta4[:, :, 2]))
            step(v.tensor_tensor(t0, meta4[:, :, 2], w3v[:, :, 0], ALU.subtract))
            step(v.tensor_copy(w3v[:, :, 1], t0))
            step(v.tensor_tensor(t0, t0, w3v[:, :, 1], ALU.subtract))
            v.tensor_copy(w3v[:, :, 2], t0).then_inc(S["tables"], 1)
            dve.wait_ge(S["tables"], 3)

            def one_hot(dst, iota, t, place):
                return v.tensor_scalar(dst, iota, meta[:, ds(t * 4 + place, 1)], None, ALU.is_equal)

            with dve.Fori(0, NT // U) as i:
                for j in range(U):
                    dve.wait_ge(S["cnt_free"], i * U + j + 1)
                    one_hot(oh_s[j], iota_nb, i * U + j, 0).then_inc(S["onehots"], 1)
                    one_hot(oh_d[j], iota_nb, i * U + j, 1).then_inc(S["onehots"], 1)
            with dve.Fori(0, NT // U) as i:
                for j in range(U):
                    dve.wait_ge(S["msg_free"], i * U + j + 1)
                    one_hot(ohf_s[j], iota_n[:, :], i * U + j, 0).then_inc(S["onef"], 1)
                    one_hot(ohf_d[j], iota_n[:, :], i * U + j, 1).then_inc(S["onef"], 1)

            def norm(ln, dst, done, make):
                for b in range(B + 1):
                    if b < B:
                        make(b)
                        step(v.bn_stats(st6[e, b * 6:b * 6 + 6], xv[e, b]))
                        dve.sem_inc(S["dve_go"], 1)
                        v.bn_aggr(mvv[e, b], st6[e, b * 6:b * 6 + 6]).then_inc(S["ln_var"], 1)
                    if b > 0:
                        c = b - 1
                        dve.wait_ge(S["ln_std"], ln * B + c + 1)
                        step(v.reciprocal(rstd[e, c:c + 1], std[e, c:c + 1]))
                        v.tensor_scalar(dst[e, c], xv[e, c], mvv[e, c, 0:1], rstd[e, c:c + 1],
                                        ALU.subtract, ALU.mult).then_inc(done, 1)

            NORM = 2 * B

            dve.wait_ge(S["x_in"], 32)
            dve.wait_ge(S["msg_free"], NT + U)

            def add_messages(b):
                hb = hself[e, b * D:(b + 1) * D]
                step(v.tensor_tensor(hb, hb, bank(b)[e], ALU.add))
                step(v.scalar_tensor_tensor(xv[e, b], hb, 0.0, xv[e, b], ALU.max, ALU.add))

            norm(0, xv, S["x0_ready"], add_messages)

            dve.wait_ge(S["csd_sb"], 1)
            step(v.tensor_reduce(degree[e], csd[e], AX.X, ALU.add))
            step(v.reciprocal(rdeg[e], degree[e]))
            for b in range(B):
                dve.wait_ge(S["beta_psum"], b + 1)
                v.tensor_copy(beta[e, b * D:(b + 1) * D], bank(b)[e]).then_inc(S["beta_sb"], 1)
            dve.wait_ge(S["m1_in"], 48)
            dve.wait_ge(S["x0_ready"], B)

            def add_mean(b):
                dve.wait_ge(S["agg_psum"], b + 1)
                q = 2 * (b % 2)
                step(v.scalar_tensor_tensor(xv[e, b], bank(q + 1)[e], rdeg[e, b:b + 1], xv[e, b], ALU.mult, ALU.add))
                step(v.tensor_tensor(xv[e, b], bank(q)[e], xv[e, b], ALU.add))
                v.tensor_tensor(xv[e, b], xv[e, b], bias1[e], ALU.add).then_inc(S["agg_used"], 1)
                dve.wait_ge(S["agg_used"], b + 1)

            norm(1, xv, S["x0_ready"], add_mean)
            dve.wait_ge(S["x0_ready"], 2 * B)
            step(v.tensor_copy(xres[e, :], x[e, :]))
            v.tensor_scalar(mask[e], cnt_sd[e, :], 0.0, FAR, ALU.is_equal, ALU.mult).then_inc(S["stage7"], 1)
            dve.wait_ge(S["stage7"], 1)

            norm(2, xnv, S["xn_ready"], lambda b: None)
            STEPS7 = 2 * NORM + 2 * B + 4 * H * B
            with dve.Fori(0, L) as l:
                step.enter(l, STEPS7)

                def modulate(h):
                    for b in range(B):
                        n = l * (2 * B) + h * B + b + 1
                        y = yTv[:, :, b * NB:(b + 1) * NB]
                        dve.wait_ge(S["mod_psum"], n)
                        dve.wait_ge(S["mod_sc"], n)
                        step(v.tensor_tensor(y, chunks(bank(2 + b % 2)), y, ALU.mult))
                        v.tensor_tensor(y, chunks(bank(6 + b % 2)), y, ALU.add).then_inc(S["mod_done"], 1)

                modulate(0)
                dve.wait_ge(S["w_in2"], 32 * l + 32)
                for b in range(B):
                    dve.wait_ge(S["v_psum"], l * B + b + 1)
                    v.tensor_tensor(vN[e, b * D:(b + 1) * D], bank(b)[e], wb[0][e], ALU.add
                                    ).then_inc(S["v_done"], 1)
                dve.wait_ge(S["w_in0"], 32 * l + 32)
                for h in range(H):
                    dve.wait_ge(S["qk_psum"], l * (2 * H) + 2 * h + 1)
                    v.tensor_scalar(blocks(qT[:, h * N:(h + 1) * N]), pair((2 * h + 3) % 4)[:, :, e],
                                    wcol[0][:, h:h + 1], float(P) ** -0.5, ALU.add, ALU.mult
                                    ).then_inc(S["q_done"], 1)
                for u in range(H * B + 1):
                    if u < H * B:
                        z, s = u % 2, u % B
                        dve.wait_ge(S["s_psum"], l * (H * B) + u + 1)
                        dve.sem_inc(S["dve_go"], 1)
                        v.tensor_tensor_reduce(blocks(sm[z][e]), pair(z)[e, :, e],
                                               blocks(mask[e, s * N:(s + 1) * N]), 1.0, -3.0e38, ALU.add, ALU.max,
                                               small[e, z:z + 1]).then_inc(S["s_read"], 1)
                        dve.wait_ge(S["s_read"], l * (H * B) + u + 1)
                        v.tensor_scalar(small[e, 2 + z:3 + z], small[e, z:z + 1], -1.0, None, ALU.mult
                                        ).then_inc(S["sm_ready"], 1)
                    if u > 0:
                        z, s = (u - 1) % 2, (u - 1) % B
                        dve.wait_ge(S["e_ready"], l * (H * B) + u)
                        if u > 2:
                            dve.wait_ge(S["pt_psum"], l * (H * (B + 1)) + (u - 3) + (u - 3) // B + 1)
                        step(v.tensor_tensor_reduce(pr[z][e], ex[z][e], csd[e, s], 1.0, 0.0, ALU.mult, ALU.add,
                                                    small[e, 4 + z:5 + z]))
                        step(v.tensor_scalar(small[e, 6 + z:7 + z], small[e, 4 + z:5 + z], 1.0e-30, None, ALU.max))
                        step(v.reciprocal(small[e, 8 + z:9 + z], small[e, 6 + z:7 + z]))
                        step(v.tensor_scalar(dg[z][e], ident[e, e], small[e, 8 + z:9 + z], None, ALU.mult))
                        v.sem_inc(S["p_ready"], 1)

                def add_output(h, psum):
                    def make(b):
                        if b == 0:
                            dve.wait_ge(S["x_biased"], 2 * l + 1 + h)
                        dve.wait_ge(S[psum], l * B + b + 1)
                        v.tensor_tensor(xv[e, b], bank(b % 2)[e], xv[e, b], ALU.add).then_inc(S["x_upd"], 1)
                        dve.wait_ge(S["x_upd"], l * (2 * B) + h * B + b + 1)
                    return make

                norm(2 * l + 3, xnv, S["xn_ready"], add_output(0, "wo_psum"))
                modulate(1)
                norm(2 * l + 4, xnv, S["xn_ready"], add_output(1, "m2_psum"))
            step.leave(L)
            add_input = lambda b: step(v.tensor_tensor(xv[e, b], xv[e, b], xresv[e, b], ALU.add))
            norm(2 * L + 3, xv, S["x0_ready"], add_input)
            dve.wait_ge(S["x0_ready"], 3 * B)
            v.tensor_copy(xres[e, :], x[e, :]).then_inc(S["stage8"], 1)
            dve.wait_ge(S["stage8"], 1)

            with dve.Fori(0, NT // U) as i:
                for j in range(U):
                    dve.wait_ge(S["ohw_free"], i * U + j + 1)
                    one_hot(ohw[j][:, 0:NB], iota_nb, i * U + j, 0).then_inc(S["ohw_ready"], 1)
                    v.tensor_copy(ohw[j][:, NB:P], w3[:, ds((i * U + j) * 3, 3)]).then_inc(S["ohw_ready"], 1)

            STEPS8 = 1 + 2 * C + 4 + B
            with dve.Fori(0, L) as l:
                step.enter(l, STEPS8)
                dve.wait_ge(S["we_in"], 112 * l + 112)
                v.tensor_tensor(xst[e].rearrange("p (b d) -> p b d", b=B), xv[e],
                                gb_e[e].unsqueeze(1).broadcast_to([NB, B, D]), ALU.add).then_inc(S["xst_ready"], 1)
                dve.wait_ge(S["xst_ready"], l + 1)
                dve.wait_ge(S["part0"], l + 1)
                v.tensor_tensor(xst, xst, xp[0], ALU.subtract).then_inc(S["rest1"], 1)
                dve.wait_ge(S["part1"], l + 1)
                v.tensor_tensor(xp[2], xst, xp[1], ALU.subtract).then_inc(S["parts"], 1)
                with dve.Fori(0, NT // U) as i:
                    for j in range(U):
                        dve.wait_ge(S["tile_free"], l * NT + i * U + j + 1)
                        one_hot(odf[j], iota_n[:, :], i * U + j, 1).then_inc(S["odf_ready"], 1)
                dve.wait_ge(S["tile_free"], l * NT + NT + U)
                step(v.tensor_scalar(gep1[e], geps[e], 1.0, None, ALU.add))
                for b in range(B):
                    v.scalar_tensor_tensor(xnv[e, b], xv[e, b], gep1[e], bank(b)[e], ALU.mult, ALU.add
                                           ).then_inc(S["xa_ready"], 1)
                for c in range(C):
                    dve.wait_ge(S["xat_psum"], l * C + c + 1)
                    v.tensor_copy(blocks(yTv[:, c]), pair(c)[:, :, e]).then_inc(S["xat_sb"], 1)
                for c in range(C):
                    dve.wait_ge(S["h1_sb"], l * C + c + 1)
                    step(v.bn_stats(st6[:, c * 12:c * 12 + 6], hp[:, c * N:c * N + 500]))
                    step(v.bn_stats(st6[:, c * 12 + 6:c * 12 + 12], hp[:, c * N + 500:(c + 1) * N]))
                dve.sem_inc(S["dve_go"], 1)
                for c in range(C):
                    v.bn_aggr(mvv[:, c], st6[:, c * 12:c * 12 + 12]).then_inc(S["bn_var"], 1)
                dve.wait_ge(S["bn_std"], l + 1)
                step(v.reciprocal(bnc[:, 0:C], std[:, 0:C]))
                step(v.tensor_tensor(bnc[:, C:2 * C], bnc[:, 0:C], gcv[:, 1], ALU.mult))
                step(v.tensor_tensor(bnc[:, 2 * C:3 * C], mvv[:, 0:C, 0], bnc[:, C:2 * C], ALU.mult))
                step(v.tensor_tensor(bnc[:, 3 * C:4 * C], gcv[:, 2], bnc[:, 2 * C:3 * C], ALU.subtract))
                v.sem_inc(S["bn_ready"], 1)
                dve.wait_ge(S["g2_in"], 32 * l + 32)
                for b in range(B):
                    dve.wait_ge(S["h2_psum"], l * B + b + 1)
                    step(v.tensor_tensor(xnv[e, b], bank(b)[e], gb_2[e], ALU.add))
                    v.tensor_scalar(xv[e, b], xnv[e, b], 0.0, None, ALU.max).then_inc(S["x_new"], 1)
                dve.wait_ge(S["x_new"], l * B + B)
            step.leave(L)
            norm(2 * L + 4, xnv, S["out_ready"], add_input)

        @block.scalar
        def _(act):
            s = nc.scalar

            def norm_std(ln):
                for b in range(B):
                    act.wait_ge(S["ln_var"], ln * B + b + 1)
                    s.activation(std[e, b:b + 1], mvv[e, b, 1:2], ACT.Sqrt, bias=eps_c[e, :]).then_inc(S["ln_std"], 1)

            act.wait_ge(S["ph_ready"], 1)
            s.activation(emb[0:2 * NF], ph[0:2 * NF], ACT.Sin).then_inc(S["emb_ready"], 1)
            cd = slice(0, CD)
            act.wait_ge(S["z1_psum"], 1)
            s.activation(blocks(z1[cd]), pair(3)[cd, :, e], ACT.Identity, bias=fb1[cd]).then_inc(S["act_step"], 1)
            act.wait_ge(S["act_step"], 1)
            s.activation(z2[cd], z1[cd], ACT.Exp, scale=-1.0).then_inc(S["z1_exp"], 1)
            act.wait_ge(S["z2_psum"], 1)
            s.activation(blocks(condT[cd, :]), pair(3)[cd, :, e], ACT.Identity, bias=fb2[cd]
                         ).then_inc(S["cond_ready"], 1)

            act.wait_ge(S["cnt_free"], NT + U)
            s.activation(cds[e], banks[e, 0:K * P].rearrange("p (k n) -> p k n", n=P)[:, :, e], ACT.Copy
                         ).then_inc(S["cnt_sb"], 1)
            act.wait_ge(S["csd_psum"], 1)
            s.activation(cnt_sd[e, :].rearrange("p (k n) -> p k n", n=NB),
                         banks[e, 0:K * P].rearrange("p (k n) -> p k n", n=P)[:, :, e], ACT.Copy
                         ).then_inc(S["csd_sb"], 1)

            norm_std(0)
            for c in range(C):
                act.wait_ge(S["t_psum"], c + 1)
                s.activation(blocks(yTv[:, c]), pair(c)[:, :, e], ACT.Copy).then_inc(S["t_sb"], 1)
            norm_std(1)

            norm_std(2)
            with act.Fori(0, L) as l:
                def modulate(h):
                    for b in range(B):
                        act.wait_ge(S["mod_psum"], l * (2 * B) + h * B + b + 1)
                        s.activation(yTv[:, :, b * NB:(b + 1) * NB], chunks(bank(4 + b % 2)), ACT.Identity,
                                     bias=ones[:, 0:1]).then_inc(S["mod_sc"], 1)

                modulate(0)
                act.wait_ge(S["w_in1"], 32 * l + 32)
                for h in range(H):
                    act.wait_ge(S["qk_psum"], l * (2 * H) + 2 * h + 2)
                    s.activation(blocks(kT[:, h * N:(h + 1) * N]), pair((2 * h + 4) % 4)[:, :, e], ACT.Identity,
                                 bias=wcol[1][:, h:h + 1]).then_inc(S["k_done"], 1)
                for u in range(H * B + 3):
                    if u < H * B:
                        act.wait_ge(S["sm_ready"], l * (H * B) + u + 1)
                        if u > 1:
                            act.wait_ge(S["p_ready"], l * (H * B) + u - 1)
                        s.activation(ex[u % 2][e], sm[u % 2][e], ACT.Exp, bias=small[e, 2 + u % 2:3 + u % 2]
                                     ).then_inc(S["e_ready"], 1)
                    if u >= 3 and (u - 3) % B == B - 1:
                        h = (u - 3) // B
                        n = h * (B + 1) + B
                        act.wait_ge(S["pt_psum"], l * (H * (B + 1)) + n + 1)
                        s.activation(blocks(oT[:, h * N:(h + 1) * N]), pair(2 + n % 2)[:, :, e], ACT.Copy
                                     ).then_inc(S["pt_done"], 1)
                    if 2 <= u <= H * B + 1:
                        n, sblk = (u - 2) + (u - 2) // B, (u - 2) % B
                        act.wait_ge(S["pt_psum"], l * (H * (B + 1)) + n + 1)
                        s.activation(pT[e].rearrange("p (d n) -> p d n", d=B)[:, :, sblk * NB:(sblk + 1) * NB],
                                     pair(2 + n % 2)[e, :, e], ACT.Copy).then_inc(S["pt_done"], 1)
                norm_std(2 * l + 3)
                modulate(1)
                act.wait_ge(S["w_in4"], 32 * l + 32)
                for c in range(C):
                    act.wait_ge(S["m1_psum"], l * C + c + 1)
                    s.activation(blocks(qT[:, c * N:(c + 1) * N]), pair(c)[:, :, e], ACT.Relu,
                                 bias=wcol[2][:, c:c + 1]).then_inc(S["h_done"], 1)
                norm_std(2 * l + 4)
            norm_std(2 * L + 3)

            act.wait_ge(S["stage8"], 1)
            psum_bf = [bank(5 + j).bitcast(BF16) for j in range(U)]
            with act.Fori(0, NT // U) as i:
                for j in range(U):
                    act.wait_ge(S["st_psum"], i * U + j + 1)
                    s.activation(stat[:, ds((i * U + j) * P, P)], psum_bf[j][:, 0:P], ACT.Copy
                                 ).then_inc(S["ohw_free"], 1)
            with act.Fori(0, L) as l:
                act.wait_ge(S["xst_ready"], l + 1)
                act.wait_ge(S["we_in"], 112 * l + 112)
                s.activation(xp[0], xst, ACT.Copy).then_inc(S["part0"], 1)
                act.wait_ge(S["rest1"], l + 1)
                s.activation(xp[1], xst, ACT.Copy).then_inc(S["part1"], 1)
                with act.Fori(0, NT // U) as i:
                    for j in range(U):
                        act.wait_ge(S["u_psum"], l * NT + i * U + j + 1)
                        act.wait_ge(S["tile_free"], l * NT + i * U + j + 1)
                        s.activation(msg[j], bank(5 + j), ACT.Relu).then_inc(S["msg_ready"], 1)
                act.wait_ge(S["g_in"], 32 * l + 32)
                for c in range(C):
                    act.wait_ge(S["h1_psum"], l * C + c + 1)
                    s.activation(blocks(hp[:, c * N:(c + 1) * N]), pair(c)[:, :, e], ACT.Identity,
                                 bias=gcv[:, 0, c:c + 1]).then_inc(S["h1_sb"], 1)
                act.wait_ge(S["bn_var"], l * C + C)
                s.activation(std[:, 0:C], mvv[:, 0:C, 1], ACT.Sqrt, bias=eps_c[:, :]).then_inc(S["bn_std"], 1)
                act.wait_ge(S["bn_ready"], l + 1)
                for c in range(C):
                    s.activation(hp[:, c * N:(c + 1) * N], hp[:, c * N:(c + 1) * N], ACT.Relu,
                                 bias=bnc[:, 3 * C + c:3 * C + c + 1], scale=bnc[:, C + c:C + c + 1]
                                 ).then_inc(S["hp_ready"], 1)
            norm_std(2 * L + 4)

        @block.tensor
        def _(pe):
            mm = nc.tensor.matmul

            def wide_mm(out_pair, lhsT, rhs, **flags):
                r = blocks(rhs)
                mm(out_pair[:, 0:4, e], lhsT, r[:, 0:4], **flags)
                return mm(out_pair[:, 4, e], lhsT, r[:, 4], **flags)

            def project(b, bnk, left, weight):
                for c in range(C):
                    ins = mm(bank(bnk)[e], left[:, c, b * NB:(b + 1) * NB], weight[:, c * D:(c + 1) * D],
                             start=(c == 0), stop=(c == C - 1))
                return ins

            def turn_chunk(c, where, src):
                for b in range(B):
                    ins = nc.tensor.transpose(pair(where)[:, b, e], src[e, b, c * P:(c + 1) * P], ident[e, e])
                return ins

            def clear(n):
                for q in range(n):
                    mm(bank(q)[e], zerob[:, e], zerob[:, :], start=True, stop=False, skip_group_check=True)

            def packed(table, i, bits):
                return nc.values_load(table[0:1, ds(i, 1)], engines=[mybir.EngineType.PE], min_val=0,
                                      max_val=2 ** (bits * U) - 1, skip_runtime_bounds_check_because=
                                      "the tables are sums of comparisons made on the chip, whatever the edges are")

            def buckets_of(i):
                word = packed(tab_k, i, 5)
                return [(((word >> (5 * j)) & 31) * P).with_bounds(min_val=0, max_val=(K - 1) * P) for j in range(U)]

            def blocks_of(i):
                word = packed(tab_sd, i, 6)
                cols = [(((word >> (3 * j)) & 7) * D).with_bounds(min_val=0, max_val=(B - 1) * D) for j in range(2 * U)]
                return cols[0::2], cols[1::2]

            pe.wait_ge(S["x_in"], 16)
            pe.wait_ge(S["wr_in0"], 32)
            for b in range(B):
                project(b, b, xTv, wr[0]).then_inc(S["proj_psum"], 1)
            pe.wait_ge(S["consts"], 1)
            pe.wait_ge(S["totals"], 1)
            tot = small[e, 0:K]
            mm(bank(7)[e, 0:K], earlier[e, e], tot, start=True, stop=True)
            mm(bank(7)[:, 32:32 + K], ones[e, :], tot, start=True, stop=True).then_inc(S["offsets_mm"], 1)
            with pe.Fori(0, R) as i:
                for j in (1, 0):
                    pe.wait_ge(S[f"wr_in{j}"], 32 * i + 64 - 32 * j)
                    for b in range(B):
                        pe.wait_ge(S["proj_free"], (2 * i + 2 - j) * B + b + 1)
                        project(b, b, xTv, wr[j]).then_inc(S["proj_psum"], 1)

            pe.wait_ge(S["emb_ready"], 1)
            pe.wait_ge(S["fnet_in"], 80)
            pe.wait_ge(S["slot_addr"], 1)
            wide_mm(pair(3)[0:CD], fw1[0:2 * NF], emb[0:2 * NF], start=True, stop=True).then_inc(S["z1_psum"], 1)
            pe.wait_ge(S["z1_ready"], 1)
            wide_mm(pair(3)[0:CD], fw2[0:CD], z1[0:CD], start=True, stop=True).then_inc(S["z2_psum"], 1)

            pe.wait_ge(S["proj_free"], B * (2 * R + 2))
            pe.wait_ge(S["cond_ready"], 1)
            pe.wait_ge(S["tables"], 3)
            clear(7)
            with pe.Fori(0, NT // U) as i:
                at_k = buckets_of(i)
                for j in range(U):
                    pe.wait_ge(S["onehots"], (i * U + j) * 2 + 2)
                    mm(banks[e, ds(at_k[j], NB)], oh_d[j], oh_s[j], start=False, stop=False, skip_group_check=True
                       ).then_inc(S["cnt_free"], 1)
            pe.wait_ge(S["cnt_sb"], 1)
            for s in range(B):
                for d in range(B):
                    k = s * B + d
                    ins = nc.tensor.transpose(banks[e, k * P:k * P + NB], cds[e, d * B + s], ident[e, e])
            ins.then_inc(S["csd_psum"], 1)

            pe.wait_ge(S["csd_sb"], 1)
            clear(B)
            with pe.Fori(0, NT // U) as i:
                at_s, at_d = blocks_of(i)
                for j in range(U):
                    pe.wait_ge(S["onef"], (i * U + j) * 2 + 2)
                    pe.wait_ge(S[f"got{j}"], 32 * i + 32)
                    mm(banks[e, ds(at_s[j], D)], ohf_s[j], got[j][0], start=False, stop=False, skip_group_check=True)
                    mm(banks[e, ds(at_d[j], D)], ohf_d[j], got[j][1], start=False, stop=False, skip_group_check=True
                       ).then_inc(S["msg_free"], 1)

            pe.wait_ge(S["x0_ready"], B)
            for c in range(C):
                turn_chunk(c, c, xv).then_inc(S["t_psum"], 1)
            pe.wait_ge(S["t_sb"], C)
            pe.wait_ge(S["m1_in"], 48)
            for b in range(B):
                project(b, b, yTv, wn).then_inc(S["beta_psum"], 1)
            pe.wait_ge(S["beta_sb"], B)
            for b in range(B):
                q = 2 * (b % 2)
                if b >= 2:
                    pe.wait_ge(S["agg_used"], b - 1)
                project(b, q, yTv, wc)
                for d in range(B):
                    ins = mm(bank(q + 1)[e], cds[e, d * B + b], beta[e, d * D:(d + 1) * D],
                             start=(d == 0), stop=(d == B - 1))
                ins.then_inc(S["agg_psum"], 1)

            with pe.Fori(0, L) as l:
                def modulate(h):
                    pe.wait_ge(S[f"ln_in{h}"], 64 * l + 64)
                    for b in range(B):
                        if b >= 2:
                            pe.wait_ge(S["mod_done"], l * (2 * B) + h * B + b - 1)
                        for q in range(2):
                            for c in range(C):
                                mm(chunks(bank(4 + 2 * q + b % 2))[:, c], lnw[2 * h + q][0:CD + 1, c * P:(c + 1) * P],
                                   condT[:, b * NB:(b + 1) * NB], start=True, stop=True)
                        pe.wait_ge(S["xn_ready"], l * (2 * B) + h * B + b + 1)
                        for c in range(C):
                            ins = nc.tensor.transpose(chunks(bank(2 + b % 2))[:, c], xnv[e, b, c * P:(c + 1) * P],
                                                      ident[e, e])
                        ins.then_inc(S["mod_psum"], 1)
                    pe.wait_ge(S["mod_done"], l * (2 * B) + h * B + B)

                def wide_project(where, left, o):
                    for c in range(C):
                        ins = wide_mm(pair(where), left[:, c * D + o * P:c * D + (o + 1) * P], yTv[:, c],
                                      start=(c == 0), stop=(c == C - 1))
                    return ins

                modulate(0)
                pe.wait_ge(S["w_in2"], 32 * l + 32)
                for b in range(B):
                    project(b, b, yTv, w2[2]).then_inc(S["v_psum"], 1)
                pe.wait_ge(S["w_in0"], 32 * l + 32)
                pe.wait_ge(S["w_in1"], 32 * l + 32)
                for u in range(2 * H):
                    if 1 <= u <= 3:
                        pe.wait_ge(S["v_done"], l * B + min(2 * u, B))
                    if u >= 4:
                        pe.wait_ge(S[("q_done", "k_done")[u % 2]], l * H + u // 2 - 1)
                    wide_project((u + 3) % 4, w2[u % 2], u // 2).then_inc(S["qk_psum"], 1)
                pe.wait_ge(S["q_done"], l * H + H - 1)
                for u in range(H * B + 3):
                    if u < H * B:
                        h, sblk = u // B, u % B
                        if u == 0:
                            pe.wait_ge(S["k_done"], l * H + H - 1)
                        if u == 1:
                            pe.wait_ge(S["q_done"], l * H + H)
                        if u == 2:
                            pe.wait_ge(S["k_done"], l * H + H)
                        if u >= 2:
                            pe.wait_ge(S["s_read"], l * (H * B) + u - 1)
                        wide_mm(pair(u % 2)[e], qT[:, h * N + sblk * NB:h * N + (sblk + 1) * NB],
                                kT[:, h * N:(h + 1) * N], start=True, stop=True).then_inc(S["s_psum"], 1)
                    if u >= 3 and (u - 3) % B == B - 1:
                        h = (u - 3) // B
                        n = h * (B + 1) + B
                        pe.wait_ge(S["pt_done"], l * (H * (B + 1)) + n)
                        for d in range(B):
                            ins = wide_mm(pair(2 + n % 2), vN[e, d * D + h * P:d * D + (h + 1) * P],
                                          pT[e, d * N:(d + 1) * N], start=(d == 0), stop=(d == B - 1))
                        ins.then_inc(S["pt_psum"], 1)
                    if 2 <= u <= H * B + 1:
                        n, z = (u - 2) + (u - 2) // B, (u - 2) % 2
                        pe.wait_ge(S["p_ready"], l * (H * B) + u - 1)
                        if n >= 2:
                            pe.wait_ge(S["pt_done"], l * (H * (B + 1)) + n - 1)
                        for d in range(B):
                            ins = mm(pair(2 + n % 2)[e, d, e], pr[z][e, d * NB:(d + 1) * NB], dg[z][e],
                                     start=True, stop=True)
                        ins.then_inc(S["pt_psum"], 1)
                pe.wait_ge(S["s_read"], l * (H * B) + H * B)
                pe.wait_ge(S["pt_done"], l * (H * (B + 1)) + H * (B + 1))
                pe.wait_ge(S["w_in3"], 32 * l + 32)
                oTv = oT.rearrange("p (c n) -> p c n", c=C)

                def outputs(h, left, weight, psum):
                    for b in range(B):
                        if b >= 2:
                            pe.wait_ge(S["x_upd"], l * (2 * B) + h * B + b - 1)
                        project(b, b % 2, left, weight).then_inc(S[psum], 1)

                outputs(0, oTv, w2[3], "wo_psum")
                modulate(1)
                pe.wait_ge(S["w_in4"], 32 * l + 32)
                for c in range(C):
                    wide_project(c, w2[4], c).then_inc(S["m1_psum"], 1)
                pe.wait_ge(S["h_done"], l * C + C)
                pe.wait_ge(S["w_in5"], 32 * l + 32)
                hT = qT.rearrange("p (c n) -> p c n", c=C)
                outputs(1, hT, w2[5], "m2_psum")

            psum_bf = [bank(5 + j).bitcast(BF16) for j in range(U)]
            with pe.Fori(0, NT // U) as i:
                for j in range(U):
                    pe.wait_ge(S["ohw_free"], i * U + j + 1)
                    pe.wait_ge(S["ohw_ready"], (i * U + j) * 2 + 2)
                    nc.tensor.transpose(psum_bf[j][:, 0:P], ohw[j], identb[:, :]).then_inc(S["st_psum"], 1)
            pe.wait_ge(S["ohw_free"], NT + U)
            with pe.Fori(0, L) as l:
                pe.wait_ge(S["parts"], l + 1)
                clear(B)
                with pe.Fori(0, NT // U) as i:
                    at_s, at_d = blocks_of(i)
                    for j in range(U):
                        for q in range(3):
                            ins = mm(bank(5 + j), stat[:, ds((i * U + j) * P, P)], xp[q][:, ds(at_s[j], D)],
                                     start=(q == 0), stop=(q == 2))
                        ins.then_inc(S["u_psum"], 1)
                    for j in range(U):
                        pe.wait_ge(S["odf_ready"], l * NT + i * U + j + 1)
                        pe.wait_ge(S["msg_ready"], l * NT + i * U + j + 1)
                        mm(banks[e, ds(at_d[j], D)], odf[j], msg[j], start=False, stop=False, skip_group_check=True
                           ).then_inc(S["tile_free"], 1)
                pe.wait_ge(S["xa_ready"], l * B + B)
                for c in range(C):
                    turn_chunk(c, c, xnv).then_inc(S["xat_psum"], 1)
                pe.wait_ge(S["xat_sb"], l * C + C)
                pe.wait_ge(S["g_in"], 32 * l + 32)
                for o in range(C):
                    for c in range(C):
                        ins = wide_mm(pair(o), g1[:, c * D + o * P:c * D + (o + 1) * P], yTv[:, c],
                                      start=(c == 0), stop=(c == C - 1))
                    ins.then_inc(S["h1_psum"], 1)
                pe.wait_ge(S["hp_ready"], l * C + C)
                pe.wait_ge(S["g2_in"], 32 * l + 32)
                hpv = hp.rearrange("p (c n) -> p c n", c=C)
                for b in range(B):
                    project(b, b, hpv, g2).then_inc(S["h2_psum"], 1)
                pe.wait_ge(S["x_new"], l * B + B)


def kernel(**inputs):
    import numpy as np
    import concourse.bacc as bacc
    from concourse.bass_utils import run_bass_kernel_spmd

    i = {n: np.asarray(v) for n, v in inputs.items()}

    def columns(v):
        return v.reshape(L, C, P).transpose(0, 2, 1)

    arrays = {n: v for n, v in i.items() if n.startswith(("L1_", "L2_", "L3_")) and n not in (
        "L2_gnn_bq", "L2_gnn_bk", "L2_gnn_m_b1", "L3_gnn_eps", "L3_gnn_b1", "L3_gnn_gamma", "L3_gnn_beta")}
    arrays["L1_gnn_bias"] = i["L1_gnn_bias"].reshape(1, D)
    arrays["L2_gnn_f_b1"] = i["L2_gnn_f_b1"].reshape(CD, 1)
    arrays["L2_gnn_f_b2"] = i["L2_gnn_f_b2"].reshape(CD, 1)
    arrays["x"] = i["x"]
    arrays["xT"] = i["x"].T
    for n in ("src", "dst", "edge_type_8", "edge_weight1"):
        arrays[n] = i[n].reshape(NB, EC)
    arrays["node_vec1"] = i["node_vec1"].reshape(1, N)
    arrays["W0"] = np.concatenate([i["L0_gnn_W_self"][None], i["L0_gnn_W_rel"]]).transpose(0, 2, 1)
    arrays["b0"] = np.concatenate([i["L0_gnn_b_self"][None], i["L0_gnn_b_rel"]])
    for n in ("bq", "bk", "m_b1"):
        arrays[n] = columns(i["L2_gnn_" + n])
    arrays["eps3"] = i["L3_gnn_eps"].reshape(L, 1)
    arrays["L3_gnn_We"] = i["L3_gnn_We"].reshape(L, D)
    arrays["cols3"] = np.concatenate([columns(i["L3_gnn_" + n]) for n in ("b1", "gamma", "beta")], axis=2)
    arrays = {n: np.ascontiguousarray(v) for n, v in arrays.items()}

    nc = bacc.Bacc("TRN2", target_bir_lowering=False, num_devices=1)
    aps = {n: nc.dram_tensor("in_" + n, v.shape, mybir.dt.from_np(v.dtype), kind="ExternalInput").ap()
           for n, v in arrays.items()}
    out = nc.dram_tensor("out_x", (N, D), F32, kind="ExternalOutput").ap()
    gnn_stack(nc, aps, out)
    r = run_bass_kernel_spmd(nc, [{"in_" + n: v for n, v in arrays.items()}], core_ids=[0])
    return r.results[0]["out_x"]
```

```python
from contextlib import ExitStack
from math import pi

import concourse.bass as bass
from concourse import mybir

F32 = mybir.dt.float32
BF16 = mybir.dt.bfloat16
I32 = mybir.dt.int32
U32 = mybir.dt.uint32
ALU = mybir.AluOpType
ACT = mybir.ActivationFunctionType
AX = mybir.AxisListType
ds = bass.ds

P = 128
N = 625
NB = 125
B = N // NB
D = 512
C = D // P
E = 20000
EC = E // NB
R = 8
EARLY = 6
K = B * B
U = 3
Q = 3 * U
G = 10
NT = -(-(E // P + K + 1) // U) * U
LATE = (R - EARLY) * 2 * B
H = 4
L = 4
NF = 32
CD = 16
EPS = 1e-5
FAR = 1.0e30
assert NT % (2 * U) == U and NT % Q == U and LATE == NT // Q and 2 * EARLY >= R
D_BITS = 9
T_A = 4 * C * D * 2 // P
assert D == 2 ** D_BITS
assert NT * P >= E + K * (P - 1)


class Chain:

    def __init__(self, eng, sem):
        self.eng, self.sem, self.base, self.n = eng, sem, 0, 0

    def __call__(self, ins):
        ins.then_inc(self.sem, 1)
        self.n += 1
        self.eng.wait_ge(self.sem, self.base + self.n)

    def enter(self, i, per):
        self.start, self.per = self.base + self.n, per
        self.base, self.n = i * per + self.start, 0

    def leave(self, times):
        assert self.n == self.per, self.n
        self.base, self.n = self.start + times * self.per, 0


def gnn_stack(nc, a, out):
    ctx = ExitStack()
    with ctx:
        def sb(name, shape, dt=F32):
            return ctx.enter_context(nc.sbuf_tensor(name, shape, dt))

        banks = ctx.enter_context(nc.psum_tensor("banks", [P, 8 * D], F32))

        def bank(i):
            return banks[:, i * D:(i + 1) * D]

        def pair(i):
            return banks[:, 2 * i * D:2 * i * D + B * P].rearrange("p (b n) -> p b n", n=P)

        def chunks(t):
            return t[:, 0:C * NB].rearrange("p (c n) -> p c n", c=C)

        def blocks(t):
            return t.rearrange("p (b n) -> p b n", n=NB)

        ident = sb("ident", [P, P])
        identb = sb("identb", [P, P], BF16)
        ones = sb("ones", [P, P])
        earlier = sb("earlier", [P, P])
        zerob = sb("zerob", [P, D], BF16)
        iota_n = sb("iota_n", [P, NB])
        iota_nb = sb("iota_nb", [P, NB + 3], BF16)[:, 0:NB]
        iota_p = sb("iota_p", [P, 1])
        iota_k = sb("iota_k", [P, K])
        iota_t = sb("iota_t", [P, NT])
        freq = sb("freq", [2 * NF, 1])
        turn = sb("turn", [2 * NF, 2])
        eps_c = sb("eps_c", [P, 1])

        meta = sb("meta", [P, NT * 4])
        meta4 = meta[:, :].rearrange("p (t v) -> p t v", v=4)
        tab_k = sb("tab_k", [P, NT // U], I32)
        tab_s = sb("tab_s", [P, NT // U], I32)
        tab_d = sb("tab_d", [P, NT // U], I32)
        tab_next = sb("tab_next", [P, NT // U + 1], I32)
        w3 = sb("w3", [P, NT * 3], BF16)
        w3v = w3[:, :].rearrange("p (t v) -> p t v", v=3)
        rows_of = sb("rows_of", [P, NT * 2], U32)
        rows_v = rows_of[:, :].rearrange("p (t v) -> p t v", v=2)
        hot_d16 = [sb(f"hot_d16_{j}", [P, 128], BF16)[:, 0:NB] for j in range(Q)]
        rows_now = [sb(f"rows_now{j}", [P, 1], U32)[:, :] for j in range(Q)]
        pay_now = [sb(f"pay_now{j}", [P, G * 4])[:, :] for j in range(2)]
        addr_now = [sb(f"addr_now{j}", [P, G], U32)[:, :] for j in range(2)]
        x = sb("x", [P, B * D])
        xv = x[:, :].rearrange("p (b d) -> p b d", b=B)
        xn = sb("xn", [P, B * D])
        xnv = xn[:, :].rearrange("p (b d) -> p b d", b=B)
        xres = sb("xres", [P, B * D])
        xresv = xres[:, :].rearrange("p (b d) -> p b d", b=B)
        yT = sb("yT", [P, C * N])
        yTv = yT[:, :].rearrange("p (c n) -> p c n", c=C)
        cnt_sd = sb("cnt_sd", [P, B * N])
        csd = cnt_sd[:, :].rearrange("p (s n) -> p s n", s=B)
        condT = sb("condT", [CD + 1, N])
        st6 = sb("st6", [P, B * 12])
        mv = sb("mv", [P, B * 2])
        mvv = mv[:, :].rearrange("p (b v) -> p b v", v=2)
        std = sb("std", [P, B])
        rstd = sb("rstd", [P, B])
        small = sb("small", [P, 64])

        ARENA = 34800
        arena = sb("arena", [P, ARENA])
        top = [0]

        def take(words, dt=F32):
            at = top[0]
            top[0] += words
            assert top[0] <= ARENA, top[0]
            v = arena[:, at:at + words]
            return v if dt == F32 else v.bitcast(dt)

        member = take(K * EC)
        rank = take(K * EC)
        wc, wn = take(C * D), take(C * D)
        bias1 = take(D)
        degree, rdeg = take(B), take(B)
        beta = xn[:, :]
        src_i, dst_i, rel_i = take(EC, I32), take(EC, I32), take(EC, I32)
        w_in = take(EC)
        s_f, d_f, s_b, d_b, key, pos = (take(EC) for _ in range(6))
        pos_i, slot_t, slot_p = (take(EC, I32) for _ in range(3))
        addr = take(EC, U32)
        payload = take(EC * 4)
        pads = take(NT * 4)
        xT = take(C * N)
        xTv = xT.rearrange("p (c n) -> p c n", c=C)
        wr = [take(C * D) for _ in range(2)]
        br = [take(D) for _ in range(2)]
        hst = [take(B * D) for _ in range(2)]
        hself = take(B * D)
        tk, tdb, tsb, t0 = (take(NT) for _ in range(4))
        tiles_i = take(K, I32)
        s16 = take(NT // 2 + 1, BF16)
        turned = take(2 * 4 * P // 2, BF16)
        turned_v = turned.rearrange("p (h v n) -> p h v n", h=2, v=4)
        emb = take(N)
        ph = take(N)
        emb_i = take(N, I32)
        z1, z2 = emb, ph
        fw1, fw2 = take(CD), take(CD)
        fb1, fb2 = take(1), take(1)
        top[0] = 0
        ohf_s = [take(NB) for _ in range(2 * U)]
        ohf_d = [take(NB) for _ in range(2 * U)]
        got = [take(D) for _ in range(2 * U)]
        for j in range(U):
            at = U * D + 2 * j * NB
            ohf_s.append(xres[:, at:at + NB])
            ohf_d.append(xres[:, at + NB:at + 2 * NB])
            got.append(xres[:, j * D:(j + 1) * D])
        hot_s16 = [t.bitcast(BF16)[:, 0:NB] for t in ohf_s]
        cnt_ds = take(B * N)
        cds = cnt_ds.rearrange("p (k n) -> p k n", n=NB)
        assert top[0] <= 2 * K * EC
        top[0] = 0
        w2 = [take(C * D) for _ in range(6)]
        wb = [take(D) for _ in range(3)]
        wcol = [take(C) for _ in range(3)]
        lnw = [take(D) for _ in range(4)]
        mask = take(B * N)
        qT, kT, vN = take(C * N), take(C * N), take(B * D)
        oT = qT
        sm, ex, pr = ([take(N) for _ in range(2)] for _ in range(3))
        dg = [take(NB) for _ in range(2)]
        pT = take(B * N)
        top[0] = 0
        stat = take(NT * P // 2, BF16)
        xp = [take(B * D // 2, BF16) for _ in range(3)]
        xst = take(B * D)
        g1, g2 = take(C * D), take(C * D)
        gb_e, gb_2 = take(D), take(D)
        gcol = take(3 * C)
        gcv = gcol.rearrange("p (v c) -> p v c", v=3)
        geps, gep1 = take(1), take(1)
        rest = [take(D) for _ in range(2 * U)]
        part = [[take(D // 2, BF16) for _ in range(2 * U)] for _ in range(3)]
        odb = [take(64, BF16)[:, 0:NB] for _ in range(2 * U)]
        hp = take(C * N)
        bnc = take(4 * C)
        gstd = take(C)

        meta_d = nc.dram_tensor("meta_d", [P * NT, 4], F32, kind="Internal").ap()
        proj_d = [nc.dram_tensor(f"proj_{way}_d", [R * N, D], F32, kind="Internal").ap() for way in ("head", "tail")]

        turned_d = nc.dram_tensor("turned_d", [4, NT * P], BF16, kind="Internal").ap()

        names = """consts edges_in x_in fnet_in pads_made pads_out totals offsets_mm slot_addr
            scattered0 scattered1 addr_set rows_set meta_in tables proj_psum proj_free proj_out0 proj_out1 wr_in0 wr_in1
            cnt_free cnt_psum csd_psum csd_sb got0 got1 got2 got3 got4 got5 got6 got7 got8 onef msg_free first_out self_biased rel_biased
            ln_var ln_std x0_ready t_psum t_sb m1_in beta_psum beta_sb agg_psum agg_used
            ph_ready emb_ready z1_psum z1_exp z1_ready z2_psum cond_ready stage7 x_biased
            w_in0 w_in1 w_in2 w_in3 w_in4 w_in5 ln_in0 ln_in1 xn_ready mod_psum mod_sc mod_done
            qk_psum q_done k_done v_psum v_done
            s_psum s_read e_ready p_ready pt_psum pt_done wo_psum x_upd m1_psum h_done m2_psum
            x_kept we_in g_in g2_in xst_ready part0 rest1 part1 parts
             turned_psum turned_sb turned_out stat_in_a stat_in_b stat_a stat_b
            u_psum hi_ready rest_ready mid_ready lo_ready odf_ready tile_free
            xa_ready xat_psum xat_sb h1_psum h1_sb bn_var bn_std bn_ready hp_ready h2_psum h2_read x_new out_ready out_done
            pool_go dve_go dve_step act_step pool_step""".split()
        S = {n: ctx.enter_context(nc.semaphore(n)) for n in names}

        def packed(engine, table, i, bits):
            return nc.values_load(table[0:1, ds(i, 1)], engines=[engine], min_val=0, max_val=2 ** bits - 1,
                                  skip_runtime_bounds_check_because=
                                  "the tables are sums of comparisons made on the chip, whatever the edges are")

        block = ctx.enter_context(nc.Block())
        e = slice(0, NB)

        @block.sync
        def _(sp):
            def load_square(dst, src):
                return sp.dma_start(dst.rearrange("p (c o) -> p c o", c=C), src.rearrange("(c p) o -> p c o", p=P))

            def one(ap, i):
                return ap[ds(i, 1)].rearrange("a b c -> (a b) c") if len(ap.shape) == 3 else ap[ds(i, 1)]

            def row_to_all(dst, src_row, n=P):
                return sp.dma_start(dst, src_row.broadcast_to([n, dst.shape[-1]]))

            for dst, name in ((src_i, "src"), (dst_i, "dst"), (rel_i, "edge_type_8"), (w_in, "edge_weight1")):
                sp.dma_start(dst[e, :], a[name]).then_inc(S["edges_in"], 16)
            sp.dma_start(xTv, a["xT"].rearrange("(c p) n -> p c n", p=P)).then_inc(S["x_in"], 16)

            def load_proj(r, j):
                load_square(wr[j], one(a["W0"], r)).then_inc(S[f"wr_in{j}"], 16)
                row_to_all(br[j], one(a["b0"], r)).then_inc(S[f"wr_in{j}"], 16)

            load_proj(0, 0)
            load_proj(1, 1)
            sp.dma_start(xv[e], a["x"].rearrange("(b p) d -> p b d", p=NB)).then_inc(S["x_in"], 16)
            row_to_all(ph[0:2 * NF], a["node_vec1"], 2 * NF).then_inc(S["fnet_in"], 16)
            sp.dma_start(fw1[0:2 * NF, :], a["L2_gnn_f_w1"]).then_inc(S["fnet_in"], 16)
            sp.dma_start(fw2[0:CD, :], a["L2_gnn_f_w2"]).then_inc(S["fnet_in"], 16)
            sp.dma_start(fb1[0:CD, :], a["L2_gnn_f_b1"]).then_inc(S["fnet_in"], 16)
            sp.dma_start(fb2[0:CD, :], a["L2_gnn_f_b2"]).then_inc(S["fnet_in"], 16)
            sp.wait_ge(S["pads_made"], 2)
            sp.dma_start(meta_d.rearrange("(p t) v -> p (t v)", p=P), pads).then_inc(S["pads_out"], 16)
            load_square(wc, a["L1_gnn_wc"]).then_inc(S["m1_in"], 16)
            load_square(wn, a["L1_gnn_wn"]).then_inc(S["m1_in"], 16)
            row_to_all(bias1, a["L1_gnn_bias"]).then_inc(S["m1_in"], 16)

            def store(way, r, j):
                rows = proj_d[way].rearrange("(r b p) d -> r p b d", p=NB, b=B)
                sp.dma_start(rows[ds(r - way * R - 1, 1)].rearrange("a p b d -> (a p) b d"),
                             hst[j].rearrange("p (b d) -> p b d", b=B)[e]).then_inc(S[f"proj_out{j}"], 16)

            sp.wait_ge(S["self_biased"], 1)
            load_proj(2, 0)
            for r in (1, 2):
                sp.wait_ge(S["rel_biased"], r)
                store(0, r, r % 2)
                load_proj(r + 2, r % 2)
            for way in range(2):
                with sp.Fori((1, R // 2)[way], (R // 2, R - 1)[way]) as i:
                    for j in (1, 0):
                        r = 2 * i + 2 - j
                        sp.wait_ge(S["proj_free"], r * B + 2 * B)
                        store(way, r, j)
                        load_proj(r + 2, j)
            for j in (1, 0):
                r = 2 * R - j
                sp.wait_ge(S["proj_free"], r * B + 2 * B)
                store(1, r, j)

            def load_w(k, l):
                load_square(w2[k], one(a["L2_gnn_" + ("wq", "wk", "wv", "wo", "m_w1", "m_w2")[k]], l)
                            ).then_inc(S[f"w_in{k}"], 16)
                if k in (0, 1, 4):
                    sp.dma_start(wcol[(0, 1, 4).index(k)], one(a[("bq", "bk", "", "", "m_b1")[k]], l)
                                 ).then_inc(S[f"w_in{k}"], 16)
                else:
                    row_to_all(wb[(2, 3, 5).index(k)], one(a["L2_gnn_" + ("", "", "bv", "bo", "", "m_b2")[k]], l)
                               ).then_inc(S[f"w_in{k}"], 16)

            def load_ln(h, l):
                for q, name in enumerate(("s", "b")):
                    sp.dma_start(lnw[2 * h + q][0:CD, :], one(a[f"L2_gnn_{name}{h + 1}_w"], l)
                                 ).then_inc(S[f"ln_in{h}"], 16)
                    sp.dma_start(lnw[2 * h + q][CD:CD + 1, :], one(a[f"L2_gnn_{name}{h + 1}_b"], l)
                                 ).then_inc(S[f"ln_in{h}"], 16)

            sp.wait_ge(S["stage7"], 1)
            load_ln(0, 0)
            for k in (2, 0, 1, 3):
                load_w(k, 0)
            load_ln(1, 0)
            for k in (4, 5):
                load_w(k, 0)
            with sp.Fori(0, L - 1) as l:
                sp.wait_ge(S["mod_done"], l * (2 * B) + B)
                load_ln(0, l + 1)
                sp.wait_ge(S["v_done"], l * B + B)
                load_w(2, l + 1)
                sp.wait_ge(S["q_done"], l * H + H)
                load_w(0, l + 1)
                sp.wait_ge(S["k_done"], l * H + H)
                load_w(1, l + 1)
                sp.wait_ge(S["x_upd"], l * (2 * B) + B)
                load_w(3, l + 1)
                sp.wait_ge(S["mod_done"], l * (2 * B) + 2 * B)
                load_ln(1, l + 1)
                sp.wait_ge(S["h_done"], l * C + C)
                load_w(4, l + 1)
                sp.wait_ge(S["x_upd"], l * (2 * B) + 2 * B)
                load_w(5, l + 1)

            def load_gine_in(l):
                row_to_all(gb_e, one(a["L3_gnn_be"], l)).then_inc(S["we_in"], 16)
                row_to_all(geps, one(a["eps3"], l)).then_inc(S["we_in"], 16)
                for b in range(B):
                    row_to_all(xst[NB:P, b * D:(b + 1) * D], one(a["L3_gnn_We"], l), P - NB
                               ).then_inc(S["we_in"], 16)

            def load_g1(l):
                load_square(g1, one(a["L3_gnn_W1"], l)).then_inc(S["g_in"], 16)
                sp.dma_start(gcol, one(a["cols3"], l)).then_inc(S["g_in"], 16)

            def load_g2(l):
                load_square(g2, one(a["L3_gnn_W2"], l)).then_inc(S["g2_in"], 16)
                row_to_all(gb_2, one(a["L3_gnn_b2"], l)).then_inc(S["g2_in"], 16)

            def load_stat(t0, t1, sem):
                cols = slice(t0 * P, t1 * P)
                row_to_all(stat[e, cols], turned_d[0:1, cols], NB).then_inc(S[sem], 16)
                sp.dma_start(stat[NB:P, cols], turned_d[1:4, cols]).then_inc(S[sem], 16)

            sp.wait_ge(S["turned_out"], 32)
            sp.wait_ge(S["v_done"], L * B)
            sp.wait_ge(S["q_done"], L * H)
            sp.wait_ge(S["k_done"], L * H)
            sp.wait_ge(S["x_upd"], (L - 1) * (2 * B) + B)
            load_stat(0, T_A, "stat_in_a")
            sp.wait_ge(S["x_upd"], L * (2 * B))
            load_stat(T_A, NT, "stat_in_b")
            load_gine_in(0)
            load_g1(0)
            load_g2(0)
            with sp.Fori(0, L - 1) as l:
                sp.wait_ge(S["parts"], l * B + B)
                sp.wait_ge(S["xa_ready"], l * B + B)
                load_gine_in(l + 1)
                sp.wait_ge(S["hp_ready"], l * C + C)
                load_g1(l + 1)
                sp.wait_ge(S["x_new"], l * B + B)
                load_g2(l + 1)

            for b in range(B):
                sp.wait_ge(S["out_ready"], b + 1)
                sp.dma_start(out[b * NB:(b + 1) * NB], xnv[e, b]).then_inc(S["out_done"], 16)
            sp.wait_ge(S["out_done"], 16 * B)

        @block.gpsimd
        def _(pool):
            step = Chain(pool, S["pool_step"])
            step(pool.memset(ident[:, :], 0.0))
            step(pool.affine_select(out=ident[:, :], in_=ident[:, :], compare_op=ALU.not_equal, fill=1.0, base=0,
                                    pattern=[[-1, P]], channel_multiplier=1))
            step(pool.tensor_copy(identb[:, :], ident[:, :]))
            step(pool.memset(ones[:, :], 1.0))
            step(pool.affine_select(out=earlier[:, :], in_=ones[:, :], compare_op=ALU.is_gt, fill=0.0, base=0,
                               pattern=[[1, P]], channel_multiplier=-1))
            step(pool.memset(zerob[:, :], 0.0))
            many = dict(allow_small_or_imprecise_dtypes=True)
            for t, n in ((iota_n[:, :], NB), (iota_nb, NB), (iota_k[:, :], K), (iota_t[:, :], NT)):
                step(pool.iota(t, [[1, n]], base=0, channel_multiplier=0, **many))
            step(pool.iota(iota_p[:, :], [[0, 1]], base=0, channel_multiplier=1, **many))
            for q in range(2):
                rows = slice(q * NF, (q + 1) * NF)
                step(pool.iota(freq[rows, :], [[0, 1]], base=1, channel_multiplier=1, **many))
                step(pool.memset(turn[rows, 0:1], 0.25 * q))
                step(pool.memset(turn[rows, 1:2], 0.5 * pi * q))
            step(pool.memset(eps_c[:, :], EPS))
            pool.memset(condT[:, :], 1.0).then_inc(S["consts"], 1)
            pool.wait_ge(S["consts"], 1)
            pv = pads.rearrange("p (t v) -> p t v", v=4)
            pool.memset(pv[:, :, 0:2], -1.0).then_inc(S["pads_made"], 1)
            pool.memset(pv[:, :, 2:4], 0.0).then_inc(S["pads_made"], 1)

            pool.wait_ge(S["wr_in0"], 32)
            pool.wait_ge(S["first_out"], B)
            hs = hself.rearrange("p (b d) -> p b d", b=B)
            pool.tensor_tensor(hs[e], hs[e], br[0][e].unsqueeze(1).broadcast_to([NB, B, D]), ALU.add
                               ).then_inc(S["self_biased"], 1)

            pool.wait_ge(S["pads_out"], 16)
            pool.wait_ge(S["slot_addr"], 1)
            def scatter_two(i, first):
                for j in range(2):
                    if not first:
                        pool.wait_ge(S[f"scattered{j}"], 16 * G * i)
                    pool.tensor_copy(addr_now[j][e], addr[e, ds((2 * i + j) * G, G)]).then_inc(S["addr_set"], 1)
                    pool.tensor_copy(pay_now[j][e], payload[e, ds((2 * i + j) * G * 4, G * 4)]
                                     ).then_inc(S["addr_set"], 1)
                    pool.wait_ge(S["addr_set"], 4 * i + 2 * j + 2)
                    pool.sem_inc(S["pool_go"], 1)
                    for q in range(G):
                        pool.indirect_dma_start(
                            out=meta_d, out_offset=bass.IndirectOffsetOnAxis(ap=addr_now[j][e, q:q + 1], axis=0),
                            in_=pay_now[j][e, q * 4:q * 4 + 4], in_offset=None
                        ).then_inc(S[f"scattered{j}"], 16)

            scatter_two(0, True)
            with pool.Fori(1, EC // (2 * G)) as i:
                scatter_two(i, False)

            def gather_rows(way, n, turn_j):
                pool.wait_ge(S["rows_set"], n + 1)
                pool.sem_inc(S["pool_go"], 1)
                pool.indirect_dma_start(
                    out=got[turn_j], out_offset=None, in_=proj_d[way],
                    in_offset=bass.IndirectOffsetOnAxis(ap=rows_now[turn_j], axis=0)
                ).then_inc(S[f"got{turn_j}"], 16)

            pool.wait_ge(S["proj_out0"], 8 * R)
            pool.wait_ge(S["proj_out1"], 8 * R)
            pool.wait_ge(S["tables"], 3)
            with pool.Fori(0, NT // Q) as i:
                for q in range(Q):
                    gather_rows(0, i * Q + q, q)
            for q in range(NT % Q):
                gather_rows(0, NT - U + q, q)
            pool.wait_ge(S["proj_out0"], 16 * R)
            pool.wait_ge(S["proj_out1"], 16 * R)
            with pool.Fori(0, NT // Q) as i:
                for q in range(Q):
                    gather_rows(1, i * Q + NT + q, (U + q) % Q)
            for q in range(NT % Q):
                gather_rows(1, 2 * NT - U + q, U + q)

            with pool.Fori(0, L) as l:
                for h in range(2):
                    pool.wait_ge(S["xn_ready"], l * (2 * B) + h * B + B)
                    pool.wait_ge(S[f"w_in{(3, 5)[h]}"], 32 * l + 32)
                    pool.tensor_tensor(xv[e], xv[e], wb[1 + h][e].unsqueeze(1).broadcast_to([NB, B, D]), ALU.add
                                       ).then_inc(S["x_biased"], 1)

            pool.wait_ge(S["stat_in_a"], 32)
            pool.tensor_scalar(stat[e, 0:T_A * P], stat[e, 0:T_A * P], iota_p[e, :], None, ALU.is_equal
                               ).then_inc(S["stat_a"], 1)

            pool.wait_ge(S["we_in"], 112)
            for b in range(B):
                pool.wait_ge(S["x0_ready"], 2 * B + b + 1)
                pool.tensor_tensor(xst[e, b * D:(b + 1) * D], xv[e, b], gb_e[e], ALU.add).then_inc(S["xst_ready"], 1)
            pool.tensor_copy(xres[e, :], x[e, :]).then_inc(S["x_kept"], 1)

            def last_part(l, i, q):
                pool.wait_ge(S["mid_ready"], l * NT + i * 2 * U + q + 1)
                pool.tensor_tensor(part[2][q], rest[q], part[1][q], ALU.subtract).then_inc(S["lo_ready"], 1)

            with pool.Fori(0, L) as l:
                with pool.Fori(0, NT // (2 * U)) as i:
                    for q in range(2 * U):
                        last_part(l, i, q)
                for q in range(NT % (2 * U)):
                    last_part(l, NT // (2 * U), q)

        @block.vector
        def _(dve):
            step = Chain(dve, S["dve_step"])
            v = nc.vector
            v.sem_inc(S["proj_free"], 4 * B)
            v.sem_inc(S["cnt_free"], U)
            v.sem_inc(S["msg_free"], Q)
            v.sem_inc(S["tile_free"], 2 * U)
            dve.wait_ge(S["edges_in"], 64)
            dve.wait_ge(S["consts"], 1)

            pay = payload.rearrange("p (e v) -> p e v", v=4)
            step(v.tensor_copy(s_f[e], src_i[e]))
            step(v.tensor_copy(d_f[e], dst_i[e]))
            for f, blk in ((s_f, s_b), (d_f, d_b)):
                step(v.tensor_scalar(blk[e], f[e], float(NB), None, ALU.is_ge))
                for b in range(2, B):
                    step(v.scalar_tensor_tensor(blk[e], f[e], float(b * NB), blk[e], ALU.is_ge, ALU.add))
            step(v.scalar_tensor_tensor(pay[e, :, 0], s_b[e], -float(NB), s_f[e], ALU.mult, ALU.add))
            step(v.scalar_tensor_tensor(pay[e, :, 1], d_b[e], -float(NB), d_f[e], ALU.mult, ALU.add))
            step(v.tensor_copy(pay[e, :, 2], w_in[e]))
            step(v.tensor_copy(pay[e, :, 3], rel_i[e]))
            step(v.scalar_tensor_tensor(key[e], d_b[e], float(B), s_b[e], ALU.mult, ALU.add))

            mem = member.rearrange("p (k e) -> p k e", k=K)
            rnk = rank.rearrange("p (k e) -> p k e", k=K)
            wide = [NB, K, EC]
            step(v.tensor_tensor(mem[e], key[e].unsqueeze(1).broadcast_to(wide),
                                 iota_k[e].unsqueeze(2).broadcast_to(wide), ALU.is_equal))
            step(v.tensor_tensor_scan(rank[e], member[e], zerob[e, 0:1].broadcast_to([NB, K * EC]), 0.0,
                                      ALU.add, ALU.add))
            tot, before = small[:, 0:K], small[:, K:2 * K]
            incl, tiles, start, off, cntf = (t0[:, q * K:(q + 1) * K] for q in range(5))
            v.tensor_reduce(tot[e], mem[e], AX.X, ALU.add).then_inc(S["totals"], 1)
            dve.wait_ge(S["totals"], 1)
            step(v.tensor_tensor_scan(before[e], tot[e], zerob[e, 0:K], 0.0, ALU.add, ALU.add))
            step(v.tensor_tensor(before[e], before[e], tot[e], ALU.subtract))
            dve.wait_ge(S["offsets_mm"], 1)
            pre, cnt = bank(7)[e, 0:K], bank(7)[:, 32:32 + K]
            step(v.tensor_scalar(cntf, cnt, float(P - 1), None, ALU.add))
            step(v.tensor_copy(tiles_i, cntf))
            step(v.tensor_scalar(tiles_i, tiles_i, 7, None, ALU.arith_shift_right))
            step(v.tensor_copy(tiles, tiles_i))
            step(v.tensor_tensor_scan(incl, tiles, zerob[:, 0:K], 0.0, ALU.add, ALU.add))
            step(v.tensor_tensor(start, incl, tiles, ALU.subtract))
            step(v.scalar_tensor_tensor(off[e], start[e], float(P), pre, ALU.mult, ALU.add))
            step(v.scalar_tensor_tensor(off[e], off[e], -1.0, before[e], ALU.add, ALU.subtract))
            step(v.tensor_tensor(rnk[e], rnk[e], off[e].unsqueeze(2).broadcast_to(wide), ALU.add))
            step(v.tensor_tensor(rank[e], rank[e], member[e], ALU.mult))
            step(v.tensor_reduce(pos[e], rank[e].rearrange("p (k e) -> p e k", k=K), AX.X, ALU.add))
            step(v.tensor_copy(pos_i[e], pos[e]))
            step(v.tensor_scalar(slot_t[e], pos_i[e], 7, None, ALU.arith_shift_right))
            step(v.tensor_scalar(slot_p[e], pos_i[e], P - 1, None, ALU.bitwise_and))
            v.scalar_tensor_tensor(addr[e], slot_p[e], float(NT), slot_t[e], ALU.mult, ALU.add
                                   ).then_inc(S["slot_addr"], 1)

            def add_bias(r):
                j = r % 2
                dve.wait_ge(S[f"wr_in{j}"], 64 - 32 * j)
                dve.wait_ge(S["first_out"], (r + 1) * B)
                h = hst[j].rearrange("p (b d) -> p b d", b=B)
                v.tensor_tensor(h[e], h[e], br[j][e].unsqueeze(1).broadcast_to([NB, B, D]), ALU.add
                                ).then_inc(S["rel_biased"], 1)

            add_bias(1)

            step(v.tensor_scalar(tk, iota_t[:, :], start[:, 1:2], None, ALU.is_ge))
            for k in range(2, K):
                step(v.scalar_tensor_tensor(tk, iota_t[:, :], start[:, k:k + 1], tk, ALU.is_ge, ALU.add))
            step(v.tensor_scalar(tdb, tk, float(B), None, ALU.is_ge))
            for b in range(2, B):
                step(v.scalar_tensor_tensor(tdb, tk, float(b * B), tdb, ALU.is_ge, ALU.add))
            step(v.scalar_tensor_tensor(tsb, tdb, -float(B), tk, ALU.mult, ALU.add))
            n = NT // U
            word, srcs, dsts, buckets = (rank[:, q * 64:q * 64 + n + 1] for q in range(4))
            for numbers, radix, dst in ((tk, 32.0, buckets), (tsb, 8.0, srcs), (tdb, 8.0, dsts)):
                nj = numbers.rearrange("p (i j) -> p i j", j=U)
                step(v.tensor_copy(dst[:, 0:n], nj[:, :, U - 1]))
                for j in range(U - 2, -1, -1):
                    step(v.scalar_tensor_tensor(dst[:, 0:n], dst[:, 0:n], radix, nj[:, :, j], ALU.mult, ALU.add))
            step(v.tensor_copy(tab_k[:, :], buckets[:, 0:n]))
            for words, table in ((srcs, tab_s), (dsts, tab_d)):
                step(v.tensor_scalar(word[:, 0:n], words[:, 0:n], float(D), None, ALU.mult))
                v.tensor_copy(table[:, :], word[:, 0:n]).then_inc(S["tables"], 1)
                dve.wait_ge(S["tables"], 1 if table is tab_s else 2)
            step(v.memset(word, 0.0))
            step(v.tensor_copy(word[:, 0:n], srcs[:, 0:n]))
            step(v.scalar_tensor_tensor(word[:, 1:n + 1], dsts[:, 0:n], float(8 ** U), word[:, 1:n + 1],
                                        ALU.mult, ALU.add))
            step(v.tensor_scalar(word, word, float(D), None, ALU.mult))
            step(v.tensor_copy(tab_next[:, :], word))

            dve.wait_ge(S["fnet_in"], 80)
            f = slice(0, 2 * NF)
            step(v.tensor_scalar(freq[f, :], freq[f, :], 2.0 * pi / 16, None, ALU.mult))
            step(v.tensor_scalar(ph[f], ph[f], freq[f, 0:1], None, ALU.mult))
            step(v.tensor_scalar(emb[f], ph[f], 1.0 / (2 * pi), turn[f, 0:1], ALU.mult, ALU.add))
            step(v.tensor_copy(emb_i[f], emb[f]))
            step(v.tensor_copy(emb[f], emb_i[f]))
            c1 = 6.28125
            c2 = float(int((2 * pi - c1) * 2 ** 20)) / 2 ** 20
            for piece in (c1, c2, 2 * pi - c1 - c2):
                step(v.scalar_tensor_tensor(ph[f], emb[f], -piece, ph[f], ALU.mult, ALU.add))
            step(v.tensor_scalar(ph[f], ph[f], turn[f, 1:2], None, ALU.add))
            v.tensor_scalar(ph[f], ph[f], 3.1415925, -3.1415925, ALU.min, ALU.max).then_inc(S["ph_ready"], 1)

            def evac_block(n, b, dst, bias, where=None):
                dve.wait_ge(S["proj_psum"], n + 1)
                v.tensor_tensor(dst[e, b * D:(b + 1) * D], bank(b if where is None else where)[e], bias[e], ALU.add
                                ).then_inc(S["proj_free"], 1)

            add_bias(2)

            def evac_two(i):
                for j in (1, 0):
                    dve.wait_ge(S[f"wr_in{j}"], 32 * i + 64 - 32 * j)
                    dve.wait_ge(S[f"proj_out{j}"], 16 * i)
                    for b in range(B):
                        evac_block((2 * i + 2 - j) * B + b, b, hst[j], br[j])

            with dve.Fori(1, 4) as i:
                evac_two(i)

            dve.wait_ge(S["z1_exp"], 1)
            cd = slice(0, CD)
            step(v.tensor_scalar(z2[cd], z2[cd], 1.0, None, ALU.add))
            step(v.reciprocal(z2[cd], z2[cd]))
            v.tensor_tensor(z1[cd], z1[cd], z2[cd], ALU.mult).then_inc(S["z1_ready"], 1)

            with dve.Fori(4, EARLY) as i:
                evac_two(i)

            dve.wait_ge(S["meta_in"], 16)
            for q, blk, col in ((0, tdb, 1), (1, tsb, 0)):
                step(v.tensor_scalar(t0, meta4[:, :, 3], float(N), None, ALU.mult))
                step(v.scalar_tensor_tensor(t0, blk, float(NB), t0, ALU.mult, ALU.add))
                step(v.scalar_tensor_tensor(rows_v[:, :, q], meta4[:, :, col], 0.0, t0, ALU.max, ALU.add))
            step(v.tensor_copy(s16[:, 0:NT], meta4[:, :, 0]))
            step(v.tensor_copy(w3v[:, :, 0], meta4[:, :, 2]))
            step(v.tensor_tensor(t0, meta4[:, :, 2], w3v[:, :, 0], ALU.subtract))
            step(v.tensor_copy(w3v[:, :, 1], t0))
            step(v.tensor_tensor(t0, t0, w3v[:, :, 1], ALU.subtract))
            v.tensor_copy(w3v[:, :, 2], t0).then_inc(S["tables"], 1)
            dve.wait_ge(S["tables"], 3)

            def counts_of(i):
                word = packed(mybir.EngineType.DVE, tab_k, i, 5 * U)
                return [(((word >> (5 * j)) & 31) * NB).with_bounds(min_val=0, max_val=(K - 1) * NB) for j in range(U)]

            def one_hot(dst, iota, t, place):
                return v.tensor_scalar(dst, iota, meta[:, ds(t * 4 + place, 1)], None, ALU.is_equal)

            def hot_src(n, t, q):
                dve.wait_ge(S["msg_free"], n + 1)
                one_hot(ohf_s[q], iota_n[:, :], t, 0).then_inc(S["onef"], 1)

            with dve.Fori(0, R - EARLY) as i:
                for j in (1, 0):
                    dve.wait_ge(S[f"wr_in{j}"], 32 * i + 32 * EARLY + 64 - 32 * j)
                    dve.wait_ge(S[f"proj_out{j}"], 16 * i + 16 * EARLY)
                    for b in range(B):
                        turn_no = (1 - j) * B + b
                        for q in range(Q):
                            t = (i * 2 * B + turn_no) * Q + q
                            hot_src(t, t, q)
                        evac_block((2 * i + 2 * EARLY + 2 - j) * B + b, b, hst[j], br[j], 5 + turn_no % 2)
            for q in range(U):
                hot_src(NT - U + q, NT - U + q, q)

            def hot_both(t, q):
                dve.wait_ge(S["msg_free"], NT + 1 + t)
                one_hot(hot_s16[q], iota_nb, t, 0).then_inc(S["onef"], 1)
                one_hot(hot_d16[q], iota_nb, t, 1).then_inc(S["onef"], 1)
                one_hot(ohf_d[q], iota_n[:, :], t, 1).then_inc(S["onef"], 1)

            def add_counts(t, col, q):
                dve.wait_ge(S["cnt_psum"], t + 1)
                dve.wait_ge(S["cnt_free"], t + U)
                c = cnt_ds[e, ds(col, NB)]
                v.tensor_tensor(c, bank(5 + q % U)[e, e], c, ALU.add).then_inc(S["cnt_free"], 1)

            step(v.memset(cnt_ds[e], 0.0))
            for q in range(U):
                hot_both(q, U + q)
            with dve.Fori(0, NT // Q) as i:
                for q in range(Q):
                    if q % U == 0:
                        at_k = counts_of(i * (Q // U) + q // U)
                    hot_both(i * Q + U + q, (2 * U + q) % Q)
                    add_counts(i * Q + q, at_k[q % U], q)
            at_k = counts_of(NT // U - 1)
            for q in range(U):
                add_counts(NT - U + q, at_k[q], q)

            def norm(ln, dst, done, make):
                for b in range(B + 1):
                    if b < B:
                        make(b)
                        step(v.bn_stats(st6[e, b * 6:b * 6 + 6], xv[e, b]))
                        dve.sem_inc(S["dve_go"], 1)
                        v.bn_aggr(mvv[e, b], st6[e, b * 6:b * 6 + 6]).then_inc(S["ln_var"], 1)
                    if b > 0:
                        c = b - 1
                        dve.wait_ge(S["ln_std"], ln * B + c + 1)
                        step(v.reciprocal(rstd[e, c:c + 1], std[e, c:c + 1]))
                        v.tensor_scalar(dst[e, c], xv[e, c], mvv[e, c, 0:1], rstd[e, c:c + 1],
                                        ALU.subtract, ALU.mult).then_inc(done, 1)

            NORM = 2 * B

            dve.wait_ge(S["x_in"], 32)
            dve.wait_ge(S["msg_free"], 2 * NT + Q)

            def add_messages(b):
                hb = hself[e, b * D:(b + 1) * D]
                step(v.tensor_tensor(hb, hb, bank(b)[e], ALU.add))
                step(v.scalar_tensor_tensor(xv[e, b], hb, 0.0, xv[e, b], ALU.max, ALU.add))

            norm(0, xv, S["x0_ready"], add_messages)

            dve.wait_ge(S["csd_sb"], B)
            step(v.tensor_reduce(degree[e], csd[e], AX.X, ALU.add))
            step(v.reciprocal(rdeg[e], degree[e]))
            for b in range(B):
                dve.wait_ge(S["beta_psum"], b + 1)
                v.tensor_copy(beta[e, b * D:(b + 1) * D], bank(b)[e]).then_inc(S["beta_sb"], 1)
            dve.wait_ge(S["m1_in"], 48)
            dve.wait_ge(S["x0_ready"], B)

            def add_mean(b):
                dve.wait_ge(S["agg_psum"], b + 1)
                q = 2 * (b % 2)
                step(v.scalar_tensor_tensor(xv[e, b], bank(q + 1)[e], rdeg[e, b:b + 1], xv[e, b], ALU.mult, ALU.add))
                step(v.tensor_tensor(xv[e, b], bank(q)[e], xv[e, b], ALU.add))
                v.tensor_tensor(xv[e, b], xv[e, b], bias1[e], ALU.add).then_inc(S["agg_used"], 1)
                dve.wait_ge(S["agg_used"], b + 1)

            norm(1, xv, S["x0_ready"], add_mean)
            dve.wait_ge(S["x0_ready"], 2 * B)
            step(v.tensor_copy(xres[e, :], x[e, :]))
            dve.wait_ge(S["turned_out"], 32)
            v.tensor_scalar(mask[e], cnt_sd[e, :], 0.0, FAR, ALU.is_equal, ALU.mult).then_inc(S["stage7"], 1)
            dve.wait_ge(S["stage7"], 1)

            norm(2, xnv, S["xn_ready"], lambda b: None)
            STEPS7 = 2 * NORM + 2 * B + 3 * H * B
            with dve.Fori(0, L) as l:
                step.enter(l, STEPS7)

                def modulate(h):
                    for b in range(B):
                        n = l * (2 * B) + h * B + b + 1
                        y = yTv[:, :, b * NB:(b + 1) * NB]
                        dve.wait_ge(S["mod_psum"], n)
                        dve.wait_ge(S["mod_sc"], n)
                        step(v.tensor_tensor(y, chunks(bank(2 + b % 2)), y, ALU.mult))
                        v.tensor_tensor(y, chunks(bank(6 + b % 2)), y, ALU.add).then_inc(S["mod_done"], 1)

                modulate(0)
                dve.wait_ge(S["w_in2"], 32 * l + 32)
                for b in range(B):
                    dve.wait_ge(S["v_psum"], l * B + b + 1)
                    v.tensor_tensor(vN[e, b * D:(b + 1) * D], bank(b)[e], wb[0][e], ALU.add
                                    ).then_inc(S["v_done"], 1)
                dve.wait_ge(S["w_in0"], 32 * l + 32)
                for h in range(H):
                    dve.wait_ge(S["qk_psum"], l * (2 * H) + 2 * h + 1)
                    v.tensor_scalar(blocks(qT[:, h * N:(h + 1) * N]), pair((2 * h + 3) % 4)[:, :, e],
                                    wcol[0][:, h:h + 1], -float(P) ** -0.5, ALU.add, ALU.mult
                                    ).then_inc(S["q_done"], 1)
                for u in range(H * B + 1):
                    if u < H * B:
                        z, s = u % 2, u % B
                        dve.wait_ge(S["s_psum"], l * (H * B) + u + 1)
                        dve.sem_inc(S["dve_go"], 1)
                        v.tensor_tensor_reduce(blocks(sm[z][e]), pair(z)[e, :, e],
                                               blocks(mask[e, s * N:(s + 1) * N]), 1.0, 3.0e38, ALU.add, ALU.min,
                                               small[e, z:z + 1]).then_inc(S["s_read"], 1)
                    if u > 0:
                        z, s = (u - 1) % 2, (u - 1) % B
                        dve.wait_ge(S["e_ready"], l * (H * B) + u)
                        if u > 2:
                            dve.wait_ge(S["pt_psum"], l * (H * (B + 1)) + (u - 3) + (u - 3) // B + 1)
                        step(v.tensor_tensor_reduce(pr[z][e], ex[z][e], csd[e, s], 1.0, 1.0e-30, ALU.mult, ALU.add,
                                                    small[e, 4 + z:5 + z]))
                        step(v.reciprocal(small[e, 8 + z:9 + z], small[e, 4 + z:5 + z]))
                        step(v.tensor_scalar(dg[z][e], ident[e, e], small[e, 8 + z:9 + z], None, ALU.mult))
                        v.sem_inc(S["p_ready"], 1)

                def add_output(h, psum):
                    def make(b):
                        if b == 0:
                            dve.wait_ge(S["x_biased"], 2 * l + 1 + h)
                        dve.wait_ge(S[psum], l * B + b + 1)
                        v.tensor_tensor(xv[e, b], bank(b % 2)[e], xv[e, b], ALU.add).then_inc(S["x_upd"], 1)
                        dve.wait_ge(S["x_upd"], l * (2 * B) + h * B + b + 1)
                    return make

                norm(2 * l + 3, xnv, S["xn_ready"], add_output(0, "wo_psum"))
                modulate(1)
                norm(2 * l + 4, xnv, S["xn_ready"], add_output(1, "m2_psum"))
            step.leave(L)
            add_input = lambda b: step(v.tensor_tensor(xv[e, b], xv[e, b], xresv[e, b], ALU.add))
            norm(2 * L + 3, xv, S["x0_ready"], add_input)
            dve.wait_ge(S["stat_in_b"], 32)
            v.tensor_scalar(stat[e, T_A * P:NT * P], stat[e, T_A * P:NT * P], iota_p[e, :], None, ALU.is_equal
                            ).then_inc(S["stat_b"], 1)

            def split_block(n, b):
                xb = xst[:, b * D:(b + 1) * D]
                dve.wait_ge(S["part0"], n + b + 1)
                v.tensor_tensor(xb, xb, xp[0][:, b * D:(b + 1) * D], ALU.subtract).then_inc(S["rest1"], 1)
                dve.wait_ge(S["part1"], n + b + 1)
                v.tensor_tensor(xp[2][:, b * D:(b + 1) * D], xb, xp[1][:, b * D:(b + 1) * D], ALU.subtract
                                ).then_inc(S["parts"], 1)

            for b in range(B):
                split_block(0, b)

            def tile(l, i, q):
                t = i * 2 * U + q
                dve.wait_ge(S["tile_free"], l * NT + t + 1)
                dve.wait_ge(S["hi_ready"], l * NT + t + 1)
                v.scalar_tensor_tensor(rest[q], bank(5 + q % U), 0.0, part[0][q], ALU.max, ALU.subtract
                                       ).then_inc(S["rest_ready"], 1)
                one_hot(odb[q], iota_nb, t, 1).then_inc(S["odf_ready"], 1)
                dve.wait_ge(S["rest_ready"], l * NT + t + 1)
                v.tensor_copy(part[1][q], rest[q]).then_inc(S["mid_ready"], 1)

            def gine(l, last):
                with dve.Fori(0, NT // (2 * U)) as i:
                    for q in range(2 * U):
                        tile(l, i, q)
                for q in range(NT % (2 * U)):
                    tile(l, NT // (2 * U), q)
                step(v.tensor_scalar(gep1[e], geps[e], 1.0, None, ALU.add))
                dve.wait_ge(S["tile_free"], l * NT + NT + 2 * U)
                for b in range(B):
                    v.scalar_tensor_tensor(xnv[e, b], xv[e, b], gep1[e], bank(b)[e], ALU.mult, ALU.add
                                           ).then_inc(S["xa_ready"], 1)
                dve.wait_ge(S["g_in"], 32 * l + 32)
                for c in range(C):
                    dve.wait_ge(S["h1_sb"], l * C + c + 1)
                    step(v.bn_stats(st6[:, c * 12:c * 12 + 6], hp[:, c * N:c * N + 500]))
                    step(v.bn_stats(st6[:, c * 12 + 6:c * 12 + 12], hp[:, c * N + 500:(c + 1) * N]))
                    dve.sem_inc(S["dve_go"], 1)
                    v.bn_aggr(mvv[:, c], st6[:, c * 12:c * 12 + 12]).then_inc(S["bn_var"], 1)
                    dve.wait_ge(S["bn_std"], l * C + c + 1)
                    step(v.reciprocal(bnc[:, c:c + 1], gstd[:, c:c + 1]))
                    step(v.tensor_tensor(bnc[:, C + c:C + c + 1], bnc[:, c:c + 1], gcv[:, 1, c:c + 1], ALU.mult))
                    step(v.tensor_tensor(bnc[:, 2 * C + c:2 * C + c + 1], mvv[:, c, 0:1], bnc[:, C + c:C + c + 1],
                                         ALU.mult))
                    v.tensor_tensor(bnc[:, 3 * C + c:3 * C + c + 1], gcv[:, 2, c:c + 1],
                                    bnc[:, 2 * C + c:2 * C + c + 1], ALU.subtract).then_inc(S["bn_ready"], 1)
                dve.wait_ge(S["x_kept"], 1)
                dve.wait_ge(S["g2_in"], 32 * l + 32)
                if not last:
                    dve.wait_ge(S["we_in"], 112 * l + 224)
                for b in range(B + 1):
                    if b < B:
                        dve.wait_ge(S["h2_psum"], l * B + b + 1)
                        v.tensor_tensor(xnv[e, b], bank(b)[e], gb_2[e], ALU.add).then_inc(S["h2_read"], 1)
                        dve.wait_ge(S["h2_read"], l * B + b + 1)
                        if not last:
                            v.scalar_tensor_tensor(xst[e, b * D:(b + 1) * D], xnv[e, b], 0.0, gb_e[e],
                                                   ALU.max, ALU.add).then_inc(S["xst_ready"], 1)
                        v.tensor_scalar(xv[e, b], xnv[e, b], 0.0, None, ALU.max).then_inc(S["x_new"], 1)
                    if b > 0 and not last:
                        split_block(l * B + B, b - 1)
                dve.wait_ge(S["x_new"], l * B + B)

            STEPS8 = 1 + 5 * C
            with dve.Fori(0, L - 1) as l:
                step.enter(l, STEPS8)
                gine(l, False)
            step.leave(L - 1)
            gine(L - 1, True)
            norm(2 * L + 4, xnv, S["out_ready"], add_input)

        @block.scalar
        def _(act):
            s = nc.scalar

            def std_block(ln, b):
                act.wait_ge(S["ln_var"], ln * B + b + 1)
                s.activation(std[e, b:b + 1], mvv[e, b, 1:2], ACT.Sqrt, bias=eps_c[e, :]).then_inc(S["ln_std"], 1)

            def norm_std(ln):
                for b in range(B):
                    std_block(ln, b)

            for n in range(3 * B):
                act.wait_ge(S["proj_psum"], n + 1)
                b = n % B
                s.activation((hself, hst[1], hst[0])[n // B][e, b * D:(b + 1) * D], bank(b)[e], ACT.Copy
                             ).then_inc(S["first_out"], 1)

            act.wait_ge(S["ph_ready"], 1)
            s.activation(emb[0:2 * NF], ph[0:2 * NF], ACT.Sin).then_inc(S["emb_ready"], 1)
            cd = slice(0, CD)
            act.wait_ge(S["z1_psum"], 1)
            s.activation(blocks(z1[cd]), pair(3)[cd, :, e], ACT.Identity, bias=fb1[cd]).then_inc(S["act_step"], 1)
            act.wait_ge(S["act_step"], 1)
            s.activation(z2[cd], z1[cd], ACT.Exp, scale=-1.0).then_inc(S["z1_exp"], 1)
            act.wait_ge(S["z2_psum"], 1)
            s.activation(blocks(condT[cd, :]), pair(3)[cd, :, e], ACT.Identity, bias=fb2[cd]
                         ).then_inc(S["cond_ready"], 1)
            act.wait_ge(S["scattered0"], 8 * EC)
            act.wait_ge(S["scattered1"], 8 * EC)
            act.dma_start(meta[:, :], meta_d.rearrange("(p t) v -> p (t v)", p=P)).then_inc(S["meta_in"], 16)

            def set_rows(way, n, t, slot):
                act.wait_ge(S["msg_free"], n + 1)
                s.activation(rows_now[slot], rows_of[:, ds(t * 2 + way, 1)], ACT.Copy).then_inc(S["rows_set"], 1)

            act.wait_ge(S["turned_psum"], 1)
            bank_v = bank(7).bitcast(BF16).rearrange("p (h v n) -> p h v n", h=2, v=4)
            for h, n in enumerate((P, NT - P)):
                s.activation(turned_v[0:n, h], bank_v[0:n, h], ACT.Copy).then_inc(S["turned_sb"], 1)
            act.wait_ge(S["turned_sb"], 2)
            tiles_d = turned_d.rearrange("v (t n) -> t v n", n=P)
            for h, n in enumerate((P, NT - P)):
                act.dma_start(tiles_d[h * P:h * P + n], turned_v[0:n, h]).then_inc(S["turned_out"], 16)

            act.wait_ge(S["tables"], 3)
            with act.Fori(0, NT // Q) as i:
                for q in range(Q):
                    set_rows(0, i * Q + q, i * Q + q, q)
            for q in range(U):
                set_rows(0, NT - U + q, NT - U + q, q)
            with act.Fori(0, NT // Q) as i:
                for q in range(Q):
                    set_rows(1, i * Q + NT + q, i * Q + q, (U + q) % Q)
            for q in range(U):
                set_rows(1, 2 * NT - U + q, NT - U + q, U + q)

            for b in range(B):
                std_block(0, b)
                act.wait_ge(S["csd_psum"], b + 1)
                s.activation(blocks(cnt_sd[e, b * N:(b + 1) * N]), pair(3)[e, :, e], ACT.Copy).then_inc(S["csd_sb"], 1)
            for c in range(C):
                act.wait_ge(S["t_psum"], c + 1)
                s.activation(blocks(yTv[:, c]), pair(c)[:, :, e], ACT.Copy).then_inc(S["t_sb"], 1)
            norm_std(1)

            norm_std(2)
            with act.Fori(0, L) as l:
                def modulate(h):
                    for b in range(B):
                        act.wait_ge(S["mod_psum"], l * (2 * B) + h * B + b + 1)
                        s.activation(yTv[:, :, b * NB:(b + 1) * NB], chunks(bank(4 + b % 2)), ACT.Identity,
                                     bias=ones[:, 0:1]).then_inc(S["mod_sc"], 1)

                modulate(0)
                act.wait_ge(S["w_in1"], 32 * l + 32)
                for h in range(H):
                    act.wait_ge(S["qk_psum"], l * (2 * H) + 2 * h + 2)
                    s.activation(blocks(kT[:, h * N:(h + 1) * N]), pair((2 * h + 4) % 4)[:, :, e], ACT.Identity,
                                 bias=wcol[1][:, h:h + 1]).then_inc(S["k_done"], 1)
                for u in range(H * B + 3):
                    if u < H * B:
                        act.wait_ge(S["s_read"], l * (H * B) + u + 1)
                        if u > 1:
                            act.wait_ge(S["p_ready"], l * (H * B) + u - 1)
                        s.activation(ex[u % 2][e], sm[u % 2][e], ACT.Exp, bias=small[e, u % 2:u % 2 + 1], scale=-1.0
                                     ).then_inc(S["e_ready"], 1)
                    if u >= 3 and (u - 3) % B == B - 1:
                        h = (u - 3) // B
                        n = h * (B + 1) + B
                        act.wait_ge(S["pt_psum"], l * (H * (B + 1)) + n + 1)
                        s.activation(blocks(oT[:, h * N:(h + 1) * N]), pair(2 + n % 2)[:, :, e], ACT.Copy
                                     ).then_inc(S["pt_done"], 1)
                    if 2 <= u <= H * B + 1:
                        n, sblk = (u - 2) + (u - 2) // B, (u - 2) % B
                        act.wait_ge(S["pt_psum"], l * (H * (B + 1)) + n + 1)
                        s.activation(pT[e].rearrange("p (d n) -> p d n", d=B)[:, :, sblk * NB:(sblk + 1) * NB],
                                     pair(2 + n % 2)[e, :, e], ACT.Copy).then_inc(S["pt_done"], 1)
                norm_std(2 * l + 3)
                modulate(1)
                act.wait_ge(S["w_in4"], 32 * l + 32)
                for c in range(C):
                    act.wait_ge(S["m1_psum"], l * C + c + 1)
                    s.activation(blocks(qT[:, c * N:(c + 1) * N]), pair(c)[:, :, e], ACT.Relu,
                                 bias=wcol[2][:, c:c + 1]).then_inc(S["h_done"], 1)
                norm_std(2 * l + 4)
            norm_std(2 * L + 3)

            def parts_01(n, b):
                xb = xst[:, b * D:(b + 1) * D]
                act.wait_ge(S["xst_ready"], n + b + 1)
                s.activation(xp[0][:, b * D:(b + 1) * D], xb, ACT.Copy).then_inc(S["part0"], 1)
                act.wait_ge(S["rest1"], n + b + 1)
                s.activation(xp[1][:, b * D:(b + 1) * D], xb, ACT.Copy).then_inc(S["part1"], 1)

            act.wait_ge(S["we_in"], 112)
            for b in range(B):
                parts_01(0, b)

            def tile(l, i, q):
                t = i * 2 * U + q
                act.wait_ge(S["u_psum"], l * NT + t + 1)
                act.wait_ge(S["tile_free"], l * NT + t + 1)
                s.activation(part[0][q], bank(5 + q % U), ACT.Relu).then_inc(S["hi_ready"], 1)

            def gine(l, last):
                with act.Fori(0, NT // (2 * U)) as i:
                    for q in range(2 * U):
                        tile(l, i, q)
                for q in range(NT % (2 * U)):
                    tile(l, NT // (2 * U), q)
                for b in range(B):
                    act.wait_ge(S["xat_psum"], l * B + b + 1)
                    s.activation(yTv[:, :, b * NB:(b + 1) * NB], chunks(bank(5 + b % 2)), ACT.Copy
                                 ).then_inc(S["xat_sb"], 1)
                act.wait_ge(S["g_in"], 32 * l + 32)
                for c in range(C):
                    act.wait_ge(S["h1_psum"], l * C + c + 1)
                    s.activation(blocks(hp[:, c * N:(c + 1) * N]), pair(c)[:, :, e], ACT.Identity,
                                 bias=gcv[:, 0, c:c + 1]).then_inc(S["h1_sb"], 1)
                    act.wait_ge(S["bn_var"], l * C + c + 1)
                    s.activation(gstd[:, c:c + 1], mvv[:, c, 1:2], ACT.Sqrt, bias=eps_c[:, :]
                                 ).then_inc(S["bn_std"], 1)
                    act.wait_ge(S["bn_ready"], l * C + c + 1)
                    s.activation(hp[:, c * N:(c + 1) * N], hp[:, c * N:(c + 1) * N], ACT.Relu,
                                 bias=bnc[:, 3 * C + c:3 * C + c + 1], scale=bnc[:, C + c:C + c + 1]
                                 ).then_inc(S["hp_ready"], 1)
                if not last:
                    act.wait_ge(S["we_in"], 112 * l + 224)
                    for b in range(B):
                        parts_01(l * B + B, b)

            with act.Fori(0, L - 1) as l:
                gine(l, False)
            gine(L - 1, True)
            norm_std(2 * L + 4)

        @block.tensor
        def _(pe):
            mm = nc.tensor.matmul

            def wide_mm(out_pair, lhsT, rhs, **flags):
                r = blocks(rhs)
                mm(out_pair[:, 0:4, e], lhsT, r[:, 0:4], **flags)
                return mm(out_pair[:, 4, e], lhsT, r[:, 4], **flags)

            def project(b, bnk, left, weight, chunk_ready=None):
                for c in range(C):
                    if chunk_ready:
                        pe.wait_ge(chunk_ready[0], chunk_ready[1] + c + 1)
                    ins = mm(bank(bnk)[e], left[:, c, b * NB:(b + 1) * NB], weight[:, c * D:(c + 1) * D],
                             start=(c == 0), stop=(c == C - 1))
                return ins

            def turn_chunk(c, where, src):
                for b in range(B):
                    ins = nc.tensor.transpose(pair(where)[:, b, e], src[e, b, c * P:(c + 1) * P], ident[e, e])
                return ins

            def clear(n):
                for q in range(n):
                    mm(bank(q)[e], zerob[:, e], zerob[:, :], start=True, stop=False, skip_group_check=True)

            def columns_of(table, i):
                word = packed(mybir.EngineType.PE, table, i, D_BITS + 6 * U)
                return [((word >> (3 * j) if j else word) & (7 * D)).with_bounds(min_val=0, max_val=(B - 1) * D)
                        for j in range(2 * U)]

            def blocks_next(i):
                cols = columns_of(tab_next, i)
                return cols[:U], cols[U:]

            pe.wait_ge(S["x_in"], 16)
            pe.wait_ge(S["wr_in0"], 32)
            for b in range(B):
                project(b, b, xTv, wr[0]).then_inc(S["proj_psum"], 1)
            pe.wait_ge(S["consts"], 1)
            pe.wait_ge(S["totals"], 1)
            tot = small[e, 0:K]
            mm(bank(7)[e, 0:K], earlier[e, e], tot, start=True, stop=True)
            mm(bank(7)[:, 32:32 + K], ones[e, :], tot, start=True, stop=True).then_inc(S["offsets_mm"], 1)
            def project_two(i, after_scalar=()):
                for j in (1, 0):
                    pe.wait_ge(S[f"wr_in{j}"], 32 * i + 64 - 32 * j)
                    for b in range(B):
                        if j in after_scalar:
                            pe.wait_ge(S["first_out"], (2 * i + 1 - j) * B + b + 1)
                        else:
                            pe.wait_ge(S["proj_free"], (2 * i + 2 - j) * B + b + 1)
                        project(b, b, xTv, wr[j]).then_inc(S["proj_psum"], 1)

            project_two(0, (1, 0))
            project_two(1, (1,))
            project_two(2)
            pe.wait_ge(S["emb_ready"], 1)
            pe.wait_ge(S["fnet_in"], 80)
            pe.wait_ge(S["slot_addr"], 1)
            wide_mm(pair(3)[0:CD], fw1[0:2 * NF], emb[0:2 * NF], start=True, stop=True).then_inc(S["z1_psum"], 1)
            with pe.Fori(3, 5) as i:
                project_two(i)
            pe.wait_ge(S["z1_ready"], 1)
            wide_mm(pair(3)[0:CD], fw2[0:CD], z1[0:CD], start=True, stop=True).then_inc(S["z2_psum"], 1)
            with pe.Fori(5, EARLY) as i:
                project_two(i)


            BODIES = NT // Q

            def bodys_columns(table, i):
                return [c for k in range(Q // U) for c in columns_of(table, i * (Q // U) + k)[:U]]


            def to_head(i, col, q):
                pe.wait_ge(S["onef"], i * Q + q + 1)
                pe.wait_ge(S[f"got{q}"], 16 * i + 16)
                mm(banks[e, ds(col, D)], ohf_s[q], got[q], start=False, stop=False, skip_group_check=True
                   ).then_inc(S["msg_free"], 1)

            pe.wait_ge(S["tables"], 3)
            pe.wait_ge(S["cond_ready"], 1)
            bank_v = bank(7).bitcast(BF16).rearrange("p (h v n) -> p h v n", h=2, v=4)
            for h, n in enumerate((P, NT - P)):
                for q in range(4):
                    columns = s16[:, h * P:h * P + n] if q == 0 else w3v[:, h * P:h * P + n, q - 1]
                    ins = nc.tensor.transpose(bank_v[0:n, h, q], columns, identb[:, :])
            ins.then_inc(S["turned_psum"], 1)
            pe.wait_ge(S["proj_free"], (2 * EARLY + 1) * B + B)
            clear(B)
            with pe.Fori(0, R - EARLY) as i:
                for j in (1, 0):
                    pe.wait_ge(S[f"wr_in{j}"], 32 * i + 32 * EARLY + 64 - 32 * j)
                    for b in range(B):
                        turn_no = (1 - j) * B + b
                        at_s = bodys_columns(tab_s, i * 2 * B + turn_no)
                        pe.wait_ge(S["proj_free"], (2 * i + 2 * EARLY + 2 - j) * B + b + B - 1)
                        project(b, 5 + turn_no % 2, xTv, wr[j]).then_inc(S["proj_psum"], 1)
                        for q in range(Q):
                            to_head(i * 2 * B + turn_no, at_s[q], q)
            at_s = columns_of(tab_s, NT // U - 1)
            for q in range(U):
                to_head(BODIES, at_s[q], q)

            pe.wait_ge(S["turned_sb"], 2)
            def to_tail(i, col, q):
                slot = (U + q) % Q
                pe.wait_ge(S["onef"], i * 3 * Q + 3 * q + NT + 3)
                pe.wait_ge(S["cnt_free"], i * Q + q + 1)
                mm(bank(5 + q % U)[e, e], hot_d16[slot], hot_s16[slot], start=True, stop=True
                   ).then_inc(S["cnt_psum"], 1)
                pe.wait_ge(S[f"got{slot}"], 16 * i + 16 * (BODIES + (1 if U + q < Q else 2)))
                mm(banks[e, ds(col, D)], ohf_d[slot], got[slot], start=False, stop=False, skip_group_check=True
                   ).then_inc(S["msg_free"], 1)

            with pe.Fori(0, BODIES) as i:
                at_d = bodys_columns(tab_d, i)
                for q in range(Q):
                    to_tail(i, at_d[q], q)
            at_d = columns_of(tab_d, NT // U - 1)
            for q in range(U):
                to_tail(BODIES, at_d[q], q)

            pe.wait_ge(S["cnt_free"], NT + U)
            for k in range(B):
                if k:
                    pe.wait_ge(S["csd_sb"], k)
                for d in range(B):
                    ins = nc.tensor.transpose(pair(3)[e, d, e], cds[e, d * B + k], ident[e, e])
                ins.then_inc(S["csd_psum"], 1)

            pe.wait_ge(S["x0_ready"], B)
            pe.wait_ge(S["csd_sb"], B)
            for c in range(C):
                turn_chunk(c, c, xv).then_inc(S["t_psum"], 1)
            pe.wait_ge(S["t_sb"], C)
            pe.wait_ge(S["m1_in"], 48)
            for b in range(B):
                project(b, b, yTv, wn).then_inc(S["beta_psum"], 1)
            pe.wait_ge(S["beta_sb"], B)
            for b in range(B):
                q = 2 * (b % 2)
                if b >= 2:
                    pe.wait_ge(S["agg_used"], b - 1)
                project(b, q, yTv, wc)
                for d in range(B):
                    ins = mm(bank(q + 1)[e], cds[e, d * B + b], beta[e, d * D:(d + 1) * D],
                             start=(d == 0), stop=(d == B - 1))
                ins.then_inc(S["agg_psum"], 1)

            with pe.Fori(0, L) as l:
                def modulate(h):
                    pe.wait_ge(S[f"ln_in{h}"], 64 * l + 64)
                    for b in range(B):
                        if b >= 2:
                            pe.wait_ge(S["mod_done"], l * (2 * B) + h * B + b - 1)
                        for q in range(2):
                            for c in range(C):
                                mm(chunks(bank(4 + 2 * q + b % 2))[:, c], lnw[2 * h + q][0:CD + 1, c * P:(c + 1) * P],
                                   condT[:, b * NB:(b + 1) * NB], start=True, stop=True)
                        pe.wait_ge(S["xn_ready"], l * (2 * B) + h * B + b + 1)
                        for c in range(C):
                            ins = nc.tensor.transpose(chunks(bank(2 + b % 2))[:, c], xnv[e, b, c * P:(c + 1) * P],
                                                      ident[e, e])
                        ins.then_inc(S["mod_psum"], 1)

                def wide_project(where, left, o):
                    for c in range(C):
                        ins = wide_mm(pair(where), left[:, c * D + o * P:c * D + (o + 1) * P], yTv[:, c],
                                      start=(c == 0), stop=(c == C - 1))
                    return ins

                modulate(0)
                pe.wait_ge(S["w_in2"], 32 * l + 32)
                for b in range(B):
                    pe.wait_ge(S["mod_done"], l * (2 * B) + (b + 1 if b < 2 else B))
                    project(b, b, yTv, w2[2]).then_inc(S["v_psum"], 1)
                pe.wait_ge(S["w_in0"], 32 * l + 32)
                pe.wait_ge(S["w_in1"], 32 * l + 32)
                for u in range(2 * H):
                    if 1 <= u <= 3:
                        pe.wait_ge(S["v_done"], l * B + min(2 * u, B))
                    if u >= 4:
                        pe.wait_ge(S[("q_done", "k_done")[u % 2]], l * H + u // 2 - 1)
                    wide_project((u + 3) % 4, w2[u % 2], u // 2).then_inc(S["qk_psum"], 1)
                pe.wait_ge(S["q_done"], l * H + H - 1)
                for u in range(H * B + 3):
                    if u < H * B:
                        h, sblk = u // B, u % B
                        if u == 0:
                            pe.wait_ge(S["k_done"], l * H + H - 1)
                        if u == 1:
                            pe.wait_ge(S["q_done"], l * H + H)
                        if u == 2:
                            pe.wait_ge(S["k_done"], l * H + H)
                        if u >= 2:
                            pe.wait_ge(S["s_read"], l * (H * B) + u - 1)
                        wide_mm(pair(u % 2)[e], qT[:, h * N + sblk * NB:h * N + (sblk + 1) * NB],
                                kT[:, h * N:(h + 1) * N], start=True, stop=True).then_inc(S["s_psum"], 1)
                    if u >= 3 and (u - 3) % B == B - 1:
                        h = (u - 3) // B
                        n = h * (B + 1) + B
                        pe.wait_ge(S["pt_done"], l * (H * (B + 1)) + n)
                        for d in range(B):
                            ins = wide_mm(pair(2 + n % 2), vN[e, d * D + h * P:d * D + (h + 1) * P],
                                          pT[e, d * N:(d + 1) * N], start=(d == 0), stop=(d == B - 1))
                        ins.then_inc(S["pt_psum"], 1)
                    if 2 <= u <= H * B + 1:
                        n, z = (u - 2) + (u - 2) // B, (u - 2) % 2
                        pe.wait_ge(S["p_ready"], l * (H * B) + u - 1)
                        if n >= 2:
                            pe.wait_ge(S["pt_done"], l * (H * (B + 1)) + n - 1)
                        for d in range(B):
                            ins = mm(pair(2 + n % 2)[e, d, e], pr[z][e, d * NB:(d + 1) * NB], dg[z][e],
                                     start=True, stop=True)
                        ins.then_inc(S["pt_psum"], 1)
                pe.wait_ge(S["s_read"], l * (H * B) + H * B)
                pe.wait_ge(S["pt_done"], l * (H * (B + 1)) + H * (B + 1))
                pe.wait_ge(S["w_in3"], 32 * l + 32)
                oTv = oT.rearrange("p (c n) -> p c n", c=C)

                def outputs(h, left, weight, psum):
                    for b in range(B):
                        if b >= 2:
                            pe.wait_ge(S["x_upd"], l * (2 * B) + h * B + b - 1)
                        project(b, b % 2, left, weight).then_inc(S[psum], 1)

                outputs(0, oTv, w2[3], "wo_psum")
                modulate(1)
                pe.wait_ge(S["w_in4"], 32 * l + 32)
                pe.wait_ge(S["mod_done"], l * (2 * B) + B + B - 1)
                for c in range(C):
                    mm(pair(0)[:, 0:4, e], w2[4][:, c * D:c * D + P], blocks(yTv[:, c])[:, 0:4],
                       start=(c == 0), stop=(c == C - 1))
                pe.wait_ge(S["mod_done"], l * (2 * B) + 2 * B)
                for c in range(C):
                    ins = mm(pair(0)[:, 4, e], w2[4][:, c * D:c * D + P], blocks(yTv[:, c])[:, 4],
                             start=(c == 0), stop=(c == C - 1))
                ins.then_inc(S["m1_psum"], 1)
                for c in range(1, C):
                    wide_project(c, w2[4], c).then_inc(S["m1_psum"], 1)
                pe.wait_ge(S["h_done"], l * C + C)
                pe.wait_ge(S["w_in5"], 32 * l + 32)
                hT = qT.rearrange("p (c n) -> p c n", c=C)
                outputs(1, hT, w2[5], "m2_psum")

            pe.wait_ge(S["stat_a"], 1)
            pe.wait_ge(S["stat_b"], 1)

            def settle(col):
                return pe.snap(col, min_val=0, max_val=(B - 1) * D)

            def gather(l, i, at_s, q0):
                at = i * (U * P)
                for j in range(U):
                    if q0 is not None:
                        pe.wait_ge(S["rest_ready"], l * NT + (i - 1) * U + j + 1)
                    tile_j = stat[:, j * P:(NT - U + 1 + j) * P]
                    for q in range(3):
                        ins = mm(bank(5 + j), tile_j[:, ds(at, P)], xp[q][:, ds(at_s[j], D)],
                                 start=(q == 0), stop=(q == 2))
                    ins.then_inc(S["u_psum"], 1)

            def scatter(l, i, at_d, q0, look=None):
                ahead = None
                for j in range(U):
                    pe.wait_ge(S["odf_ready"], l * NT + i * U + j + 1)
                    pe.wait_ge(S["lo_ready"], l * NT + i * U + j + 1)
                    for q in range(3):
                        ins = mm(banks[e, ds(at_d[j], D)], odb[q0 + j], part[q][q0 + j], start=False, stop=False,
                                 skip_group_check=True)
                        if q == 2:
                            ins.then_inc(S["tile_free"], 1)
                        if look is not None and j == 0 and q == 1:
                            ahead = blocks_next(look)
                        if look is not None and j > 0 and q < 2 and 2 * j - 2 + q < U:
                            ahead[0][2 * j - 2 + q] = settle(ahead[0][2 * j - 2 + q])
                return ahead

            W = 6
            assert NT // U % W == 1

            def gine(l):
                at_s, _ = blocks_next(0)
                clear(B)
                pe.wait_ge(S["parts"], l * B + B)
                gather(l, 0, at_s, None)
                with pe.Fori(0, NT // U // W) as i:
                    ahead = blocks_next(W * i + 1)
                    for k in range(W):
                        at_s, at_d = ahead
                        gather(l, W * i + 1 + k, at_s, 0)
                        ahead = scatter(l, W * i + k, at_d, U * (k % 2), W * i + 2 + k if k < W - 1 else None)
                _, at_d = blocks_next(NT // U)
                scatter(l, NT // U - 1, at_d, 0)
                for b in range(B):
                    pe.wait_ge(S["xa_ready"], l * B + b + 1)
                    if b >= 2:
                        pe.wait_ge(S["xat_sb"], l * B + b - 1)
                    for c in range(C):
                        ins = nc.tensor.transpose(chunks(bank(5 + b % 2))[:, c], xnv[e, b, c * P:(c + 1) * P],
                                                  ident[e, e])
                    ins.then_inc(S["xat_psum"], 1)
                pe.wait_ge(S["g_in"], 32 * l + 32)
                pe.wait_ge(S["xat_sb"], l * B + B - 1)
                for c in range(C):
                    mm(pair(0)[:, 0:4, e], g1[:, c * D:c * D + P], blocks(yTv[:, c])[:, 0:4],
                       start=(c == 0), stop=(c == C - 1))
                pe.wait_ge(S["xat_sb"], l * B + B)
                for c in range(C):
                    ins = mm(pair(0)[:, 4, e], g1[:, c * D:c * D + P], blocks(yTv[:, c])[:, 4],
                             start=(c == 0), stop=(c == C - 1))
                ins.then_inc(S["h1_psum"], 1)
                for o in range(1, C):
                    for c in range(C):
                        ins = wide_mm(pair(o), g1[:, c * D + o * P:c * D + (o + 1) * P], yTv[:, c],
                                      start=(c == 0), stop=(c == C - 1))
                    ins.then_inc(S["h1_psum"], 1)
                pe.wait_ge(S["g2_in"], 32 * l + 32)
                hpv = hp.rearrange("p (c n) -> p c n", c=C)
                for b in range(B):
                    project(b, b, hpv, g2, (S["hp_ready"], l * C) if b == 0 else None).then_inc(S["h2_psum"], 1)
                pe.wait_ge(S["h2_read"], l * B + B)

            with pe.Fori(0, L) as l:
                gine(l)


def kernel(**inputs):
    import numpy as np
    import concourse.bacc as bacc
    from concourse.bass_utils import run_bass_kernel_spmd

    i = {n: np.asarray(v) for n, v in inputs.items()}

    def columns(v):
        return v.reshape(L, C, P).transpose(0, 2, 1)

    arrays = {n: v for n, v in i.items() if n.startswith(("L1_", "L2_", "L3_")) and n not in (
        "L2_gnn_bq", "L2_gnn_bk", "L2_gnn_m_b1", "L3_gnn_eps", "L3_gnn_b1", "L3_gnn_gamma", "L3_gnn_beta")}
    arrays["L1_gnn_bias"] = i["L1_gnn_bias"].reshape(1, D)
    arrays["L2_gnn_f_b1"] = i["L2_gnn_f_b1"].reshape(CD, 1)
    arrays["L2_gnn_f_b2"] = i["L2_gnn_f_b2"].reshape(CD, 1)
    arrays["x"] = i["x"]
    arrays["xT"] = i["x"].T
    for n in ("src", "dst", "edge_type_8", "edge_weight1"):
        arrays[n] = i[n].reshape(NB, EC)
    arrays["node_vec1"] = i["node_vec1"].reshape(1, N)
    arrays["W0"] = np.concatenate([i["L0_gnn_W_self"][None], i["L0_gnn_W_rel"]]).transpose(0, 2, 1)
    arrays["b0"] = np.concatenate([i["L0_gnn_b_self"][None], i["L0_gnn_b_rel"]])
    for n in ("bq", "bk", "m_b1"):
        arrays[n] = columns(i["L2_gnn_" + n])
    arrays["eps3"] = i["L3_gnn_eps"].reshape(L, 1)
    arrays["L3_gnn_We"] = i["L3_gnn_We"].reshape(L, D)
    arrays["cols3"] = np.concatenate([columns(i["L3_gnn_" + n]) for n in ("b1", "gamma", "beta")], axis=2)
    arrays = {n: np.ascontiguousarray(v) for n, v in arrays.items()}

    nc = bacc.Bacc("TRN2", target_bir_lowering=False, num_devices=1)
    aps = {n: nc.dram_tensor("in_" + n, v.shape, mybir.dt.from_np(v.dtype), kind="ExternalInput").ap()
           for n, v in arrays.items()}
    out = nc.dram_tensor("out_x", (N, D), F32, kind="ExternalOutput").ap()
    gnn_stack(nc, aps, out)
    r = run_bass_kernel_spmd(nc, [{"in_" + n: v for n, v in arrays.items()}], core_ids=[0])
    return r.results[0]["out_x"]
```
